# Optimizing a Trainium2 kernel written in Bass

```python
import numpy as np
import jax
import jax.numpy as jnp

def _softmax(x, axis=-1):
    return jax.nn.softmax(x, axis=axis)
def _gelu(x):
    return jax.nn.gelu(x, approximate=True)
def _silu(x):
    return jax.nn.silu(x)
def _sigmoid(x):
    return jax.nn.sigmoid(x)
def _layernorm(x, axis=-1, eps=1e-5):
    m = jnp.mean(x, axis=axis, keepdims=True)
    v = jnp.var(x, axis=axis, keepdims=True)
    return (x - m) / jnp.sqrt(v + eps)
def _scatter_add(tgt, idx, src, axis=0):
    return tgt.at[idx].add(src)
def _segment_sum(src, seg, n):
    return jax.ops.segment_sum(src, seg, n)

kernel_name = 'mk_adj_resnorm_d4_adj_128_fc5a19'

def setup_inputs(seed: int = 0):
    np.random.seed(seed)
    _w = jnp.asarray
    def _rec_inputs():
        import jax
        import jax.numpy as jnp
        _gk = jax.random.key(seed)
        x = -9.806e-05 + 1 * jax.random.normal(jax.random.fold_in(_gk, 1), (16, 1024, 128), jnp.float32)
        _a = jax.random.bernoulli(jax.random.fold_in(_gk, 2), 0.03125, (16, 1024, 1024))
        _af = _a.astype(jnp.float32)
        adj = _af
        return x, adj
    x, adj = _rec_inputs()
    def _L0_gnn_setup():
        import jax, jax.numpy as jnp
        import numpy as np
        B, N, F = (8, 512, 128)
        NEG = jnp.float32(-10000000000.0)
        key = jax.random.key(seed)
        kx, ka = jax.random.split(key)
        X = jax.random.normal(kx, (B, N, F), dtype=jnp.float32)
        A = jax.random.randint(ka, (B, N, N), 0, 2).astype(jnp.float32)
        return {'X': X, 'A': A}
    _L0_gnn_all = _L0_gnn_setup()
    _L0_gnn_in = {k: v for k, v in _L0_gnn_all.items() if k in ()}
    del _L0_gnn_all

    def _L1_gnn_setup():
        import jax, jax.numpy as jnp
        import numpy as np
        B, T, C_IN, C_OUT = (2, 1024, 128, 64)
        NEG_INF = -1e+22
        key = jax.random.key(seed)
        k_feat, k_adj, k_w1, k_w2, k_a = jax.random.split(key, 5)
        feat = jax.random.normal(k_feat, (B, T, C_IN), dtype=jnp.float32)
        adj = jax.random.randint(k_adj, (B, T, T), 0, 2).astype(jnp.float32)
        s_in = 1.0 / np.sqrt(C_IN)
        s_out = 1.0 / np.sqrt(C_OUT)
        W1 = jax.random.uniform(k_w1, (C_OUT, C_IN), jnp.float32, -s_in, s_in)
        W2 = jax.random.uniform(k_w2, (C_OUT, C_IN), jnp.float32, -s_in, s_in)
        a = jax.random.uniform(k_a, (C_OUT,), jnp.float32, -s_out, s_out)
        return {'feat': feat, 'adj': adj, 'W1': W1, 'W2': W2, 'a': a}
    _L1_gnn_all = _L1_gnn_setup()
    _L1_gnn_in = {k: v for k, v in _L1_gnn_all.items() if k in ('W1', 'W2', 'a', )}
    del _L1_gnn_all

    def _L2_gnn_setup():
        import jax, jax.numpy as jnp
        import numpy as np
        EPS = 1e-05
        N_LAYERS_TOTAL = 4
        key = jax.random.key(seed)
        ks = jax.random.split(key, 6)
        B, N, C = (16, 2048, 128)
        x = jax.random.normal(ks[0], (B, N, C), dtype=jnp.float32)
        adj = jax.random.uniform(ks[1], (B, N, N), dtype=jnp.float32)
        W = jax.random.normal(ks[2], (N_LAYERS_TOTAL, C, C), dtype=jnp.float32) * (1.0 / np.sqrt(C))
        b = jnp.zeros((N_LAYERS_TOTAL, C), dtype=jnp.float32)
        gamma = jnp.ones((N_LAYERS_TOTAL, C), dtype=jnp.float32)
        beta = jnp.zeros((N_LAYERS_TOTAL, C), dtype=jnp.float32)
        return {'x': x, 'adj': adj, 'W': W, 'b': b, 'gamma': gamma, 'beta': beta}
    _L2_gnn_all = _L2_gnn_setup()
    _L2_gnn_in = {k: v for k, v in _L2_gnn_all.items() if k in ('W', 'b', 'gamma', 'beta', )}
    del _L2_gnn_all

    def _L3_gnn_setup():
        import jax, jax.numpy as jnp
        import numpy as np
        B, N, D, L = (16, 2048, 128, 3)
        LN_EPS = 1e-05

        def _layer_norm(z, gamma, beta):
            mu = jnp.mean(z, axis=-1, keepdims=True)
            var = jnp.mean(jnp.square(z - mu), axis=-1, keepdims=True)
            return (z - mu) * jax.lax.rsqrt(var + LN_EPS) * gamma + beta
        key = jax.random.key(seed)
        k_x, k_a, k_w = jax.random.split(key, 3)
        X = jax.random.normal(k_x, (B, N, D), dtype=jnp.float32)
        adj_mat = jax.random.uniform(k_a, (B, N, N), dtype=jnp.float32)
        limit = np.sqrt(6.0 / (D + D))
        Ws = jax.random.uniform(k_w, (L, D, D), dtype=jnp.float32, minval=-limit, maxval=limit)
        bs = jnp.zeros((L, D), dtype=jnp.float32)
        gammas = jnp.ones((L, D), dtype=jnp.float32)
        betas = jnp.zeros((L, D), dtype=jnp.float32)
        return {'X': X, 'adj_mat': adj_mat, 'Ws': Ws, 'bs': bs, 'gammas': gammas, 'betas': betas}
    _L3_gnn_all = _L3_gnn_setup()
    _L3_gnn_in = {k: v for k, v in _L3_gnn_all.items() if k in ('Ws', 'bs', 'gammas', 'betas', )}
    del _L3_gnn_all

    return {
        "x": x,
        "adj": adj,
        "L1_gnn_W1": _L1_gnn_in["W1"],
        "L1_gnn_W2": _L1_gnn_in["W2"],
        "L1_gnn_a": _L1_gnn_in["a"],
        "L2_gnn_W": _L2_gnn_in["W"],
        "L2_gnn_b": _L2_gnn_in["b"],
        "L2_gnn_gamma": _L2_gnn_in["gamma"],
        "L2_gnn_beta": _L2_gnn_in["beta"],
        "L3_gnn_Ws": _L3_gnn_in["Ws"],
        "L3_gnn_bs": _L3_gnn_in["bs"],
        "L3_gnn_gammas": _L3_gnn_in["gammas"],
        "L3_gnn_betas": _L3_gnn_in["betas"],
    }

def reference(x, adj, L1_gnn_W1, L1_gnn_W2, L1_gnn_a, L2_gnn_W, L2_gnn_b, L2_gnn_gamma, L2_gnn_beta, L3_gnn_Ws, L3_gnn_bs, L3_gnn_gammas, L3_gnn_betas):
    import jax
    import jax.numpy as jnp
    def _L0_gnn_ref(X, A):
        import jax, jax.numpy as jnp
        import numpy as np
        B, N, F = (8, 512, 128)
        NEG = jnp.float32(-10000000000.0)
        mask = jnp.where(A == 0, NEG, jnp.float32(0.0))
        out = jnp.max(X[:, :, None, :] + mask[:, :, :, None], axis=1)
        return out

    def _L1_gnn_ref(feat, adj, W1, W2, a):
        import jax, jax.numpy as jnp
        import numpy as np
        B, T, C_IN, C_OUT = (2, 1024, 128, 64)
        NEG_INF = -1e+22
        mask = jnp.where(adj > 0, jnp.float32(0.0), jnp.float32(NEG_INF))
        q = feat @ W1.T
        k = feat @ W2.T
        e = jax.nn.relu(q[:, None, :, :] + k[:, :, None, :])
        scores = jnp.einsum('bijd,d->bij', e, a)
        att = jax.nn.softmax(scores + mask, axis=-1)
        return att @ feat

    def _L2_gnn_ref(x, adj, W, b, gamma, beta):
        import jax, jax.numpy as jnp
        import numpy as np
        EPS = 1e-05
        N_LAYERS_TOTAL = 4
        h = x
        for i in range(N_LAYERS_TOTAL):
            h = jnp.einsum('bnm,bmc->bnc', adj, h @ W[i]) + b[i]
            h = jax.nn.relu(h)
            mu = jnp.mean(h, axis=(0, 1))
            var = jnp.mean(jnp.square(h - mu), axis=(0, 1))
            h = gamma[i] * (h - mu) * jax.lax.rsqrt(var + EPS) + beta[i]
        return h

    def _L3_gnn_ref(X, adj_mat, Ws, bs, gammas, betas):
        import jax, jax.numpy as jnp
        import numpy as np
        B, N, D, L = (16, 2048, 128, 3)
        LN_EPS = 1e-05

        def _layer_norm(z, gamma, beta):
            mu = jnp.mean(z, axis=-1, keepdims=True)
            var = jnp.mean(jnp.square(z - mu), axis=-1, keepdims=True)
            return (z - mu) * jax.lax.rsqrt(var + LN_EPS) * gamma + beta
        h = X
        for i in range(L):
            res = h
            hw = jnp.einsum('bnd,de->bne', h, Ws[i])
            agg = jnp.einsum('bij,bie->bje', adj_mat, hw)
            conv = agg + bs[i]
            h = jax.nn.relu(_layer_norm(conv + res, gammas[i], betas[i]))
        return h

    x = _layernorm(x + _L0_gnn_ref(x, adj), axis=-1)
    x = _layernorm(x + _L1_gnn_ref(x, adj, L1_gnn_W1, L1_gnn_W2, L1_gnn_a), axis=-1)
    x = _layernorm(x + _L2_gnn_ref(x, adj, L2_gnn_W, L2_gnn_b, L2_gnn_gamma, L2_gnn_beta), axis=-1)
    x = _layernorm(x + _L3_gnn_ref(x, adj, L3_gnn_Ws, L3_gnn_bs, L3_gnn_gammas, L3_gnn_betas), axis=-1)
    return x


_drawn_inputs = setup_inputs


def setup_inputs(seed=0):
    import zlib

    import numpy as np

    out = dict(_drawn_inputs(seed))
    spreads = {'L2_gnn_b': (0.0, 0.8),
     'L2_gnn_gamma': (1.0, 0.2),
     'L2_gnn_beta': (0.0, 0.1),
     'L3_gnn_bs': (0.0, 0.8),
     'L3_gnn_gammas': (1.0, 0.2),
     'L3_gnn_betas': (0.0, 0.1)}
    factors = {'L1_gnn_W2': 3.76}
    for name, (base, spread) in spreads.items():
        noise = np.random.default_rng([zlib.crc32(name.encode()), seed]).standard_normal(out[name].shape)
        drawn = base * np.exp(spread * noise) if base else spread * noise
        out[name] = jnp.asarray(drawn.astype(out[name].dtype))
    for name, factor in factors.items():
        out[name] = (out[name] * factor).astype(out[name].dtype)
    return out
```

```python
from contextlib import ExitStack

import concourse.bass as bass
from concourse import mybir

ALU = mybir.AluOpType
ACT = mybir.ActivationFunctionType
F32 = mybir.dt.float32
BF16 = mybir.dt.bfloat16
FP8 = mybir.dt.float8e4
U8 = mybir.dt.uint8

P = 128
N = 1024
F = 128
NT = N // P
HALF = 512

BLK = 5
PAT = 1 << BLK
NBLK = -(-P // BLK)
PADDED = NBLK * BLK
PARTS = 3
CODE = PARTS * PAT
NO_EDGE = -1.0e10

D1 = 64
PAIRS = P // 2
QUADS = 4
GROUPS = PAIRS // QUADS
RSLOTS = 4
NO_ATT = -1.0e22
EPS = 1e-5


def wait_apart(eng, sem, value, ready):
    eng.wait_ge(sem, value)
    eng.sem_inc(ready, 1)


class Chain:

    def __init__(self, eng, sem, per, ready):
        self.eng, self.sem, self.per, self.ready, self.n, self.base = eng, sem, per, ready, 0, 0

    def round(self, index):
        assert self.n in (0, self.per), self.n
        self.n, self.base = 0, index * self.per

    def step(self, instruction):
        instruction.then_inc(self.sem, 1)
        self.n += 1

    def wait(self):
        wait_apart(self.eng, self.sem, self.base + self.n, self.ready)


def tile_units(it):
    for u in range(NBLK):
        yield ("code", u)
        if u == 4:
            yield ("turn", 0)
        if it < NT - 1 and u in (13, 15):
            yield ("table", (u - 13) // 2)


PRE = 4
TURN_AT = 5
UNITS = NBLK + 3
RING = PRE + UNITS * (NT - 1) + NBLK + 1
LOOKS = NBLK * NT
SPLIT = [(0, 16), (16, NBLK)]
assert RING % 2 == 0 and LOOKS % 4 == 0 and UNITS % 2 == 1 and NBLK % 4 == 2


def unit_at(it, what):
    return list(tile_units(0 if it != NT - 1 else it)).index(what)


def over_tiles(eng, tile):
    tile(0, 0)
    tile(1, 1)
    with eng.Fori(1, NT // 2 - 1) as i:
        tile(i * 2, 2)
        tile(i * 2 + 1, 3)
    tile(NT - 2, NT - 2)
    tile(NT - 1, NT - 1)


def over_batches(eng, B, batch):
    with eng.Fori(0, B // 2) as pair:
        with eng.Fori(0, 2) as parity:
            batch(pair * 2 + parity, parity)


def graph_layers_0_1(nc, B, x, adj, w1, w2, a_col, code_w, pat_bias, at_d, x2_d):
    with ExitStack() as ctx:
        def sb(name, shape, dt=F32):
            return ctx.enter_context(nc.sbuf_tensor(name, shape, dt))

        def sem(name):
            return ctx.enter_context(nc.semaphore(name))

        ringA = ctx.enter_context(nc.psum_tensor("ringA", [P, 2, N], F32))
        ringC = ctx.enter_context(nc.psum_tensor("ringC", [P, 2, N], F32))

        adj_sb = sb("adj_sb", [P, 2 * NT, N], BF16)
        x_sb = sb("x_sb", [P, NT, F])
        xT = sb("xT", [P, NT, PADDED])
        low = sb("low", [P, 1])
        tab = sb("tab", [P, NBLK, PAT])
        tab_r = sb("tab_r", [P, NBLK, PAT])
        tab_s = sb("tab_s", [P, NBLK, PARTS, PAT], BF16)
        look = [sb(f"look{i}", [CODE, NBLK, F], BF16) for i in range(2)]
        hot = sb("hot", [CODE, 4, N], BF16)
        best = sb("best", [P, 2, N])
        at8 = sb("at8", [P, 2, NT, P], FP8)
        code_sb = sb("code_sb", [P, NBLK, CODE], BF16)
        bias_sb = sb("bias_sb", [CODE, 1])
        ident = sb("ident0", [P, P])
        ident_b = sb("ident_b", [P, P], BF16)
        z = sb("z", [P, NT, F])
        x1 = sb("x1", [P, NT, F])
        x1T = sb("x1T", [P, N])
        stats = sb("stats", [P, NT, 6])
        mv = sb("mv", [P, NT, 2])
        rstd = sb("rstd", [P, NT])
        power = sb("power", [P, NT])
        ones = sb("ones", [P, NT])
        w1_sb = sb("w1_sb", [P, 2 * D1])
        w2_sb = sb("w2_sb", [P, 2 * D1])
        a_sb = sb("a_sb", [P, 1])
        a_wide = sb("a_wide", [P, GROUPS, 32])
        q_sb = sb("q_sb", [P, N])
        k_sb = sb("k_sb", [P, N // 2])
        hid = sb("hid", [P, RSLOTS, QUADS, N])
        mask = sb("mask", [P, N])
        sc = sb("sc", [P, N])
        pr = sb("pr", [P, N])
        prT = sb("prT", [P, NT, P])
        top = sb("top", [P, 1])
        neg_top = sb("neg_top", [P, 1])
        total = sb("total", [P, 1])
        inv = sb("inv", [P, 1])
        x2 = sb("x2_sb", [P, NT, F])

        const_loaded = sem("const_loaded")
        code_loaded = sem("code_loaded")
        const_built = sem("const_built")
        id_zero = sem("id_zero")
        adj_loaded = sem("adj_loaded")
        adj_free = sem("adj_free")
        x_loaded = sem("x_loaded")
        ring_full = sem("ring_full")
        ring_free = sem("ring_free")
        look_full = sem("look_full")
        look_free = sem("look_free")
        table_split = sem("table_split")
        pool_step = sem("pool_step")
        tab_step = sem("tab_step")
        eps_added = sem("eps_added")
        dve_step = sem("dve_step")
        best_done = sem("best_done")
        best_turned = sem("best_turned")
        z0_done = sem("z0_done")
        ln_stats = sem("ln_stats")
        ln_rstd = sem("ln_rstd")
        x1_done = sem("x1_done")
        x1_turned = sem("x1_turned")
        x1T_done = sem("x1T_done")
        qk_done = sem("qk_done")
        q_copied = sem("q_copied")
        k_copied = sem("k_copied")
        hid_dve = sem("hid_dve")
        hid_act = sem("hid_act")
        score_grp = sem("score_grp")
        max_done = sem("max_done")
        mask_done = sem("mask_done")
        inv_done = sem("inv_done")
        neg_done = sem("neg_done")
        exp_done = sem("exp_done")
        pr_turned = sem("pr_turned")
        prT_done = sem("prT_done")
        att_done = sem("att_done")
        z1_done = sem("z1_done")
        x2_done = sem("x2_done")
        a_ready = sem("a_ready")
        act_passed, dve_passed, pool_passed = sem("act_passed"), sem("dve_passed"), sem("pool_passed")
        at_stored = [sem(f"at_stored{i}") for i in range(2)]
        x2_stored = sem("x2_stored")

        def on_dve(t, c):
            return c < 3 - t % 2

        block = ctx.enter_context(nc.Block())

        @block.sync
        def _(sp):
            sp.dma_start(bias_sb[:, :], pat_bias).then_inc(const_loaded, 16)
            sp.dma_start(w1_sb[:, :], w1).then_inc(const_loaded, 16)
            sp.dma_start(w2_sb[:, :], w2).then_inc(const_loaded, 16)
            sp.dma_start(a_sb[:, :], a_col).then_inc(const_loaded, 16)
            sp.dma_start(x_sb[:, :, :], x[0].rearrange("(t p) f -> p t f", p=P)).then_inc(x_loaded, 16)

            def batch(b, load_next):
                with sp.Fori(0, NT // 2) as i:
                    for par in range(2):
                        sp.wait_ge(ring_free, b * RING + PRE + TURN_AT + 1 + i * (2 * UNITS) + par * UNITS)
                        sp.dma_start(at_d[bass.ds(b * NT + i * 2 + par, 1), :, :].rearrange("o p n -> p (o n)"),
                                     at8[:, par, :, :].rearrange("p t i -> p (t i)").bitcast(U8)
                                     ).then_inc(at_stored[par], 16)
                if load_next:
                    sp.wait_ge(z0_done, b + 1)
                    sp.dma_start(x_sb[:, :, :],
                                 x[bass.ds(b + 1, 1), :, :].rearrange("o (t p) f -> p (o t) f", p=P)
                                 ).then_inc(x_loaded, 16)
                sp.wait_ge(x2_done, b + 1)
                sp.dma_start(x2_d[bass.ds(b, 1), :, :].rearrange("o p n -> p (o n)"),
                             x2[:, :, :].rearrange("p t f -> p (t f)")).then_inc(x2_stored, 16)

            with sp.Fori(0, B - 1) as b:
                batch(b, True)
            batch(B - 1, False)
            sp.wait_ge(x2_stored, 16 * B)
            for par in range(2):
                sp.wait_ge(at_stored[par], 8 * NT * B)

        @block.gpsimd
        def _(pool):
            ready = pool_passed
            pool.dma_start(code_sb[:, :, :], code_w).then_inc(code_loaded, 16)
            pool.memset(ones[:, :], 1.0).then_inc(id_zero, 1)
            pool.memset(ident[:, :], 0.0).then_inc(id_zero, 1)
            pool.memset(a_wide[:, :, :], 0.0).then_inc(const_built, 1)
            pool.memset(power[:, :], -0.5).then_inc(const_built, 1)
            pool.wait_ge(id_zero, 2)
            pool.affine_select(out=ident[:, :], in_=ident[:, :], compare_op=ALU.not_equal, fill=1.0,
                               base=0, pattern=[[-1, P]], channel_multiplier=1).then_inc(const_built, 1)
            pool.wait_ge(const_built, 3)
            pool.tensor_copy(ident_b[:, :], ident[:, :]).then_inc(const_built, 1)
            for g in range(2):
                if g:
                    pool.wait_ge(adj_loaded, 16)
                pool.dma_start(adj_sb[:, g * NT:(g + 1) * NT, :], adj[g].rearrange("(t p) j -> p t j", p=P)
                               ).then_inc(adj_loaded, 16)
            def split_table(b, it):
                wait_apart(pool, tab_step, (b * NT + it) * BLK + BLK, ready)
                if isinstance(it, int) and it == 1:
                    wait_apart(pool, ring_full, b * RING + PRE, ready)
                elif not isinstance(it, int):
                    wait_apart(pool, ring_full,
                               b * RING + it * UNITS + (PRE - 2 * UNITS + unit_at(0, ("table", 1)) + 1), ready)
                steps = b * (3 * NT) + it * 3
                pool.tensor_copy(tab_s[:, :, 0, :], tab[:, :, :]).then_inc(pool_step, 1)
                wait_apart(pool, pool_step, steps + 1, ready)
                pool.tensor_tensor(tab_r[:, :, :], tab[:, :, :], tab_s[:, :, 0, :], ALU.subtract).then_inc(pool_step, 1)
                wait_apart(pool, pool_step, steps + 2, ready)
                pool.tensor_copy(tab_s[:, :, 1, :], tab_r[:, :, :]).then_inc(pool_step, 1)
                wait_apart(pool, pool_step, steps + 3, ready)
                pool.tensor_tensor(tab_s[:, :, 2, :], tab_r[:, :, :], tab_s[:, :, 1, :],
                                   ALU.subtract).then_inc(table_split, 1)

            def rsqrt(index):
                wait_apart(pool, ln_stats, index + 1, ready)
                pool.tensor_scalar(rstd[:, :], mv[:, :, 1], EPS, None, ALU.add).then_inc(eps_added, 1)
                wait_apart(pool, eps_added, index + 1, ready)
                pool.tensor_tensor(rstd[:, :], rstd[:, :], power[:, :], ALU.pow).then_inc(ln_rstd, 1)

            def batch(b, load_parity):
                split_table(b, 0)
                split_table(b, 1)
                with pool.Fori(2, NT) as it:
                    split_table(b, it)
                rsqrt(b * 2)
                if load_parity is not None:
                    pool.wait_ge(adj_loaded, b * 16 + 32)
                    wait_apart(pool, adj_free, b + 1, ready)
                    pool.dma_start(adj_sb[:, bass.ds(load_parity * NT, NT), :],
                                   adj[bass.ds(b + 2, 1), :, :].rearrange("o (t p) j -> p (o t) j", p=P)
                                   ).then_inc(adj_loaded, 16)
                rsqrt(b * 2 + 1)

            with pool.Fori(0, B // 2 - 1) as pair:
                with pool.Fori(0, 2) as parity:
                    batch(pair * 2 + parity, parity)
            with pool.Fori(B - 2, B) as b:
                batch(b, None)

        @block.scalar
        def _(act):
            ready = act_passed
            act.wait_ge(const_loaded, 4 * 16)
            act.wait_ge(const_built, 4)

            def max_tile(b):
                def tile(it, known):
                    for pos, (what, u) in enumerate(tile_units(known)):
                        k = it * UNITS + (PRE + pos)
                        slot = (known + pos) % 2
                        n = it * NBLK + u
                        if what == "code":
                            wait_apart(act, ring_full, b * RING + k + 1, ready)
                            if known * NBLK + u >= 4:
                                act.wait_ge(look_full, b * LOOKS + n - 3)
                            act.activation(hot[:, (2 * (known % 2) + u) % 4, :], ringA[0:CODE, slot, :],
                                           ACT.Relu, bias=bias_sb[:, 0:1]).then_inc(ring_free, 1)
                        elif what == "turn":
                            if known >= 2:
                                act.wait_ge(at_stored[known % 2], b * (8 * NT) + it * 8 - 8 * (known % 2))
                            wait_apart(act, ring_full, b * RING + k + 1, ready)
                            act.activation(at8[:, known % 2, :, :],
                                           ringA[:, slot, :].rearrange("p (t i) -> p t i", t=NT),
                                           ACT.Copy, saturate=False).then_inc(ring_free, 1)
                        else:
                            lo, hi = SPLIT[u]
                            act.wait_ge(ring_full, b * RING + k + 1)
                            turned = ringA[0:CODE, slot, :].bitcast(BF16)[:, 0:(hi - lo) * F]
                            act.activation(look[(known + 1) % 2][:, lo:hi, :],
                                           turned.rearrange("p (k f) -> p k f", f=F),
                                           ACT.Copy).then_inc(ring_free, 1)
                return tile

            def hidden(t, c, it_base, t_all):
                return act.activation(hid[:, t % RSLOTS, c, :], q_sb[:, :], ACT.Relu,
                                      bias=k_sb[:, bass.ds(it_base + c * GROUPS + t, 1)])

            def att_tile(b):
                def tile(it, known):
                    for t in range(GROUPS):
                        if known > 0 or t >= RSLOTS:
                            act.wait_ge(score_grp, b * (NT * GROUPS) + it * GROUPS + t - RSLOTS + 1)
                        for c in range(QUADS):
                            if not on_dve(t, c):
                                last = hidden(t, c, it * PAIRS, None)
                        last.then_inc(hid_act, 1)
                        if known > 0 and t == 3:
                            exponent(b, it, known)
                        if known > 0 and t == 7:
                            copy_turned(b, it, known)
                return tile

            def exponent(b, it, known):
                if known >= 2:
                    act.wait_ge(pr_turned, b * NT + it - 1)
                act.wait_ge(neg_done, b * NT + it)
                act.activation(pr[:, :], sc[:, :], ACT.Exp, bias=neg_top[:, 0:1],
                               accum_out=total[:, 0:1]).then_inc(exp_done, 1)

            def copy_turned(b, it, known):
                if known >= 2:
                    act.wait_ge(att_done, b * NT + it - 1)
                act.wait_ge(pr_turned, b * NT + it)
                act.activation(prT[:, :, :], ringC[:, 0, :].rearrange("p (t i) -> p t i", t=NT),
                               ACT.Copy).then_inc(prT_done, 1)

            def batch(b, parity):
                for h in range(2):
                    act.wait_ge(ring_full, b * RING + h + 1)
                    src = ringA[:, h, 0:HALF].rearrange("p (t i) -> p t i", t=NT // 2)
                    dst = xT[:, h * NT // 2:(h + 1) * NT // 2, :]
                    act.activation(dst[:, :, 0:P], src, ACT.Copy)
                    act.activation(dst[:, :, P:PADDED], src[:, :, 2 * P - PADDED:P], ACT.Copy
                                   ).then_inc(ring_free, 1)
                for part, (lo, hi) in enumerate(SPLIT):
                    act.wait_ge(ring_full, b * RING + 2 + part + 1)
                    turned = ringA[0:CODE, part, :].bitcast(BF16)[:, 0:(hi - lo) * F]
                    act.activation(look[0][:, lo:hi, :], turned.rearrange("p (k f) -> p k f", f=F),
                                   ACT.Copy).then_inc(ring_free, 1)
                over_tiles(act, max_tile(b))
                act.wait_ge(x1_turned, b + 1)
                act.activation(x1T[:, :], ringC[:, 1, :], ACT.Copy).then_inc(x1T_done, 1)
                act.wait_ge(qk_done, b + 1)
                act.activation(q_sb[:, :], ringA[:, 0, :], ACT.Copy).then_inc(q_copied, 1)
                act.wait_ge(q_copied, b + 1)
                act.wait_ge(k_copied, b + 1)
                over_tiles(act, att_tile(b))
                exponent(b, NT, NT)
                copy_turned(b, NT, NT)
                for par in range(2):
                    act.wait_ge(at_stored[par], b * (8 * NT) + 8 * NT)

            over_batches(act, B, batch)

        @block.tensor
        def _(pe):
            pe.wait_ge(code_loaded, 16)
            pe.wait_ge(const_built, 4)
            pe.wait_ge(a_ready, 2)

            def look_up(b, it, known, u):
                pe.wait_ge(ring_free, b * RING + it * UNITS + (PRE + unit_at(known, ("code", u)) + 1))
                if known * NBLK + u >= 2:
                    pe.wait_ge(look_free, b * LOOKS + it * NBLK + (u - 1))
                for h in range(2):
                    mm = pe.matmul(ringC[:, u % 2, h * HALF:(h + 1) * HALF], look[known % 2][:, u, :],
                                   hot[:, (2 * (known % 2) + u) % 4, h * HALF:(h + 1) * HALF],
                                   start=True, stop=True)
                mm.then_inc(look_full, 1)

            def max_tile(b, parity):
                def tile(it, known):
                    for pos, (what, u) in enumerate(tile_units(known)):
                        k = it * UNITS + (PRE + pos)
                        slot = (known + pos) % 2
                        pe.wait_ge(ring_free, b * RING + k - 1)
                        a_tile = adj_sb[:, bass.ds(parity * NT + it, 1), :]
                        if what == "code":
                            for h in range(2):
                                mm = pe.matmul(ringA[0:CODE, slot, h * HALF:(h + 1) * HALF], code_sb[:, u, :],
                                               a_tile[:, :, h * HALF:(h + 1) * HALF].rearrange("p o j -> p (o j)"),
                                               start=True, stop=True)
                            mm.then_inc(ring_full, 1)
                            if u >= 1:
                                look_up(b, it, known, u - 1)
                            elif known > 0:
                                look_up(b, it - 1, known - 1, NBLK - 1)
                        elif what == "turn":
                            for j in range(NT):
                                mm = pe.matmul(ringA[:, slot, j * P:(j + 1) * P],
                                               a_tile[:, :, j * P:(j + 1) * P].rearrange("p o j -> p (o j)"),
                                               ident_b[:, :], start=j % 4 == 0, stop=True, skip_group_check=True)
                            mm.then_inc(ring_full, 1)
                        else:
                            if u == 0:
                                pe.wait_ge(table_split, b * NT + it + 2)
                            turn_table(slot, u).then_inc(ring_full, 1)
                return tile

            def turn_table(slot, part):
                lo, hi = SPLIT[part]
                for k in range(lo, hi):
                    mm = pe.transpose(ringA[0:CODE, slot, :].bitcast(BF16)[:, (k - lo) * F:(k - lo + 1) * F],
                                      tab_s[:, k, :, :].rearrange("p s q -> p (s q)"), ident_b[:, :])
                return mm

            def att_tile(b):
                def tile(it, known):
                    if known >= 2:
                        pe.wait_ge(max_done, b * NT + it - 1)
                    for t in range(GROUPS):
                        group = it * GROUPS + t
                        pe.wait_ge(hid_dve, b * (NT * GROUPS) + group + 1)
                        pe.wait_ge(hid_act, b * (NT * GROUPS) + group + 1)
                        for h in range(2):
                            for c in range(QUADS):
                                mm = pe.matmul(ringA[32 * c:32 * c + 32, known % 2, h * HALF:(h + 1) * HALF],
                                               a_wide[:, t, :], hid[:, t % RSLOTS, c, h * HALF:(h + 1) * HALF],
                                               start=t == 0, stop=t == GROUPS - 1, tile_position=(0, 32 * c))
                        mm.then_inc(score_grp, 1)
                        if known > 0 and t == 5:
                            turn_probs(b, it)
                        if known > 0 and t == 9:
                            attend(b, it, known)
                return tile

            def turn_probs(b, it):
                pe.wait_ge(exp_done, b * NT + it)
                for j in range(NT):
                    mm = pe.transpose(ringC[:, 0, j * P:(j + 1) * P], pr[:, j * P:(j + 1) * P], ident[:, :])
                mm.then_inc(pr_turned, 1)

            def attend(b, it, known):
                pe.wait_ge(prT_done, b * NT + it)
                if known >= 2:
                    pe.wait_ge(z1_done, b * NT + it - 1)
                for j in range(NT):
                    mm = pe.matmul(ringC[:, 1, 0:F], prT[:, j, :], x1[:, j, :], start=j == 0, stop=j == NT - 1)
                mm.then_inc(att_done, 1)

            def batch(b, parity):
                pe.wait_ge(x_loaded, b * 16 + 16)
                for h in range(2):
                    for t in range(NT // 2):
                        mm = pe.transpose(ringA[:, h, t * P:(t + 1) * P], x_sb[:, h * NT // 2 + t, :], ident[:, :])
                    mm.then_inc(ring_full, 1)
                pe.wait_ge(ring_free, b * RING + 2)
                pe.wait_ge(table_split, b * NT + 1)
                for part in range(2):
                    turn_table(part, part).then_inc(ring_full, 1)
                pe.wait_ge(adj_loaded, b * 16 + 16)
                over_tiles(pe, max_tile(b, parity))
                look_up(b, NT - 1, NT - 1, NBLK - 1)
                pe.wait_ge(best_done, b + 1)
                for t in range(NT):
                    mm = pe.transpose(ringC[:, 0, t * P:(t + 1) * P], best[:, 0, t * P:(t + 1) * P], ident[:, :])
                mm.then_inc(best_turned, 1)
                pe.wait_ge(x1_done, b + 1)
                for t in range(NT):
                    mm = pe.transpose(ringC[:, 1, t * P:(t + 1) * P], x1[:, t, :], ident[:, :])
                mm.then_inc(x1_turned, 1)
                pe.wait_ge(x1T_done, b + 1)
                for slot, w in enumerate((w1_sb, w2_sb)):
                    for h in range(2):
                        mm = pe.matmul(ringA[:, slot, h * HALF:(h + 1) * HALF], w[:, :],
                                       x1T[:, h * HALF:(h + 1) * HALF], start=True, stop=True)
                mm.then_inc(qk_done, 1)
                over_tiles(pe, att_tile(b))
                turn_probs(b, NT)
                attend(b, NT, NT)

            over_batches(pe, B, batch)

        @block.vector
        def _(dve):
            ready = dve_passed
            dve.wait_ge(const_loaded, 4 * 16)
            dve.wait_ge(const_built, 4)
            for h in range(2):
                half = slice(h * D1, (h + 1) * D1)
                flat = a_wide[half, :, :].rearrange("p t m -> p (t m)")
                diagonal = flat[:, h:h + 34 * (GROUPS - 1) + 1:34]
                dve.tensor_copy(diagonal, a_sb[half, 0:1].broadcast_to([D1, GROUPS])).then_inc(a_ready, 1)
            chain = Chain(dve, dve_step, 4, ready)

            def build_table(b, it):
                if not isinstance(it, int) or it > 0:
                    dve.wait_ge(table_split, b * NT + it)
                for place in range(BLK):
                    n = 1 << place
                    if place:
                        dve.wait_ge(tab_step, (b * NT + it) * BLK + place)
                    of_place = xT[:, bass.ds(it, 1), place:PADDED:BLK].rearrange("p o k -> p (o k)")
                    dve.tensor_tensor(tab[:, :, n:2 * n], tab[:, :, 0:n],
                                      of_place.rearrange("p (k o) -> p k o", o=1).broadcast_to([P, NBLK, n]),
                                      ALU.max).then_inc(tab_step, 1)

            def max_tile(b):
                def tile(it, known):
                    for u in range(NBLK):
                        if u == 2 and known < NT - 1:
                            build_table(b, it + 1)
                        n = it * NBLK + u
                        if known * NBLK + u >= 2:
                            dve.wait_ge(look_free, b * LOOKS + n - 1)
                        dve.wait_ge(look_full, b * LOOKS + n + 1)
                        if known == 0 and u < 2:
                            op = dve.tensor_copy(best[:, u, :], ringC[:, u, :])
                        else:
                            op = dve.tensor_tensor(best[:, u % 2, :], best[:, u % 2, :], ringC[:, u % 2, :], ALU.max)
                        op.then_inc(look_free, 1)
                return tile

            def normalise(dst, index):
                for t in range(NT):
                    op = dve.bn_stats(stats[:, t, :], z[:, t, :])
                chain.step(op)
                wait_apart(dve, dve_step, chain.base + chain.n, ready)
                for t in range(NT):
                    op = dve.bn_aggr(mv[:, t, :], stats[:, t, :])
                op.then_inc(ln_stats, 1)
                dve.wait_ge(ln_rstd, index + 1)
                for t in range(NT):
                    op = dve.tensor_scalar(dst[:, t, :], z[:, t, :], mv[:, t, 0:1], rstd[:, t:t + 1],
                                           ALU.subtract, ALU.mult)
                return op

            def att_tile(b, parity):
                def tile(it, known):
                    for t in range(GROUPS):
                        if known > 0 or t >= RSLOTS:
                            dve.wait_ge(score_grp, b * (NT * GROUPS) + it * GROUPS + t - RSLOTS + 1)
                        for c in range(QUADS):
                            if on_dve(t, c):
                                op = dve.tensor_scalar(hid[:, t % RSLOTS, c, :], q_sb[:, :],
                                                       k_sb[:, bass.ds(it * PAIRS + c * GROUPS + t, 1)], 0.0,
                                                       ALU.add, ALU.max)
                        op.then_inc(hid_dve, 1)
                        if known > 0 and t == 1:
                            row_max(b, parity, it, known)
                        if known > 0 and t == 11:
                            add_residual(b, it)
                return tile

            def row_max(b, parity, it, known):
                dve.tensor_scalar(mask[:, :],
                                  adj_sb[:, bass.ds(parity * NT + it - 1, 1), :].rearrange("p o j -> p (o j)"),
                                  0.0, NO_ATT, ALU.is_le, ALU.mult).then_inc(mask_done, 1)
                if known >= 2:
                    dve.wait_ge(exp_done, b * NT + it - 1)
                dve.wait_ge(score_grp, b * (NT * GROUPS) + it * GROUPS)
                wait_apart(dve, mask_done, b * NT + it, ready)
                dve.tensor_tensor_reduce(sc[:, :], ringA[:, (known - 1) % 2, :], mask[:, :], 1.0, -3.0e38,
                                         ALU.add, ALU.max, top[:, 0:1]).then_inc(max_done, 1)
                dve.wait_ge(max_done, b * NT + it)
                dve.tensor_scalar(neg_top[:, :], top[:, :], -1.0, None, ALU.mult).then_inc(neg_done, 1)

            def add_residual(b, it):
                dve.wait_ge(exp_done, b * NT + it)
                dve.reciprocal(inv[:, :], total[:, :]).then_inc(inv_done, 1)
                dve.wait_ge(att_done, b * NT + it)
                dve.wait_ge(inv_done, b * NT + it)
                dve.scalar_tensor_tensor(z[:, bass.ds(it - 1, 1), :].rearrange("p o f -> p (o f)"),
                                         ringC[:, 1, 0:F], inv[:, 0:1],
                                         x1[:, bass.ds(it - 1, 1), :].rearrange("p o f -> p (o f)"),
                                         ALU.mult, ALU.add).then_inc(z1_done, 1)

            def batch(b, parity):
                chain.round(b)
                dve.wait_ge(ring_free, b * RING + 2)
                chain.step(dve.tensor_reduce(low[:, 0:1], xT[:, :, :], mybir.AxisListType.XY, ALU.max))
                dve.wait_ge(dve_step, chain.base + chain.n)
                chain.step(dve.tensor_scalar(tab[:, :, 0], low[:, 0:1].broadcast_to([P, NBLK]), NO_EDGE, None, ALU.add))
                dve.wait_ge(dve_step, chain.base + chain.n)
                build_table(b, 0)
                over_tiles(dve, max_tile(b))
                dve.wait_ge(look_free, b * LOOKS + LOOKS)
                dve.tensor_tensor(best[:, 0, :], best[:, 0, :], best[:, 1, :], ALU.max).then_inc(best_done, 1)
                dve.wait_ge(best_turned, b + 1)
                dve.tensor_tensor(z[:, :, :], ringC[:, 0, :].rearrange("p (t f) -> p t f", t=NT),
                                  x_sb[:, :, :], ALU.add).then_inc(z0_done, 1)
                dve.wait_ge(z0_done, b + 1)
                op = normalise(x1, b * 2)
                op.then_inc(x1_done, 1)
                dve.wait_ge(qk_done, b + 1)
                dve.tensor_copy(k_sb[0:D1, :], ringA[0:D1, 1, 0:N:2])
                dve.tensor_copy(k_sb[D1:P, :], ringA[D1:P, 1, 1:N:2]).then_inc(k_copied, 1)
                dve.wait_ge(k_copied, b + 1)
                dve.wait_ge(q_copied, b + 1)
                over_tiles(dve, att_tile(b, parity))
                row_max(b, parity, NT, NT)
                dve.wait_ge(mask_done, b * NT + NT)
                dve.sem_inc(adj_free, 1)
                add_residual(b, NT)
                dve.wait_ge(z1_done, b * NT + NT)
                op = normalise(x2, b * 2 + 1)
                op.then_inc(x2_done, 1)

            over_batches(dve, B, batch)


def code_constants():
    import numpy as np

    weights = np.zeros((P, NBLK, PARTS, PAT), np.float32)
    for u in range(NBLK):
        for place in range(BLK):
            source = u * BLK + place
            source = source if source < P else source - (PADDED - P)
            for q in range(PAT):
                weights[source, u, :, q] += 2 * (q >> place & 1) - 1
    bits = np.array([bin(q).count("1") for q in range(PAT)], np.float32)
    return weights.reshape(P, NBLK, CODE), np.tile(1 - bits, PARTS).reshape(CODE, 1)


def graph_layers_2_3(nc, B, adj, at_d, x2_d, W2, b2, g2, be2, W3, b3, g3, be3, out):
    L2, L3 = W2.shape[1], W3.shape[1]
    PAIRED = B // 2

    with ExitStack() as ctx:
        def sb(name, shape, dt=F32):
            return ctx.enter_context(nc.sbuf_tensor(name, shape, dt))

        def sem(name):
            return ctx.enter_context(nc.semaphore(name))

        def sems(name):
            return [sem(f"{name}{q}") for q in range(2)]

        ps_h = ctx.enter_context(nc.psum_tensor("ps_h", [P, 2, N], F32))
        ps_g = ctx.enter_context(nc.psum_tensor("ps_g", [P, 2, N], F32))

        h2 = sb("h2", [P, B, N])
        affine = sb("affine", [P, 2])
        ident = sb("ident1", [P, P])
        power = sb("power1", [P, NT])
        hT = sb("hT", [P, 2, N])
        hw = sb("hw", [P, 2, PARTS, N], BF16)
        rest = sb("rest", [P, 2, N])
        x2_in = sb("x2_in", [P, 2, N])
        w2_sb = sb("w2_all", [P, L2, F])
        w3_sb = sb("w3_all", [P, L3, F])
        b2_sb, g2_sb, be2_sb = sb("b2_sb", [P, L2]), sb("g2_sb", [P, L2]), sb("be2_sb", [P, L2])
        b3_sb, g3_sb, be3_sb = (sb(n, [P, L3, F]) for n in ("b3_sb", "g3_sb", "be3_sb"))

        params_loaded = sem("params_loaded")
        ident_zero = sem("ident_zero")
        built = sem("built")
        passed = {e: sem(f"passed_{e}") for e in ("act", "dve", "pool", "pe")}
        affine_done = sem("affine_done")

        layer_2(nc, ctx, locals())
        layer_3(nc, ctx, locals())


def layer_2(nc, outer, v):
    B, L2, PAIRED = v["B"], v["L2"], v["PAIRED"]
    ps_h, ps_g, h2, affine, ident, power = (v[n] for n in ("ps_h", "ps_g", "h2", "affine", "ident", "power"))
    hT, hw, rest, x2_in = (v[n] for n in ("hT", "hw", "rest", "x2_in"))
    w2_sb, w3_sb, b2_sb, g2_sb, be2_sb = (v[n] for n in ("w2_sb", "w3_sb", "b2_sb", "g2_sb", "be2_sb"))
    at_d, x2_d, passed = v["at_d"], v["x2_d"], v["passed"]
    params_loaded, ident_zero, built, affine_done = (v[n] for n in ("params_loaded", "ident_zero", "built", "affine_done"))
    loads = [(w2_sb, v["W2"]), (w3_sb, v["W3"]), (b2_sb, v["b2"]), (g2_sb, v["g2"]), (be2_sb, v["be2"]),
             (v["b3_sb"], v["b3"]), (v["g3_sb"], v["g3"]), (v["be3_sb"], v["be3"])]
    with ExitStack() as ctx:
        def sb(name, shape, dt=F32):
            return ctx.enter_context(nc.sbuf_tensor(name, shape, dt))

        def sem(name):
            return ctx.enter_context(nc.semaphore(name))

        at = sb("at", [P, 2, NT, N], FP8)
        stats = sb("bn_st", [P, 2 * B, 6])
        mv = sb("bn_mv", [P, 2])
        rstd = sb("bn_rstd", [P, 1])
        prod = sb("bn_prod", [P, 1])

        x2_in_loaded = [sem(f"x2_in_loaded{q}") for q in range(2)]
        at_loaded = [sem(f"at_loaded{q}") for q in range(2)]
        x2_turned = sem("x2_turned")
        x2_copied = sem("x2_copied")
        hin_done, hw_done, high_done = sem("hin_done"), sem("hw_done"), sem("high_done")
        rest_done, mid_done, split_done = sem("rest_done"), sem("mid_done"), sem("split_done")
        sum_done, relu_done = sem("sum_done"), sem("relu_done")
        bn_stats_done, bn_aggr_done = sem("bn_stats_done"), sem("bn_aggr_done")
        bn_eps_added, bn_rstd_done = sem("bn_eps_added"), sem("bn_rstd_done")
        scale_done, prod_done = sem("scale_done"), sem("prod_done")

        def pipelined(eng, l, first, ahead, behind):
            ahead(l, first, 0)
            with eng.Fori(0, PAIRED - 1) as i:
                for q in range(2):
                    ahead(l, i * 2 + q + 1, 1 - q)
                    behind(l, i * 2 + q, q)
            ahead(l, B - 1, 1)
            behind(l, B - 2, 0)
            behind(l, B - 1, 1)

        block = ctx.enter_context(nc.Block())

        @block.sync
        def _(sp):
            def load_at(b, q):
                src = at_d[bass.ds(b * NT, NT), :, :].rearrange("t p n -> p t n")
                sp.dma_start(at[:, q, :, :].bitcast(U8), src).then_inc(at_loaded[q], 16)

            for dst, src in loads:
                sp.dma_start(dst[tuple([slice(None)] * len(src.shape))], src).then_inc(params_loaded, 16)
            for q in range(2):
                sp.dma_start(x2_in[:, q, :], x2_d[q]).then_inc(x2_in_loaded[q], 16)
                load_at(q, q)
            with sp.Fori(1, PAIRED) as i:
                for q in range(2):
                    sp.wait_ge(x2_turned, i * 2 + q - 1)
                    sp.dma_start(x2_in[:, q, :], x2_d[bass.ds(i * 2 + q, 1), :, :].rearrange("o p n -> p (o n)")
                                 ).then_inc(x2_in_loaded[q], 16)

            def layer(l, last):
                with sp.Fori(0, PAIRED - 1) as i:
                    for q in range(2):
                        sp.wait_ge(sum_done, l * B + i * 2 + q + 1)
                        load_at(i * 2 + q + 2, q)
                if not last:
                    for q in range(2):
                        sp.wait_ge(sum_done, l * B + B - 2 + q + 1)
                        load_at(q, q)

            with sp.Fori(0, L2 - 1) as l:
                layer(l, False)
            layer(L2 - 1, True)

        @block.gpsimd
        def _(pool):
            pool.memset(ident[:, :], 0.0).then_inc(ident_zero, 1)
            pool.memset(power[:, :], -0.5).then_inc(built, 1)
            pool.wait_ge(ident_zero, 1)
            pool.affine_select(out=ident[:, :], in_=ident[:, :], compare_op=ALU.not_equal, fill=1.0,
                               base=0, pattern=[[-1, P]], channel_multiplier=1).then_inc(built, 1)
            pool.wait_ge(built, 2)
            with pool.Fori(0, L2) as l:
                wait_apart(pool, bn_aggr_done, l + 1, passed["pool"])
                pool.tensor_scalar(rstd[:, :], mv[:, 1:2], EPS, None, ALU.add).then_inc(bn_eps_added, 1)
                wait_apart(pool, bn_eps_added, l + 1, passed["pool"])
                pool.tensor_tensor(rstd[:, :], rstd[:, :], power[:, 0:1], ALU.pow).then_inc(bn_rstd_done, 1)

        @block.tensor
        def _(pe):
            pe.wait_ge(built, 2)
            pe.wait_ge(params_loaded, 16 * len(loads))

            def turn_x2(b, q):
                pe.wait_ge(x2_in_loaded[q], (b - q) * 8 + 16)
                for t in range(NT):
                    mm = pe.transpose(ps_h[:, q, t * P:(t + 1) * P], x2_in[:, q, t * F:(t + 1) * F], ident[:, :])
                mm.then_inc(x2_turned, 1)

            for q in range(2):
                turn_x2(q, q)
            with pe.Fori(1, PAIRED) as i:
                for q in range(2):
                    pe.wait_ge(x2_copied, i * 2 + q - 1)
                    turn_x2(i * 2 + q, q)

            def project(l, b, q):
                pe.wait_ge(hin_done, l * B + b + 1)
                for t in range(NT):
                    mm = pe.matmul(ps_h[:, q, t * P:(t + 1) * P], hT[:, q, t * P:(t + 1) * P],
                                   w2_sb[:, bass.ds(l, 1), :].rearrange("p o f -> p (o f)"),
                                   start=True, stop=True)
                mm.then_inc(hw_done, 1)

            def neighbours(l, b, q):
                wait_apart(pe, split_done, l * B + b + 1, passed["pe"])
                wait_apart(pe, at_loaded[q], l * (8 * B) + (b - q) * 8 + 16, passed["pe"])
                for k in range(NT):
                    for part in range(PARTS):
                        for h in range(2):
                            mm = pe.matmul(ps_g[:, q, h * HALF:(h + 1) * HALF], hw[:, q, part, k * P:(k + 1) * P],
                                           at[:, q, h * NT // 2:(h + 1) * NT // 2, k * P:(k + 1) * P],
                                           start=(k, part) == (0, 0), stop=(k, part) == (NT - 1, PARTS - 1))
                mm.then_inc(sum_done, 1)

            with pe.Fori(0, L2) as l:
                pipelined(pe, l, 0, project, neighbours)

        @block.scalar
        def _(act):
            act.wait_ge(x2_copied, B)
            act.wait_ge(params_loaded, 16 * len(loads))

            def row(b):
                return h2[:, bass.ds(b, 1), :].rearrange("p o n -> p (o n)")

            def enter(l, b, q):
                act.activation(hT[:, q, :], row(b), ACT.Identity, bias=affine[:, 1:2],
                               scale=affine[:, 0:1]).then_inc(hin_done, 1)
                act.wait_ge(hw_done, l * B + b + 1)
                act.activation(hw[:, q, 0, :], ps_h[:, q, :], ACT.Copy).then_inc(high_done, 1)

            def leave(l, b, q):
                wait_apart(act, sum_done, l * B + b + 1, passed["act"])
                act.activation(row(b), ps_g[:, q, :], ACT.Relu, bias=b2_sb[:, bass.ds(l, 1)]
                               ).then_inc(relu_done, 1)

            with act.Fori(0, L2) as l:
                act.wait_ge(affine_done, l + 1)
                pipelined(act, l, 0, enter, leave)

        @block.vector
        def _(dve):
            dve.wait_ge(params_loaded, 16 * len(loads))
            dve.memset(affine[:, 0:1], 1.0)
            dve.memset(affine[:, 1:2], 0.0).then_inc(affine_done, 1)

            def keep_x2(b, q):
                dve.wait_ge(x2_turned, b + 1)
                dve.tensor_copy(h2[:, bass.ds(b, 1), :].rearrange("p o n -> p (o n)"), ps_h[:, q, :]
                                ).then_inc(x2_copied, 1)

            with dve.Fori(0, PAIRED) as i:
                for q in range(2):
                    keep_x2(i * 2 + q, q)

            def split(l, b, q):
                s = l * B + b + 1
                dve.wait_ge(high_done, s)
                dve.tensor_tensor(rest[:, q, :], ps_h[:, q, :], hw[:, q, 0, :], ALU.subtract).then_inc(rest_done, 1)
                dve.wait_ge(rest_done, s)
                dve.tensor_copy(hw[:, q, 1, :], rest[:, q, :]).then_inc(mid_done, 1)
                dve.wait_ge(mid_done, s)
                dve.tensor_tensor(hw[:, q, 2, :], rest[:, q, :], hw[:, q, 1, :], ALU.subtract).then_inc(split_done, 1)

            def measure(l, b, q):
                dve.wait_ge(relu_done, l * B + b + 1)
                for h in range(2):
                    op = dve.bn_stats(stats[:, bass.ds(b * 2 + h, 1), :].rearrange("p o s -> p (o s)"),
                                      h2[:, bass.ds(b, 1), h * HALF:(h + 1) * HALF].rearrange("p o n -> p (o n)"))
                op.then_inc(bn_stats_done, 1)

            with dve.Fori(0, L2) as l:
                pipelined(dve, l, 0, split, measure)
                wait_apart(dve, bn_stats_done, l * B + B, passed["dve"])
                dve.bn_aggr(mv[:, :], stats[:, :, :].rearrange("p k s -> p (k s)")).then_inc(bn_aggr_done, 1)
                dve.wait_ge(bn_rstd_done, l + 1)
                dve.tensor_tensor(affine[:, 0:1], g2_sb[:, bass.ds(l, 1)], rstd[:, :], ALU.mult).then_inc(scale_done, 1)
                dve.wait_ge(scale_done, l + 1)
                dve.tensor_tensor(prod[:, :], mv[:, 0:1], affine[:, 0:1], ALU.mult).then_inc(prod_done, 1)
                dve.wait_ge(prod_done, l + 1)
                dve.tensor_tensor(affine[:, 1:2], be2_sb[:, bass.ds(l, 1)], prod[:, :], ALU.subtract
                                  ).then_inc(affine_done, 1)


def layer_3(nc, outer, v):
    B, L2, L3, PAIRED = v["B"], v["L2"], v["L3"], v["PAIRED"]
    ps_h, ps_g, h2, affine, ident, power = (v[n] for n in ("ps_h", "ps_g", "h2", "affine", "ident", "power"))
    hT, hw, rest, x2_in = (v[n] for n in ("hT", "hw", "rest", "x2_in"))
    w3_sb, b3_sb, g3_sb, be3_sb = (v[n] for n in ("w3_sb", "b3_sb", "g3_sb", "be3_sb"))
    adj, x2_d, out, passed = v["adj"], v["x2_d"], v["out"], v["passed"]
    built, affine_done = v["built"], v["affine_done"]
    STAGES = L3 + 2
    with ExitStack() as ctx:
        def sb(name, shape, dt=F32):
            return ctx.enter_context(nc.sbuf_tensor(name, shape, dt))

        def sem(name):
            return ctx.enter_context(nc.semaphore(name))

        def sems(name):
            return [sem(f"l3_{name}{q}") for q in range(2)]

        adj_in = [sb(f"adj_in{q}", [P, NT, N], BF16) for q in range(2)]
        x3 = sb("x3", [P, 2, N])
        h = sb("h", [P, 2, N])
        hb = sb("hb", [P, 2, N])
        z = sb("z3", [P, 2, N])
        res = sb("res", [P, 2, N])
        stats = sb("st3", [P, 2, NT, 6])
        mv = sb("mv3", [P, 2, NT, 2])
        rstd = sb("rstd3", [P, 2, NT])

        adj_loaded, x2_loaded = sems("adj_loaded"), sems("x2_loaded")
        y_done, y_turned = sems("y_done"), sems("y_turned")
        z_done, st_done, mv_done = sems("z_done"), sems("st_done"), sems("mv_done")
        eps_done, rstd_done, norm_done = sems("eps_done"), sems("rstd_done"), sems("norm_done")
        scaled, shifted = sems("scaled"), sems("shifted")
        h_done, h_turned, hT_done = sems("h_done"), sems("h_turned"), sems("hT_done")
        hb_done = sems("hb_done")
        hw_done, high_done = sems("hw_done"), sems("high_done")
        rest_done, mid_done, split_done = sems("rest_done"), sems("mid_done"), sems("split_done")
        sum_done, out_stored = sems("sum_done"), sems("out_stored")

        block = ctx.enter_context(nc.Block())

        def by_node(t):
            return t.rearrange("p (t f) -> p t f", t=NT)

        @block.sync
        def _(sp):
            def load_x2(b, q):
                sp.dma_start(x2_in[:, q, :], x2_d[bass.ds(b, 1), :, :].rearrange("o p n -> p (o n)")
                             ).then_inc(x2_loaded[q], 16)

            for q in range(2):
                load_x2(q, q)
            def pair(i, last):
                if not last:
                    for q in range(2):
                        sp.wait_ge(z_done[q], i * STAGES + 1)
                        load_x2(i * 2 + 2 + q, q)
                for q in range(2):
                    sp.wait_ge(norm_done[q], i * STAGES + STAGES)
                    sp.dma_start(out[bass.ds(i * 2 + q, 1), :, :].rearrange("o (t p) f -> p (o t) f", p=P),
                                 by_node(res[:, q, :])).then_inc(out_stored[q], 16)

            with sp.Fori(0, PAIRED - 1) as i:
                pair(i, False)
            pair(PAIRED - 1, True)
            for q in range(2):
                sp.wait_ge(out_stored[q], 16 * PAIRED)

        @block.gpsimd
        def _(pool):
            def load_adj(b, q):
                pool.dma_start(adj_in[q][:, :, :], adj[bass.ds(b, 1), :, :].rearrange("o (t p) j -> p (o t) j", p=P)
                               ).then_inc(adj_loaded[q], 16)

            def rsqrt(n, q):
                wait_apart(pool, mv_done[q], n + 1, passed["pool"])
                pool.tensor_scalar(rstd[:, q, :], mv[:, q, :, 1], EPS, None, ALU.add).then_inc(eps_done[q], 1)
                wait_apart(pool, eps_done[q], n + 1, passed["pool"])
                pool.tensor_tensor(rstd[:, q, :], rstd[:, q, :], power[:, :], ALU.pow).then_inc(rstd_done[q], 1)

            def add_bias(i, l, q):
                wait_apart(pool, h_done[q], i * (L3 + 1) + l + 1, passed["pool"])
                pool.tensor_tensor(by_node(hb[:, q, :]), by_node(h[:, q, :]),
                                   b3_sb[:, l:l + 1, :].broadcast_to([P, NT, F]), ALU.add).then_inc(hb_done[q], 1)

            for q in range(2):
                load_adj(q, q)

            def pair(i, last):
                for q in range(2):
                    rsqrt(i * STAGES, q)
                for l in range(L3):
                    add_bias(i, l, 0)
                    if l > 0:
                        rsqrt(i * STAGES + l, 1)
                    add_bias(i, l, 1)
                    rsqrt(i * STAGES + 1 + l, 0)
                rsqrt(i * STAGES + L3, 1)
                if not last:
                    for q in range(2):
                        wait_apart(pool, sum_done[q], i * L3 + L3, passed["pool"])
                        load_adj(i * 2 + 2 + q, q)
                for q in range(2):
                    rsqrt(i * STAGES + STAGES - 1, q)

            with pool.Fori(0, PAIRED - 1) as i:
                pair(i, False)
            pair(PAIRED - 1, True)

        @block.tensor
        def _(pe):
            def turn(src, q):
                for t in range(NT):
                    mm = pe.transpose(ps_h[:, q, t * P:(t + 1) * P], src[:, q, t * P:(t + 1) * P], ident[:, :])
                return mm

            def project(i, l, q):
                pe.wait_ge(h_done[q], i * (L3 + 1) + l + 1)
                turn(h, q).then_inc(h_turned[q], 1)
                pe.wait_ge(hT_done[q], i * L3 + l + 1)
                for t in range(NT):
                    mm = pe.matmul(ps_h[:, q, t * P:(t + 1) * P], hT[:, q, t * P:(t + 1) * P], w3_sb[:, l, :],
                                   start=True, stop=True)
                mm.then_inc(hw_done[q], 1)

            def neighbours(i, l, q):
                pe.wait_ge(split_done[q], i * L3 + l + 1)
                if l == 0:
                    pe.wait_ge(adj_loaded[q], i * 16 + 16)
                for j in range(NT):
                    for k in range(NT):
                        for part in range(PARTS):
                            mm = pe.matmul(ps_g[:, q, j * P:(j + 1) * P], adj_in[q][:, k, j * P:(j + 1) * P],
                                           hw[:, q, part, k * P:(k + 1) * P],
                                           start=(k, part) == (0, 0), stop=(k, part) == (NT - 1, PARTS - 1))
                mm.then_inc(sum_done[q], 1)

            with pe.Fori(0, PAIRED) as i:
                for q in range(2):
                    pe.wait_ge(y_done[q], i + 1)
                    turn(hT, q).then_inc(y_turned[q], 1)
                for l in range(L3):
                    for q in range(2):
                        project(i, l, q)
                        neighbours(i, l, q)

        @block.scalar
        def _(act):
            def enter(i, q):
                b = i * 2 + q
                act.activation(hT[:, q, :], h2[:, bass.ds(b, 1), :].rearrange("p o n -> p (o n)"), ACT.Identity,
                               bias=affine[:, 1:2], scale=affine[:, 0:1]).then_inc(y_done[q], 1)

            def keep(i, q):
                act.wait_ge(norm_done[q], i * STAGES + 1)
                act.activation(h[:, q, :], x3[:, q, :], ACT.Copy).then_inc(h_done[q], 1)

            def feed(i, l, q):
                act.wait_ge(h_turned[q], i * L3 + l + 1)
                act.activation(hT[:, q, :], ps_h[:, q, :], ACT.Copy).then_inc(hT_done[q], 1)
                act.wait_ge(hw_done[q], i * L3 + l + 1)
                act.activation(hw[:, q, 0, :], ps_h[:, q, :], ACT.Copy).then_inc(high_done[q], 1)

            def relu(i, l, q):
                act.wait_ge(shifted[q], i * L3 + l + 1)
                act.activation(h[:, q, :], z[:, q, :], ACT.Relu).then_inc(h_done[q], 1)

            with act.Fori(0, PAIRED) as i:
                for q in range(2):
                    enter(i, q)
                for q in range(2):
                    keep(i, q)
                for l in range(L3):
                    feed(i, l, 0)
                    if l > 0:
                        relu(i, l - 1, 1)
                    feed(i, l, 1)
                    relu(i, l, 0)
                relu(i, L3 - 1, 1)

        @block.vector
        def _(dve):
            def normalise(i, n, q, dst):
                s = i * STAGES + n + 1
                dve.wait_ge(z_done[q], s)
                for t in range(NT):
                    op = dve.bn_stats(stats[:, q, t, :], z[:, q, t * F:(t + 1) * F])
                op.then_inc(st_done[q], 1)
                wait_apart(dve, st_done[q], s, passed["dve"])
                for t in range(NT):
                    op = dve.bn_aggr(mv[:, q, t, :], stats[:, q, t, :])
                op.then_inc(mv_done[q], 1)
                dve.wait_ge(rstd_done[q], s)
                for t in range(NT):
                    op = dve.tensor_scalar(dst[:, q, t * F:(t + 1) * F], z[:, q, t * F:(t + 1) * F],
                                           mv[:, q, t, 0:1], rstd[:, q, t:t + 1], ALU.subtract, ALU.mult)
                op.then_inc(norm_done[q], 1)

            def enter(i, q):
                dve.wait_ge(y_turned[q], i + 1)
                dve.wait_ge(x2_loaded[q], i * 16 + 16)
                dve.tensor_tensor(z[:, q, :], ps_h[:, q, :], x2_in[:, q, :], ALU.add).then_inc(z_done[q], 1)
                normalise(i, 0, q, x3)

            def split(i, l, q):
                s = i * L3 + l + 1
                dve.wait_ge(high_done[q], s)
                dve.tensor_tensor(rest[:, q, :], ps_h[:, q, :], hw[:, q, 0, :], ALU.subtract).then_inc(rest_done[q], 1)
                dve.wait_ge(rest_done[q], s)
                dve.tensor_copy(hw[:, q, 1, :], rest[:, q, :]).then_inc(mid_done[q], 1)
                dve.wait_ge(mid_done[q], s)
                dve.tensor_tensor(hw[:, q, 2, :], rest[:, q, :], hw[:, q, 1, :], ALU.subtract
                                  ).then_inc(split_done[q], 1)

            def finish(i, l, q):
                s = i * L3 + l + 1
                dve.wait_ge(hb_done[q], s)
                dve.wait_ge(sum_done[q], s)
                dve.tensor_tensor(z[:, q, :], ps_g[:, q, :], hb[:, q, :], ALU.add).then_inc(z_done[q], 1)
                normalise(i, 1 + l, q, z)
                dve.wait_ge(norm_done[q], i * STAGES + l + 2)
                dve.tensor_tensor(by_node(z[:, q, :]), by_node(z[:, q, :]),
                                  g3_sb[:, l:l + 1, :].broadcast_to([P, NT, F]), ALU.mult).then_inc(scaled[q], 1)
                dve.wait_ge(scaled[q], s)
                dve.tensor_tensor(by_node(z[:, q, :]), by_node(z[:, q, :]),
                                  be3_sb[:, l:l + 1, :].broadcast_to([P, NT, F]), ALU.add).then_inc(shifted[q], 1)

            def leave(i, q):
                dve.wait_ge(h_done[q], i * (L3 + 1) + L3 + 1)
                dve.tensor_tensor(z[:, q, :], h[:, q, :], x3[:, q, :], ALU.add).then_inc(z_done[q], 1)
                normalise(i, STAGES - 1, q, res)

            with dve.Fori(0, PAIRED) as i:
                for q in range(2):
                    enter(i, q)
                for l in range(L3):
                    split(i, l, 0)
                    if l > 0:
                        finish(i, l - 1, 1)
                    split(i, l, 1)
                    finish(i, l, 0)
                finish(i, L3 - 1, 1)
                for q in range(2):
                    leave(i, q)
                for q in range(2):
                    dve.wait_ge(out_stored[q], i * 16 + 16)


def kernel(**inputs):
    import numpy as np
    import concourse.bacc as bacc
    from concourse.bass_utils import run_bass_kernel_spmd

    def rows(a):
        return np.ascontiguousarray(np.asarray(inputs[a]))

    code, bias = code_constants()
    w1, w2, a = rows("L1_gnn_W1").T, rows("L1_gnn_W2").T, rows("L1_gnn_a").reshape(D1, 1)
    arrays = {
        "x_in": rows("x"),
        "adj_in": rows("adj"),
        "w1_in": np.concatenate([w1, w1], 1),
        "w2_in": np.concatenate([w2, w2], 1),
        "a_in": np.concatenate([a, a], 0),
        "code_in": code,
        "bias_in": bias,
        "W2_in": rows("L2_gnn_W").transpose(1, 0, 2),
        "b2_in": rows("L2_gnn_b").T,
        "g2_in": rows("L2_gnn_gamma").T,
        "be2_in": rows("L2_gnn_beta").T,
        "W3_in": rows("L3_gnn_Ws").transpose(1, 0, 2),
        "b3_in": np.broadcast_to(rows("L3_gnn_bs"), (P, 3, F)),
        "g3_in": np.broadcast_to(rows("L3_gnn_gammas"), (P, 3, F)),
        "be3_in": np.broadcast_to(rows("L3_gnn_betas"), (P, 3, F)),
    }
    arrays = {n: np.ascontiguousarray(v) for n, v in arrays.items()}
    nc = bacc.Bacc("TRN2", target_bir_lowering=False, num_devices=1)
    args = [nc.dram_tensor(n, v.shape, mybir.dt.from_np(v.dtype), kind="ExternalInput").ap()
            for n, v in arrays.items()]
    out = nc.dram_tensor("out", arrays["x_in"].shape, F32, kind="ExternalOutput").ap()
    program(nc, *args, out)
    return run_bass_kernel_spmd(nc, [arrays], core_ids=[0]).results[0]["out"]


def program(nc, x, adj, w1, w2, a, code, bias, W2, b2, g2, be2, W3, b3, g3, be3, out):
    B = x.shape[0]
    at_d = nc.dram_tensor("adj_turned", (B * NT, P, N), U8).ap()
    x2_d = nc.dram_tensor("x2_rows", (B, P, N), F32).ap()
    graph_layers_0_1(nc, B, x, adj, w1, w2, a, code, bias, at_d, x2_d)
    graph_layers_2_3(nc, B, adj, at_d, x2_d, W2, b2, g2, be2, W3, b3, g3, be3, out)
```

```python
from contextlib import ExitStack

import concourse.bass as bass
from concourse import mybir

ALU = mybir.AluOpType
ACT = mybir.ActivationFunctionType
F32 = mybir.dt.float32
BF16 = mybir.dt.bfloat16
FP8 = mybir.dt.float8e4
U8 = mybir.dt.uint8

P = 128
N = 1024
F = 128
NT = N // P
HALF = 512

BLK = 5
PAT = 1 << BLK
NBLK = -(-P // BLK)
PADDED = NBLK * BLK
PARTS = 3
CODE = PARTS * PAT
NO_EDGE = -1.0e10

D1 = 64
PAIRS = P // 2
QUADS = 4
GROUPS = PAIRS // QUADS
RSLOTS = 4
NO_ATT = -1.0e22
EPS = 1e-5


def wait_apart(eng, sem, value, ready):
    eng.wait_ge(sem, value)
    eng.sem_inc(ready, 1)


EXP_AT, PROBS_AT, ATTEND_AT = 6, 10, 13
TABLES_AT = (16, 20)
ROW_MAX_AT = 4
SCORES_FROM = 6
TABLE_AT = 4


def hidden_place(t, c):
    return (2 * (t * QUADS + c) + 1) * NBLK // (2 * PAIRS)


def score_place(t, h):
    return max(SCORES_FROM + t, hidden_place(t, QUADS - 1) + 3 + h)


SCORES = [(t, h) for t in range(GROUPS) for h in range(2)]


def tile_units(known, layer0, layer1):
    for place in range(NBLK):
        if layer0:
            yield place, "code", place
            if place == 2 and known == NT - 1:
                yield place, "x", 0
            if place == 4:
                yield place, "turn", 0
            if place in TABLES_AT:
                yield place, "table", TABLES_AT.index(place)
        if layer1 and known > 0 and place == PROBS_AT:
            yield place, "probs", 0


PRE = 3
UNITS = NBLK + 3
ALONE = PRE + UNITS * NT + 2
RING = (UNITS + 1) * NT + 2
LOOKS = NBLK * NT
BESIDE = LOOKS + NT
SPLIT = [(0, 16), (16, NBLK)]
TILE_GROUPS = NT * GROUPS
SLOTS = 3
LAG = 2
HOTS = 4
AFTER_TABLES = NBLK - 1 - TABLES_AT[1] + 1
assert 2 * NBLK % HOTS == 0 and NBLK % 2 == 0


def units_before(B, b0, b1, it, known):
    if b1 is None:
        return it * UNITS + (PRE if known < NT else PRE + 1)
    if b0 is None:
        return ALONE + (B - 1) * RING + it - (known > 0)
    extra = (-1 if 0 < known else 0) + (1 if known == NT else 0)
    return b1 * RING + it * (UNITS + 1) + (ALONE + extra)


def unit_pos(known, b1, what, u):
    return [w[1:] for w in tile_units(known, True, b1 is not None)].index((what, u))


def looks_before(B, b0, b1, it, known, u):
    if b1 is None:
        return it * NBLK + u
    atts = 0 if known == 0 else it - 1 + (u > ATTEND_AT - LAG)
    if b0 is None:
        return LOOKS + (B - 1) * BESIDE + atts
    return b1 * BESIDE + it * NBLK + (LOOKS + u) + atts


def ring_order(known, layer0, layer1):
    if known == NT:
        looks = [("look", u) for u in range(NBLK - LAG, NBLK)] + [("maxima", 0)]
        return (looks if layer0 else []) + ([("probs", 0), ("attention", 0)] if layer1 else []) + (
            [("x1", 0), ("k", 0)] if layer0 else [])
    order = []
    units = list(tile_units(known, layer0, layer1))
    for place in range(NBLK):
        for at, what, u in units:
            if at == place:
                order.append((what, u))
                if what == "code" and (u >= LAG or known > 0):
                    order.append(("look", (u - LAG) % NBLK))
        if layer1 and known > 0 and place == ATTEND_AT:
            order.append(("attention", 0))
    return order


def ring_start(known, layer0, layer1):
    if known == 0:
        return -len(ring_order(0, layer0, layer1)) % SLOTS
    return len(ring_order(NT - 1, layer0, layer1)) % SLOTS if known == NT else 0


def ring_slot(known, b0, b1, what, u=0):
    here = known + (what == "look" and u >= NBLK - LAG)
    layers = (b0 is not None, b1 is not None)
    return (ring_start(here, *layers) + ring_order(here, *layers).index((what, u))) % SLOTS


def last_in_slot(known, b0, b1, what, u):
    layers = (b0 is not None, b1 is not None)
    order, start = ring_order(known, *layers), ring_start(known, *layers)
    at = order.index((what, u))
    for i in range(at - SLOTS, -1, -SLOTS):
        return order[i], 0
    if known == 0:
        return None
    slot = (start + at) % SLOTS
    order, start = ring_order(known - 1, *layers), ring_start(known - 1, *layers)
    for i in range(len(order) - 1, -1, -1):
        if (start + i) % SLOTS == slot:
            return order[i], 1
    return None


def hot_slot(known, u):
    return (known * NBLK + u) % HOTS


def over_tiles(eng, tile):
    tile(0, 0)
    tile(1, 1)
    with eng.Fori(1, NT // 2 - 1) as i:
        tile(i * 2, 2)
        tile(i * 2 + 1, 3)
    tile(NT - 2, NT - 2)
    tile(NT - 1, NT - 1)


def interleave(known, graph0, graph1, unit, layer_1):
    units = list(tile_units(known, graph0 is not None, graph1 is not None))
    for place in range(NBLK):
        for pos, (at, what, u) in enumerate(units):
            if at == place:
                unit(pos, what, u)
        if graph1 is not None:
            layer_1(place)


def over_graphs(eng, B, tiles, boundary):
    tiles(0, None)
    boundary(0, None)
    with eng.Fori(0, B - 1) as b:
        tiles(b + 1, b)
        boundary(b + 1, b)
    tiles(None, B - 1)
    boundary(None, B - 1)


def graph_layers_0_1(nc, B, x, adj, w1, w2, a_col, code_w, pat_bias, at_d, x2_d):
    with ExitStack() as ctx:
        def sb(name, shape, dt=F32):
            return ctx.enter_context(nc.sbuf_tensor(name, shape, dt))

        def sem(name):
            return ctx.enter_context(nc.semaphore(name))

        def psum(name):
            return ctx.enter_context(nc.psum_tensor(name, [P, N], F32))

        rings = [psum(f"ring{i}") for i in range(SLOTS)]
        scores = psum("scores")

        adj_sb = sb("adj_sb", [P, 2 * NT, N], BF16)
        x_next = sb("x_next", [P, NT, F])
        x_sb = sb("x_sb", [P, NT, F])
        xT = sb("xT", [P, NT, PADDED])
        low = sb("low", [P, 1])
        tab = sb("tab", [P, NBLK, PAT])
        tab_r = sb("tab_r", [P, NBLK, PAT])
        tab_s = sb("tab_s", [P, NBLK, PARTS, PAT], BF16)
        look = [sb(f"look{i}", [CODE, NBLK, F], BF16) for i in range(2)]
        hot = sb("hot", [CODE, HOTS, N], BF16)
        best = sb("best", [P, 2, N])
        at8 = sb("at8", [P, 2, NT, P], FP8)
        code_sb = sb("code_sb", [P, NBLK, CODE], BF16)
        bias_sb = sb("bias_sb", [CODE, 1])
        ident = sb("ident0", [P, P])
        ident_b = sb("ident_b", [P, P], BF16)
        z0 = sb("z0", [P, NT, F])
        z1 = sb("z1", [P, NT, F])
        x1 = sb("x1", [P, NT, F])
        x1T = sb("x1T", [P, N])
        stats = sb("stats", [P, 2, NT, 6])
        mv = sb("mv", [P, 2, NT, 2])
        rstd = sb("rstd", [P, 2, NT])
        power = sb("power", [P, NT])
        w1_sb = sb("w1_sb", [P, 2 * D1])
        w2_sb = sb("w2_sb", [P, 2 * D1])
        a_sb = sb("a_sb", [P, 1])
        a_wide = sb("a_wide", [P, GROUPS, 32])
        q_sb = sb("q_sb", [P, N])
        k_sb = sb("k_sb", [P, N // 2])
        hid = sb("hid", [P, RSLOTS, QUADS, N])
        mask = sb("mask", [P, N])
        sc = sb("sc", [P, N])
        pr = sb("pr", [P, N])
        prT = sb("prT", [P, NT, P])
        top = sb("top", [P, 1])
        neg_top = sb("neg_top", [P, 1])
        total = sb("total", [P, 1])
        inv = sb("inv", [P, 1])
        x2 = sb("x2_sb", [P, NT, F])

        const_loaded, code_loaded, id_zero = sem("const_loaded"), sem("code_loaded"), sem("id_zero")
        const_built, a_ready = sem("const_built"), sem("a_ready")
        adj_loaded, x_loaded, x_kept = sem("adj_loaded"), sem("x_loaded"), sem("x_kept")
        unit_full, unit_free = sem("unit_full"), sem("unit_free")
        look_full, look_free = sem("look_full"), sem("look_free")
        floor_step = sem("floor_step")
        tab_step, part_step, table_split = sem("tab_step"), sem("part_step"), sem("table_split")
        best_done, best_turned = sem("best_done"), sem("best_turned")
        z0_done = sem("z0_done")
        norm_stats = [sem(f"norm_stats{i}") for i in range(2)]
        norm_aggr = [sem(f"norm_aggr{i}") for i in range(2)]
        norm_eps = [sem(f"norm_eps{i}") for i in range(2)]
        norm_rstd = [sem(f"norm_rstd{i}") for i in range(2)]
        x1_done = sem("x1_done")
        qk_done, q_copied, k_copied = sem("qk_done"), sem("q_copied"), sem("k_copied")
        hid_dve, hid_act, group_done = sem("hid_dve"), sem("hid_act"), sem("group_done")
        mask_done, max_done, neg_done, exp_done = sem("mask_done"), sem("max_done"), sem("neg_done"), sem("exp_done")
        inv_done = sem("inv_done")
        x2_done, x2_stored, x2_free = sem("x2_done"), sem("x2_stored"), sem("x2_free")
        at_stored = [sem(f"at_stored{i}") for i in range(2)]
        sp_passed = sem("sp_passed")
        act_passed, dve_passed, pool_passed = sem("act_passed"), sem("dve_passed"), sem("pool_passed")

        def before(b0, b1, it, known):
            return units_before(B, b0, b1, it, known)

        def turned_last(b0, b1, it, known):
            return before(b0, b1, it, known) + (unit_pos(known, b1, "table", 1) + 1)

        def att_number(b0, b1, it, known):
            if known == NT:
                return b1 * BESIDE + (LOOKS + BESIDE - 1) if b0 is not None else LOOKS + (B - 1) * BESIDE + NT - 1
            return looks_before(B, b0, b1, it, known, ATTEND_AT + 1 - LAG) - 1

        def ring_of(known, b0, b1, what, u=0):
            return rings[ring_slot(known, b0, b1, what, u)]

        def on_dve(t, c):
            return (t * QUADS + c) % 8 not in (1, 4, 7)

        block = ctx.enter_context(nc.Block())

        @block.sync
        def _(sp):
            sp.dma_start(x_next[:, :, :], x[0].rearrange("(t p) f -> p t f", p=P)).then_inc(x_loaded, 16)
            sp.dma_start(bias_sb[:, :], pat_bias).then_inc(const_loaded, 16)
            sp.dma_start(w1_sb[:, :], w1).then_inc(const_loaded, 16)
            sp.dma_start(w2_sb[:, :], w2).then_inc(const_loaded, 16)
            sp.dma_start(a_sb[:, :], a_col).then_inc(const_loaded, 16)
            sp.sem_inc(x2_free, 1)

            def layer_0(b, b1, after):
                sp.wait_ge(x_kept, b + 1)
                sp.dma_start(x_next[:, :, :], x[bass.ds(after, 1), :, :].rearrange("o (t p) f -> p (o t) f", p=P)
                             ).then_inc(x_loaded, 16)
                with sp.Fori(0, NT // 2) as i:
                    for par in range(2):
                        wait_apart(sp, unit_free, before(b, b1, i * 2 + par, 0)
                                   + (unit_pos(NT - 1, b1, "turn", 0) + 1), sp_passed)
                        sp.dma_start(at_d[bass.ds(b * NT + i * 2 + par, 1), :, :].rearrange("o p n -> p (o n)"),
                                     at8[:, par, :, :].rearrange("p t i -> p (t i)").bitcast(U8)
                                     ).then_inc(at_stored[par], 16)

            def store_x2(b):
                sp.wait_ge(x2_done, b + 1)
                sp.dma_start(x2_d[bass.ds(b, 1), :, :].rearrange("o p n -> p (o n)"),
                             x2[:, :, :].rearrange("p t f -> p (t f)")).then_inc(x2_stored, 16)
                sp.wait_ge(x2_stored, b * 16 + 16)
                sp.sem_inc(x2_free, 1)

            layer_0(0, None, 1)
            with sp.Fori(0, B - 2) as b:
                layer_0(b + 1, b, b + 2)
                store_x2(b)
            layer_0(B - 1, B - 2, 0)
            store_x2(B - 2)
            store_x2(B - 1)
            for par in range(2):
                sp.wait_ge(at_stored[par], 8 * NT * B)

        @block.gpsimd
        def _(pool):
            pool.dma_start(code_sb[:, :, :], code_w).then_inc(code_loaded, 16)
            pool.memset(ident[:, :], 0.0).then_inc(id_zero, 1)
            pool.memset(a_wide[:, :, :], 0.0).then_inc(const_built, 1)
            pool.memset(power[:, :], -0.5).then_inc(const_built, 1)
            pool.wait_ge(id_zero, 1)
            pool.affine_select(out=ident[:, :], in_=ident[:, :], compare_op=ALU.not_equal, fill=1.0,
                               base=0, pattern=[[-1, P]], channel_multiplier=1).then_inc(const_built, 1)
            pool.wait_ge(const_built, 3)
            pool.tensor_copy(ident_b[:, :], ident[:, :]).then_inc(const_built, 1)

            def load_adj(half, b, it):
                pool.dma_start(adj_sb[:, bass.ds(half * NT + it, 1), :],
                               adj[bass.ds(b, 1), bass.ds(it * P, P), :].rearrange("o p j -> p o j")
                               ).then_inc(adj_loaded, 16)

            def split_table(n, turned):
                wait_apart(pool, tab_step, n * BLK + BLK, pool_passed)
                if turned is not None:
                    wait_apart(pool, unit_full, turned, pool_passed)
                pool.tensor_copy(tab_s[:, :, 0, :], tab[:, :, :]).then_inc(part_step, 1)
                wait_apart(pool, part_step, n * 3 + 1, pool_passed)
                pool.tensor_tensor(tab_r[:, :, :], tab[:, :, :], tab_s[:, :, 0, :], ALU.subtract).then_inc(part_step, 1)
                wait_apart(pool, part_step, n * 3 + 2, pool_passed)
                pool.tensor_copy(tab_s[:, :, 1, :], tab_r[:, :, :]).then_inc(part_step, 1)
                wait_apart(pool, part_step, n * 3 + 3, pool_passed)
                pool.tensor_tensor(tab_s[:, :, 2, :], tab_r[:, :, :], tab_s[:, :, 1, :],
                                   ALU.subtract).then_inc(table_split, 1)

            def rsqrt(i, n):
                wait_apart(pool, norm_aggr[i], n + 1, pool_passed)
                pool.tensor_scalar(rstd[:, i, :], mv[:, i, :, 1], EPS, None, ALU.add).then_inc(norm_eps[i], 1)
                wait_apart(pool, norm_eps[i], n + 1, pool_passed)
                pool.tensor_tensor(rstd[:, i, :], rstd[:, i, :], power[:, :], ALU.pow).then_inc(norm_rstd[i], 1)

            def keep_x(n, x_turned):
                if not isinstance(n, int) or n:
                    wait_apart(pool, z0_done, n, pool_passed)
                wait_apart(pool, unit_full, x_turned, pool_passed)
                pool.tensor_copy(x_sb[:, :, :], x_next[:, :, :]).then_inc(x_kept, 1)

            def next_x_turned(b0, b1):
                return before(b0, b1, NT - 1, NT - 1) + (unit_pos(NT - 1, b1, "x", 0) + 1)

            pool.wait_ge(x_loaded, 16)
            keep_x(0, 1)
            for it in range(NT):
                if it:
                    pool.wait_ge(adj_loaded, 16 * it)
                load_adj(0, 0, it)
                if it == 1:
                    split_table(0, None)
            split_table(1, PRE)
            with pool.Fori(1, NT) as it:
                split_table(it + 1, turned_last(0, None, it - 1, 0))
                pool.wait_ge(adj_loaded, it * 16 + 16 * (NT - 1))
                load_adj(1, 1, it - 1)
            rsqrt(0, 0)
            keep_x(1, next_x_turned(0, None))
            pool.wait_ge(adj_loaded, 16 * (2 * NT - 1))
            load_adj(1, 1, NT - 1)

            def graph(b, half, more, first):
                def load_next(it):
                    if more:
                        wait_apart(pool, mask_done, b * NT + it + 1, pool_passed)
                        pool.wait_ge(adj_loaded, b * (16 * NT) + it * 16 + 16 * 2 * NT)
                        load_adj(half, b + 2, it)

                n = (b + 1) * NT
                split_table(n + 1, first)
                split_table(n + 2, turned_last(b + 1, b, 0, 0))
                load_next(0)
                with pool.Fori(2, NT) as it:
                    split_table(n + 1 + it, turned_last(b + 1, b, it - 1, 1))
                    load_next(it - 1)
                rsqrt(0, b + 1)
                if more:
                    keep_x(b + 2, next_x_turned(b + 1, b))
                rsqrt(1, b)
                load_next(NT - 1)

            with pool.Fori(0, (B - 2) // 2) as pair:
                with pool.Fori(0, 2) as half:
                    b = pair * 2 + half
                    graph(b, half, True, before(b + 1, b, 0, 0) - AFTER_TABLES)
            graph(B - 2, None, False, before(B - 1, B - 2, 0, 0) - AFTER_TABLES)
            rsqrt(1, B - 1)

        @block.scalar
        def _(act):
            act.wait_ge(const_loaded, 4 * 16)
            act.wait_ge(const_built, 4)

            def copy_x(ring):
                src = ring.rearrange("p (t i) -> p t i", t=NT)
                act.activation(xT[:, :, 0:P], src, ACT.Copy)
                act.activation(xT[:, :, P:PADDED], src[:, :, 2 * P - PADDED:P], ACT.Copy).then_inc(unit_free, 1)

            def copy_table(ring, dst, part):
                lo, hi = SPLIT[part]
                turned = ring[0:CODE, :].bitcast(BF16)[:, 0:(hi - lo) * F]
                act.activation(dst[:, lo:hi, :], turned.rearrange("p (k f) -> p k f", f=F),
                               ACT.Copy).then_inc(unit_free, 1)

            def tiles(b0, b1):
                def tile(it, known):
                    def unit(pos, what, u):
                        full = before(b0, b1, it, known) + (pos + 1)
                        ring = ring_of(known, b0, b1, what, u)
                        if what == "code":
                            wait_apart(act, unit_full, full, act_passed)
                            if known * NBLK + u >= HOTS:
                                ago = ((it, known, u - HOTS) if u >= HOTS
                                       else (it - 1, known - 1, NBLK + u - HOTS))
                                act.wait_ge(look_full, looks_before(B, b0, b1, *ago) + 1)
                            act.activation(hot[:, hot_slot(known, u), :], ring[0:CODE, :],
                                           ACT.Relu, bias=bias_sb[:, 0:1]).then_inc(unit_free, 1)
                        elif what == "turn":
                            if known >= 2:
                                act.wait_ge(at_stored[known % 2], b0 * (8 * NT) + it * 8 - 8 * (known % 2))
                            wait_apart(act, unit_full, full, act_passed)
                            act.activation(at8[:, known % 2, :, :], ring[:, :].rearrange("p (t i) -> p t i", t=NT),
                                           ACT.Copy, saturate=False).then_inc(unit_free, 1)
                        elif what == "x":
                            act.wait_ge(tab_step, b0 * (NT * BLK) + NT * BLK)
                            wait_apart(act, unit_full, full, act_passed)
                            copy_x(ring)
                        elif what == "probs":
                            copy_turned(b0, b1, it, known, pos)
                        else:
                            act.wait_ge(unit_full, full)
                            copy_table(ring, look[(known + 1) % 2], u)

                    def layer_1(place):
                        for t in range(GROUPS):
                            for c in range(QUADS):
                                if on_dve(t, c) or hidden_place(t, c) != place:
                                    continue
                                if (known > 0 or t >= RSLOTS) and c == min(c for c in range(QUADS) if not on_dve(t, c)):
                                    act.wait_ge(group_done, b1 * TILE_GROUPS + it * GROUPS + (t - RSLOTS + 1))
                                op = act.activation(hid[:, t % RSLOTS, c, :], q_sb[:, :], ACT.Relu,
                                                    bias=k_sb[:, bass.ds(it * PAIRS + (c * GROUPS + t), 1)])
                                if c == max(c for c in range(QUADS) if not on_dve(t, c)):
                                    op.then_inc(hid_act, 1)
                        if known > 0 and place == EXP_AT:
                            exponent(b1, it, known)

                    interleave(known, b0, b1, unit, layer_1)

                over_tiles(act, tile)

            def exponent(b, it, known):
                act.wait_ge(neg_done, b * NT + it)
                act.activation(pr[:, :], sc[:, :], ACT.Exp, bias=neg_top[:, 0:1],
                               accum_out=total[:, 0:1]).then_inc(exp_done, 1)

            def copy_turned(b0, b1, it, known, pos):
                if known >= 2:
                    act.wait_ge(look_full, att_number(b0, b1, it - 1, known - 1) + 1)
                act.wait_ge(unit_full, before(b0, b1, it, known) + (pos + 1))
                ring = ring_of(known, b0, b1, "probs")
                act.activation(prT[:, :, :], ring[:, :].rearrange("p (t i) -> p t i", t=NT),
                               ACT.Copy).then_inc(unit_free, 1)

            def boundary(b0, b1):
                if b1 is not None:
                    exponent(b1, NT, NT)
                    copy_turned(b0, b1, NT, NT, 0)
                if b0 is not None:
                    pos = int(b1 is not None)
                    act.wait_ge(unit_full, before(b0, b1, NT, NT) + (pos + 1))
                    act.activation(x1T[:, :], ring_of(NT, b0, b1, "x1")[:, :], ACT.Copy).then_inc(unit_free, 1)
                    act.wait_ge(qk_done, b0 + 1)
                    act.activation(q_sb[:, :], scores[:, :], ACT.Copy).then_inc(q_copied, 1)
                    act.wait_ge(q_copied, b0 + 1)
                    act.wait_ge(k_copied, b0 + 1)
                    for par in range(2):
                        act.wait_ge(at_stored[par], b0 * (8 * NT) + 8 * NT)

            act.wait_ge(unit_full, 1)
            copy_x(rings[0])
            for part in range(2):
                act.wait_ge(unit_full, 2 + part)
                copy_table(rings[1 + part], look[0], part)
            over_graphs(act, B, tiles, boundary)

        @block.tensor
        def _(pe):
            pe.wait_ge(code_loaded, 16)
            pe.wait_ge(const_built, 4)
            pe.wait_ge(a_ready, 2)

            def turn_x(ring, b):
                pe.wait_ge(x_loaded, b * 16 + 16)
                for t in range(NT):
                    mm = pe.transpose(ring[:, t * P:(t + 1) * P], x_next[:, t, :], ident[:, :])
                mm.then_inc(unit_full, 1)

            def turn_table(ring, part):
                lo, hi = SPLIT[part]
                for k in range(lo, hi):
                    mm = pe.transpose(ring[0:CODE, :].bitcast(BF16)[:, (k - lo) * F:(k - lo + 1) * F],
                                      tab_s[:, k, :, :].rearrange("p s q -> p (s q)"), ident_b[:, :])
                mm.then_inc(unit_full, 1)

            def wait_slot(b0, b1, it, known, what, u=0):
                last = last_in_slot(known, b0, b1, what, u)
                if last is None:
                    return
                (what, u), ago = last
                if what == "look":
                    assert u < NBLK - LAG or not ago
                    carried = u >= NBLK - LAG
                    pe.wait_ge(look_free, looks_before(B, b0, b1, it - ago - carried, known - ago - carried, u) + 1)
                elif what == "attention":
                    pe.wait_ge(look_free, att_number(b0, b1, it - ago, known - ago) + 1)
                elif what == "maxima":
                    pe.wait_ge(z0_done, b0 + 1)
                else:
                    pos = 0 if known - ago == NT else unit_pos(known - ago, b1, what, u) if b0 is not None else 0
                    pe.wait_ge(unit_free, before(b0, b1, it - ago, known - ago) + (pos + 1))

            def look_up(b0, b1, it, known, u, behind):
                pe.wait_ge(unit_free, before(b0, b1, it, known) + (unit_pos(known, b1, "code", u) + 1))
                wait_slot(b0, b1, it + behind, known + behind, "look", u)
                looked = ring_of(known, b0, b1, "look", u)
                for h in range(2):
                    mm = pe.matmul(looked[:, h * HALF:(h + 1) * HALF], look[known % 2][:, u, :],
                                   hot[:, hot_slot(known, u), h * HALF:(h + 1) * HALF], start=True, stop=True)
                mm.then_inc(look_full, 1)

            def score(b, n, t, h):
                if h == 0:
                    pe.wait_ge(hid_dve, b * TILE_GROUPS + n + 1)
                    pe.wait_ge(hid_act, b * TILE_GROUPS + n + 1)
                for c in range(QUADS):
                    mm = pe.matmul(scores[32 * c:32 * c + 32, h * HALF:(h + 1) * HALF],
                                   a_wide[:, t, :], hid[:, t % RSLOTS, c, h * HALF:(h + 1) * HALF],
                                   start=t == 0, stop=t == GROUPS - 1, tile_position=(0, 32 * c))
                if h == 1:
                    mm.then_inc(group_done, 1)

            def turn_probs(ring, b, it):
                pe.wait_ge(exp_done, b * NT + it)
                for j in range(NT):
                    mm = pe.transpose(ring[:, j * P:(j + 1) * P], pr[:, j * P:(j + 1) * P], ident[:, :])
                mm.then_inc(unit_full, 1)

            def attend(b0, b1, it, known):
                pe.wait_ge(unit_free, before(b0, b1, it, known) + (1 if b0 is None or known == NT
                                                                   else unit_pos(known, b1, "probs", 0) + 1))
                wait_slot(b0, b1, it, known, "attention")
                looked = ring_of(known, b0, b1, "attention")
                for j in range(NT):
                    mm = pe.matmul(looked[:, 0:F], prT[:, j, :], x1[:, j, :], start=j == 0, stop=j == NT - 1)
                mm.then_inc(look_full, 1)

            def tiles(b0, b1):
                half = b0 % 2 if b0 is not None else None

                def tile(it, known):
                    def unit(pos, what, u):
                        if what == "code" and u == 0:
                            pe.wait_ge(adj_loaded, b0 * (16 * NT) + it * 16 + 16)
                        ring = ring_of(known, b0, b1, what, u)
                        wait_slot(b0, b1, it, known, what, u)
                        if what == "probs":
                            turn_probs(ring, b1, it)
                            return
                        a_tile = adj_sb[:, bass.ds(half * NT + it, 1), :]
                        if what == "code":
                            for h in range(2):
                                mm = pe.matmul(ring[0:CODE, h * HALF:(h + 1) * HALF], code_sb[:, u, :],
                                               a_tile[:, :, h * HALF:(h + 1) * HALF].rearrange("p o j -> p (o j)"),
                                               start=True, stop=True)
                            mm.then_inc(unit_full, 1)
                            if u >= LAG:
                                look_up(b0, b1, it, known, u - LAG, 0)
                            elif known > 0:
                                look_up(b0, b1, it - 1, known - 1, NBLK - LAG + u, 1)
                        elif what == "turn":
                            for j in range(NT):
                                mm = pe.matmul(ring[:, j * P:(j + 1) * P],
                                               a_tile[:, :, j * P:(j + 1) * P].rearrange("p o j -> p (o j)"),
                                               ident_b[:, :], start=j % 4 == 0, stop=True, skip_group_check=True)
                            mm.then_inc(unit_full, 1)
                        elif what == "x":
                            turn_x(ring, b0 + 1)
                        else:
                            if u == 0:
                                pe.wait_ge(table_split, b0 * NT + it + 2)
                            turn_table(ring, u)

                    def layer_1(place):
                        if known > 0:
                            for t, h in SCORES:
                                if score_place(t, h) == place + NBLK:
                                    score(b1, it * GROUPS - GROUPS + t, t, h)
                        for t, h in SCORES:
                            if score_place(t, h) == place:
                                if (t, h) == (0, 0) and known > 0:
                                    pe.wait_ge(max_done, b1 * NT + it)
                                score(b1, it * GROUPS + t, t, h)
                        if known > 0 and place == ATTEND_AT:
                            attend(b0, b1, it, known)

                    interleave(known, b0, b1, unit, layer_1)

                over_tiles(pe, tile)

            def boundary(b0, b1):
                if b0 is not None:
                    for u in range(NBLK - LAG, NBLK):
                        look_up(b0, b1, NT - 1, NT - 1, u, 1)
                if b1 is not None:
                    for t, h in SCORES:
                        if score_place(t, h) >= NBLK:
                            score(b1, TILE_GROUPS - GROUPS + t, t, h)
                if b0 is not None:
                    pe.wait_ge(best_done, b0 + 1)
                    wait_slot(b0, b1, NT, NT, "maxima")
                    for t in range(NT):
                        mm = pe.transpose(ring_of(NT, b0, b1, "maxima")[:, t * P:(t + 1) * P], best[:, 0, t * P:(t + 1) * P], ident[:, :])
                    mm.then_inc(best_turned, 1)
                if b1 is not None:
                    wait_slot(b0, b1, NT, NT, "probs")
                    turn_probs(ring_of(NT, b0, b1, "probs"), b1, NT)
                    attend(b0, b1, NT, NT)
                if b0 is not None:
                    pos = int(b1 is not None)
                    pe.wait_ge(x1_done, b0 + 1)
                    wait_slot(b0, b1, NT, NT, "x1")
                    ring = ring_of(NT, b0, b1, "x1")
                    for t in range(NT):
                        mm = pe.transpose(ring[:, t * P:(t + 1) * P], x1[:, t, :], ident[:, :])
                    mm.then_inc(unit_full, 1)
                    pe.wait_ge(unit_free, before(b0, b1, NT, NT) + (pos + 1))
                    wait_slot(b0, b1, NT, NT, "k")
                    for dst, w in ((scores, w1_sb), (ring_of(NT, b0, b1, "k"), w2_sb)):
                        for h in range(2):
                            mm = pe.matmul(dst[:, h * HALF:(h + 1) * HALF], w[:, :],
                                           x1T[:, h * HALF:(h + 1) * HALF], start=True, stop=True)
                    mm.then_inc(qk_done, 1)
                    pe.wait_ge(k_copied, b0 + 1)
                    if b1 is not None:
                        pe.wait_ge(look_free, att_number(b0, b1, NT, NT) + 1)

            turn_x(rings[0], 0)
            pe.wait_ge(unit_free, 1)
            pe.wait_ge(table_split, 1)
            for part in range(2):
                turn_table(rings[1 + part], part)
            pe.wait_ge(unit_free, PRE)
            over_graphs(pe, B, tiles, boundary)

        @block.vector
        def _(dve):
            dve.wait_ge(const_loaded, 4 * 16)
            dve.wait_ge(const_built, 4)
            for h in range(2):
                half = slice(h * D1, (h + 1) * D1)
                flat = a_wide[half, :, :].rearrange("p t m -> p (t m)")
                diagonal = flat[:, h:h + 34 * (GROUPS - 1) + 1:34]
                dve.tensor_copy(diagonal, a_sb[half, 0:1].broadcast_to([D1, GROUPS])).then_inc(a_ready, 1)

            def floor(b):
                dve.tensor_reduce(low[:, 0:1], xT[:, :, :], mybir.AxisListType.XY, ALU.max).then_inc(floor_step, 1)
                dve.wait_ge(floor_step, b * 2 + 1)
                dve.tensor_scalar(tab[:, :, 0], low[:, 0:1].broadcast_to([P, NBLK]), NO_EDGE, None, ALU.add
                                  ).then_inc(floor_step, 1)
                dve.wait_ge(floor_step, b * 2 + 2)

            def build_table(n, it):
                for place in range(BLK):
                    m = 1 << place
                    if place:
                        dve.wait_ge(tab_step, n * BLK + place)
                    of_place = xT[:, bass.ds(it, 1), place:PADDED:BLK].rearrange("p o k -> p (o k)")
                    dve.tensor_tensor(tab[:, :, m:2 * m], tab[:, :, 0:m],
                                      of_place.rearrange("p (k o) -> p k o", o=1).broadcast_to([P, NBLK, m]),
                                      ALU.max).then_inc(tab_step, 1)

            def take_max(b0, b1, it, known, u):
                n = looks_before(B, b0, b1, it, known, u)
                if known * NBLK + u >= 2:
                    dve.wait_ge(look_free, n - 1)
                dve.wait_ge(look_full, n + 1)
                looked = ring_of(known, b0, b1, "look", u)
                if known == 0 and u < 2:
                    op = dve.tensor_copy(best[:, u, :], looked[:, :])
                else:
                    op = dve.tensor_tensor(best[:, u % 2, :], best[:, u % 2, :], looked[:, :], ALU.max)
                op.then_inc(look_free, 1)

            def measure(i, n, z):
                for t in range(NT):
                    op = dve.bn_stats(stats[:, i, t, :], z[:, t, :])
                op.then_inc(norm_stats[i], 1)
                wait_apart(dve, norm_stats[i], n + 1, dve_passed)
                for t in range(NT):
                    op = dve.bn_aggr(mv[:, i, t, :], stats[:, i, t, :])
                op.then_inc(norm_aggr[i], 1)

            def normalise(i, n, z, dst):
                dve.wait_ge(norm_rstd[i], n + 1)
                for t in range(NT):
                    op = dve.tensor_scalar(dst[:, t, :], z[:, t, :], mv[:, i, t, 0:1], rstd[:, i, t:t + 1],
                                           ALU.subtract, ALU.mult)
                return op

            def build_mask(b, it):
                half = b % 2
                dve.tensor_scalar(mask[:, :],
                                  adj_sb[:, bass.ds(half * NT + it - 1, 1), :].rearrange("p o j -> p (o j)"),
                                  0.0, NO_ATT, ALU.is_le, ALU.mult).then_inc(mask_done, 1)

            def row_max(b, it, known):
                if known >= 2:
                    dve.wait_ge(exp_done, b * NT + it - 1)
                dve.wait_ge(group_done, b * TILE_GROUPS + it * GROUPS)
                wait_apart(dve, mask_done, b * NT + it, dve_passed)
                dve.tensor_tensor_reduce(sc[:, :], scores[:, :], mask[:, :], 1.0, -3.0e38,
                                         ALU.add, ALU.max, top[:, 0:1]).then_inc(max_done, 1)
                dve.wait_ge(max_done, b * NT + it)
                dve.tensor_scalar(neg_top[:, :], top[:, :], -1.0, None, ALU.mult).then_inc(neg_done, 1)

            def add_residual(b0, b1, it, known):
                n = att_number(b0, b1, it, known)
                dve.wait_ge(exp_done, b1 * NT + it)
                dve.reciprocal(inv[:, :], total[:, :]).then_inc(inv_done, 1)
                dve.wait_ge(look_full, n + 1)
                dve.wait_ge(inv_done, b1 * NT + it)
                looked = ring_of(known, b0, b1, "attention")
                dve.scalar_tensor_tensor(z1[:, bass.ds(it - 1, 1), :].rearrange("p o f -> p (o f)"),
                                         looked[:, 0:F], inv[:, 0:1],
                                         x1[:, bass.ds(it - 1, 1), :].rearrange("p o f -> p (o f)"),
                                         ALU.mult, ALU.add).then_inc(look_free, 1)
                return n

            def tiles(b0, b1):
                def tile(it, known):
                    def unit(pos, what, u):
                        if what != "code":
                            return
                        if u >= LAG:
                            take_max(b0, b1, it, known, u - LAG)
                        elif known > 0:
                            take_max(b0, b1, it - 1, known - 1, NBLK - LAG + u)
                        table = b0 * NT + it + 1
                        if u == TABLE_AT and known < NT - 1:
                            dve.wait_ge(table_split, table)
                            build_table(table, it + 1)
                        if u == 4 and known == NT - 1:
                            dve.wait_ge(unit_free, before(b0, b1, it, known) + (unit_pos(known, b1, "x", 0) + 1))
                            dve.wait_ge(table_split, table)
                            floor(b0 + 1)
                            build_table(table, 0)

                    def layer_1(place):
                        if place == 0 and known > 0:
                            build_mask(b1, it)
                        if place == ROW_MAX_AT and known > 0:
                            row_max(b1, it, known)
                        for t in range(GROUPS):
                            own = [c for c in range(QUADS) if on_dve(t, c)]
                            for c in own:
                                if hidden_place(t, c) != place:
                                    continue
                                if c == own[0] and (known > 0 or t >= RSLOTS):
                                    dve.wait_ge(group_done, b1 * TILE_GROUPS + it * GROUPS + (t - RSLOTS + 1))
                                op = dve.tensor_scalar(hid[:, t % RSLOTS, c, :], q_sb[:, :],
                                                       k_sb[:, bass.ds(it * PAIRS + (c * GROUPS + t), 1)], 0.0,
                                                       ALU.add, ALU.max)
                                if c == own[-1]:
                                    op.then_inc(hid_dve, 1)
                        if known > 0 and place == ATTEND_AT:
                            add_residual(b0, b1, it, known)

                    interleave(known, b0, b1, unit, layer_1)

                over_tiles(dve, tile)

            def boundary(b0, b1):
                if b0 is not None:
                    for u in range(NBLK - LAG, NBLK):
                        take_max(b0, b1, NT - 1, NT - 1, u)
                    dve.wait_ge(look_free, looks_before(B, b0, b1, NT - 1, NT - 1, NBLK - 1) + 1)
                    dve.tensor_tensor(best[:, 0, :], best[:, 0, :], best[:, 1, :], ALU.max).then_inc(best_done, 1)
                if b1 is not None:
                    build_mask(b1, NT)
                    row_max(b1, NT, NT)
                if b0 is not None:
                    dve.wait_ge(best_turned, b0 + 1)
                    dve.wait_ge(x_kept, b0 + 1)
                    dve.tensor_tensor(z0[:, :, :], ring_of(NT, b0, b1, "maxima")[:, :].rearrange("p (t f) -> p t f", t=NT),
                                      x_sb[:, :, :], ALU.add).then_inc(z0_done, 1)
                    dve.wait_ge(z0_done, b0 + 1)
                    measure(0, b0, z0)
                if b1 is not None:
                    n = add_residual(b0, b1, NT, NT)
                    dve.wait_ge(look_free, n + 1)
                if b0 is not None:
                    normalise(0, b0, z0, x1).then_inc(x1_done, 1)
                if b1 is not None:
                    measure(1, b1, z1)
                if b0 is not None:
                    dve.wait_ge(qk_done, b0 + 1)
                    looked = ring_of(NT, b0, b1, "k")
                    dve.tensor_copy(k_sb[0:D1, :], looked[0:D1, 0:N:2])
                    dve.tensor_copy(k_sb[D1:P, :], looked[D1:P, 1:N:2]).then_inc(k_copied, 1)
                if b1 is not None:
                    dve.wait_ge(x2_free, b1 + 1)
                    normalise(1, b1, z1, x2).then_inc(x2_done, 1)
                if b0 is not None:
                    dve.wait_ge(k_copied, b0 + 1)
                    dve.wait_ge(q_copied, b0 + 1)

            dve.wait_ge(unit_free, 1)
            floor(0)
            build_table(0, 0)
            over_graphs(dve, B, tiles, boundary)


def code_constants():
    import numpy as np

    weights = np.zeros((P, NBLK, PARTS, PAT), np.float32)
    for u in range(NBLK):
        for place in range(BLK):
            source = u * BLK + place
            source = source if source < P else source - (PADDED - P)
            for q in range(PAT):
                weights[source, u, :, q] += 2 * (q >> place & 1) - 1
    bits = np.array([bin(q).count("1") for q in range(PAT)], np.float32)
    return weights.reshape(P, NBLK, CODE), np.tile(1 - bits, PARTS).reshape(CODE, 1)


def graph_layers_2_3(nc, B, adj, at_d, x2_d, W2, b2, g2, be2, W3, b3, g3, be3, out):
    L2, L3 = W2.shape[1], W3.shape[1]
    PAIRED = B // 2

    with ExitStack() as ctx:
        def sb(name, shape, dt=F32):
            return ctx.enter_context(nc.sbuf_tensor(name, shape, dt))

        def sem(name):
            return ctx.enter_context(nc.semaphore(name))

        def sems(name):
            return [sem(f"{name}{q}") for q in range(2)]

        ps_h = ctx.enter_context(nc.psum_tensor("ps_h", [P, 2, N], F32))
        ps_g = ctx.enter_context(nc.psum_tensor("ps_g", [P, 2, N], F32))

        h2 = sb("h2", [P, B, N])
        affine = sb("affine", [P, 2])
        ident = sb("ident1", [P, P])
        power = sb("power1", [P, NT])
        hT = sb("hT", [P, 2, N])
        hw = sb("hw", [P, 2, PARTS, N], BF16)
        rest = sb("rest", [P, 2, N])
        x2_in = sb("x2_in", [P, 2, N])
        w2_sb = sb("w2_all", [P, L2, F])
        w3_sb = sb("w3_all", [P, L3, F])
        b2_sb, g2_sb, be2_sb = sb("b2_sb", [P, L2]), sb("g2_sb", [P, L2]), sb("be2_sb", [P, L2])
        b3_sb, g3_sb, be3_sb = (sb(n, [P, L3, F]) for n in ("b3_sb", "g3_sb", "be3_sb"))

        params_loaded = sem("params_loaded")
        ident_zero = sem("ident_zero")
        built = sem("built")
        passed = {e: sem(f"passed_{e}") for e in ("act", "dve", "pool", "pe")}
        affine_done = sem("affine_done")

        layer_2(nc, ctx, locals())
        layer_3(nc, ctx, locals())


def layer_2(nc, outer, v):
    B, L2, PAIRED = v["B"], v["L2"], v["PAIRED"]
    ps_h, ps_g, h2, affine, ident, power = (v[n] for n in ("ps_h", "ps_g", "h2", "affine", "ident", "power"))
    hT, hw, rest, x2_in = (v[n] for n in ("hT", "hw", "rest", "x2_in"))
    w2_sb, w3_sb, b2_sb, g2_sb, be2_sb = (v[n] for n in ("w2_sb", "w3_sb", "b2_sb", "g2_sb", "be2_sb"))
    at_d, x2_d, passed = v["at_d"], v["x2_d"], v["passed"]
    params_loaded, ident_zero, built, affine_done = (v[n] for n in ("params_loaded", "ident_zero", "built", "affine_done"))
    loads = [(w2_sb, v["W2"]), (w3_sb, v["W3"]), (b2_sb, v["b2"]), (g2_sb, v["g2"]), (be2_sb, v["be2"]),
             (v["b3_sb"], v["b3"]), (v["g3_sb"], v["g3"]), (v["be3_sb"], v["be3"])]
    with ExitStack() as ctx:
        def sb(name, shape, dt=F32):
            return ctx.enter_context(nc.sbuf_tensor(name, shape, dt))

        def sem(name):
            return ctx.enter_context(nc.semaphore(name))

        at = sb("at", [P, 2, NT, N], FP8)
        stats = sb("bn_st", [P, 2 * B, 6])
        mv = sb("bn_mv", [P, 2])
        rstd = sb("bn_rstd", [P, 1])
        prod = sb("bn_prod", [P, 1])

        x2_in_loaded = [sem(f"x2_in_loaded{q}") for q in range(2)]
        at_loaded = [sem(f"at_loaded{q}") for q in range(2)]
        x2_turned = sem("x2_turned")
        x2_copied = sem("x2_copied")
        hin_done, hw_done, high_done = sem("hin_done"), sem("hw_done"), sem("high_done")
        rest_done, mid_done, split_done = sem("rest_done"), sem("mid_done"), sem("split_done")
        sum_done, relu_done = sem("sum_done"), sem("relu_done")
        bn_stats_done, bn_aggr_done = sem("bn_stats_done"), sem("bn_aggr_done")
        bn_eps_added, bn_rstd_done = sem("bn_eps_added"), sem("bn_rstd_done")
        scale_done, prod_done = sem("scale_done"), sem("prod_done")

        def pipelined(eng, l, first, ahead, behind):
            ahead(l, first, 0)
            with eng.Fori(0, PAIRED - 1) as i:
                for q in range(2):
                    ahead(l, i * 2 + q + 1, 1 - q)
                    behind(l, i * 2 + q, q)
            ahead(l, B - 1, 1)
            behind(l, B - 2, 0)
            behind(l, B - 1, 1)

        block = ctx.enter_context(nc.Block())

        @block.sync
        def _(sp):
            def load_at(b, q):
                src = at_d[bass.ds(b * NT, NT), :, :].rearrange("t p n -> p t n")
                sp.dma_start(at[:, q, :, :].bitcast(U8), src).then_inc(at_loaded[q], 16)

            for dst, src in loads:
                sp.dma_start(dst[tuple([slice(None)] * len(src.shape))], src).then_inc(params_loaded, 16)
            for q in range(2):
                sp.dma_start(x2_in[:, q, :], x2_d[q]).then_inc(x2_in_loaded[q], 16)
                load_at(q, q)
            with sp.Fori(1, PAIRED) as i:
                for q in range(2):
                    sp.wait_ge(x2_turned, i * 2 + q - 1)
                    sp.dma_start(x2_in[:, q, :], x2_d[bass.ds(i * 2 + q, 1), :, :].rearrange("o p n -> p (o n)")
                                 ).then_inc(x2_in_loaded[q], 16)

            def layer(l, last):
                with sp.Fori(0, PAIRED - 1) as i:
                    for q in range(2):
                        sp.wait_ge(sum_done, l * B + i * 2 + q + 1)
                        load_at(i * 2 + q + 2, q)
                if not last:
                    for q in range(2):
                        sp.wait_ge(sum_done, l * B + B - 2 + q + 1)
                        load_at(q, q)

            with sp.Fori(0, L2 - 1) as l:
                layer(l, False)
            layer(L2 - 1, True)

        @block.gpsimd
        def _(pool):
            pool.memset(ident[:, :], 0.0).then_inc(ident_zero, 1)
            pool.memset(power[:, :], -0.5).then_inc(built, 1)
            pool.wait_ge(ident_zero, 1)
            pool.affine_select(out=ident[:, :], in_=ident[:, :], compare_op=ALU.not_equal, fill=1.0,
                               base=0, pattern=[[-1, P]], channel_multiplier=1).then_inc(built, 1)
            pool.wait_ge(built, 2)
            with pool.Fori(0, L2) as l:
                wait_apart(pool, bn_aggr_done, l + 1, passed["pool"])
                pool.tensor_scalar(rstd[:, :], mv[:, 1:2], EPS, None, ALU.add).then_inc(bn_eps_added, 1)
                wait_apart(pool, bn_eps_added, l + 1, passed["pool"])
                pool.tensor_tensor(rstd[:, :], rstd[:, :], power[:, 0:1], ALU.pow).then_inc(bn_rstd_done, 1)

        @block.tensor
        def _(pe):
            pe.wait_ge(built, 2)
            pe.wait_ge(params_loaded, 16 * len(loads))

            def turn_x2(b, q):
                pe.wait_ge(x2_in_loaded[q], (b - q) * 8 + 16)
                for t in range(NT):
                    mm = pe.transpose(ps_h[:, q, t * P:(t + 1) * P], x2_in[:, q, t * F:(t + 1) * F], ident[:, :])
                mm.then_inc(x2_turned, 1)

            for q in range(2):
                turn_x2(q, q)
            with pe.Fori(1, PAIRED) as i:
                for q in range(2):
                    pe.wait_ge(x2_copied, i * 2 + q - 1)
                    turn_x2(i * 2 + q, q)

            def project(l, b, q):
                pe.wait_ge(hin_done, l * B + b + 1)
                for t in range(NT):
                    mm = pe.matmul(ps_h[:, q, t * P:(t + 1) * P], hT[:, q, t * P:(t + 1) * P],
                                   w2_sb[:, bass.ds(l, 1), :].rearrange("p o f -> p (o f)"),
                                   start=True, stop=True)
                mm.then_inc(hw_done, 1)

            def neighbours(l, b, q):
                wait_apart(pe, split_done, l * B + b + 1, passed["pe"])
                wait_apart(pe, at_loaded[q], l * (8 * B) + (b - q) * 8 + 16, passed["pe"])
                for k in range(NT):
                    for part in range(PARTS):
                        for h in range(2):
                            mm = pe.matmul(ps_g[:, q, h * HALF:(h + 1) * HALF], hw[:, q, part, k * P:(k + 1) * P],
                                           at[:, q, h * NT // 2:(h + 1) * NT // 2, k * P:(k + 1) * P],
                                           start=(k, part) == (0, 0), stop=(k, part) == (NT - 1, PARTS - 1))
                mm.then_inc(sum_done, 1)

            with pe.Fori(0, L2) as l:
                pipelined(pe, l, 0, project, neighbours)

        @block.scalar
        def _(act):
            act.wait_ge(x2_copied, B)
            act.wait_ge(params_loaded, 16 * len(loads))

            def row(b):
                return h2[:, bass.ds(b, 1), :].rearrange("p o n -> p (o n)")

            def enter(l, b, q):
                act.activation(hT[:, q, :], row(b), ACT.Identity, bias=affine[:, 1:2],
                               scale=affine[:, 0:1]).then_inc(hin_done, 1)
                act.wait_ge(hw_done, l * B + b + 1)
                act.activation(hw[:, q, 0, :], ps_h[:, q, :], ACT.Copy).then_inc(high_done, 1)

            def leave(l, b, q):
                wait_apart(act, sum_done, l * B + b + 1, passed["act"])
                act.activation(row(b), ps_g[:, q, :], ACT.Relu, bias=b2_sb[:, bass.ds(l, 1)]
                               ).then_inc(relu_done, 1)

            with act.Fori(0, L2) as l:
                act.wait_ge(affine_done, l + 1)
                pipelined(act, l, 0, enter, leave)

        @block.vector
        def _(dve):
            dve.wait_ge(params_loaded, 16 * len(loads))
            dve.memset(affine[:, 0:1], 1.0)
            dve.memset(affine[:, 1:2], 0.0).then_inc(affine_done, 1)

            def keep_x2(b, q):
                dve.wait_ge(x2_turned, b + 1)
                dve.tensor_copy(h2[:, bass.ds(b, 1), :].rearrange("p o n -> p (o n)"), ps_h[:, q, :]
                                ).then_inc(x2_copied, 1)

            with dve.Fori(0, PAIRED) as i:
                for q in range(2):
                    keep_x2(i * 2 + q, q)

            def split(l, b, q):
                s = l * B + b + 1
                dve.wait_ge(high_done, s)
                dve.tensor_tensor(rest[:, q, :], ps_h[:, q, :], hw[:, q, 0, :], ALU.subtract).then_inc(rest_done, 1)
                dve.wait_ge(rest_done, s)
                dve.tensor_copy(hw[:, q, 1, :], rest[:, q, :]).then_inc(mid_done, 1)
                dve.wait_ge(mid_done, s)
                dve.tensor_tensor(hw[:, q, 2, :], rest[:, q, :], hw[:, q, 1, :], ALU.subtract).then_inc(split_done, 1)

            def measure(l, b, q):
                dve.wait_ge(relu_done, l * B + b + 1)
                for h in range(2):
                    op = dve.bn_stats(stats[:, bass.ds(b * 2 + h, 1), :].rearrange("p o s -> p (o s)"),
                                      h2[:, bass.ds(b, 1), h * HALF:(h + 1) * HALF].rearrange("p o n -> p (o n)"))
                op.then_inc(bn_stats_done, 1)

            with dve.Fori(0, L2) as l:
                pipelined(dve, l, 0, split, measure)
                wait_apart(dve, bn_stats_done, l * B + B, passed["dve"])
                dve.bn_aggr(mv[:, :], stats[:, :, :].rearrange("p k s -> p (k s)")).then_inc(bn_aggr_done, 1)
                dve.wait_ge(bn_rstd_done, l + 1)
                dve.tensor_tensor(affine[:, 0:1], g2_sb[:, bass.ds(l, 1)], rstd[:, :], ALU.mult).then_inc(scale_done, 1)
                dve.wait_ge(scale_done, l + 1)
                dve.tensor_tensor(prod[:, :], mv[:, 0:1], affine[:, 0:1], ALU.mult).then_inc(prod_done, 1)
                dve.wait_ge(prod_done, l + 1)
                dve.tensor_tensor(affine[:, 1:2], be2_sb[:, bass.ds(l, 1)], prod[:, :], ALU.subtract
                                  ).then_inc(affine_done, 1)


def layer_3(nc, outer, v):
    B, L2, L3, PAIRED = v["B"], v["L2"], v["L3"], v["PAIRED"]
    ps_h, ps_g, h2, affine, ident, power = (v[n] for n in ("ps_h", "ps_g", "h2", "affine", "ident", "power"))
    hT, hw, rest, x2_in = (v[n] for n in ("hT", "hw", "rest", "x2_in"))
    w3_sb, b3_sb, g3_sb, be3_sb = (v[n] for n in ("w3_sb", "b3_sb", "g3_sb", "be3_sb"))
    adj, x2_d, out, passed = v["adj"], v["x2_d"], v["out"], v["passed"]
    built, affine_done = v["built"], v["affine_done"]
    STAGES = L3 + 2
    with ExitStack() as ctx:
        def sb(name, shape, dt=F32):
            return ctx.enter_context(nc.sbuf_tensor(name, shape, dt))

        def sem(name):
            return ctx.enter_context(nc.semaphore(name))

        def sems(name):
            return [sem(f"l3_{name}{q}") for q in range(2)]

        adj_in = [sb(f"adj_in{q}", [P, NT, N], BF16) for q in range(2)]
        x3 = sb("x3", [P, 2, N])
        h = sb("h", [P, 2, N])
        hb = sb("hb", [P, 2, N])
        z = sb("z3", [P, 2, N])
        res = sb("res", [P, 2, N])
        stats = sb("st3", [P, 2, NT, 6])
        mv = sb("mv3", [P, 2, NT, 2])
        rstd = sb("rstd3", [P, 2, NT])

        adj_loaded, x2_loaded = sems("adj_loaded"), sems("x2_loaded")
        y_done, y_turned = sems("y_done"), sems("y_turned")
        z_done, st_done, mv_done = sems("z_done"), sems("st_done"), sems("mv_done")
        eps_done, rstd_done, norm_done = sems("eps_done"), sems("rstd_done"), sems("norm_done")
        scaled, shifted = sems("scaled"), sems("shifted")
        h_done, h_turned, hT_done = sems("h_done"), sems("h_turned"), sems("hT_done")
        hb_done = sems("hb_done")
        hw_done, high_done = sems("hw_done"), sems("high_done")
        rest_done, mid_done, split_done = sems("rest_done"), sems("mid_done"), sems("split_done")
        sum_done, out_stored = sems("sum_done"), sems("out_stored")

        block = ctx.enter_context(nc.Block())

        def by_node(t):
            return t.rearrange("p (t f) -> p t f", t=NT)

        @block.sync
        def _(sp):
            def load_x2(b, q):
                sp.dma_start(x2_in[:, q, :], x2_d[bass.ds(b, 1), :, :].rearrange("o p n -> p (o n)")
                             ).then_inc(x2_loaded[q], 16)

            for q in range(2):
                load_x2(q, q)
            def pair(i, last):
                if not last:
                    for q in range(2):
                        sp.wait_ge(z_done[q], i * STAGES + 1)
                        load_x2(i * 2 + 2 + q, q)
                for q in range(2):
                    sp.wait_ge(norm_done[q], i * STAGES + STAGES)
                    sp.dma_start(out[bass.ds(i * 2 + q, 1), :, :].rearrange("o (t p) f -> p (o t) f", p=P),
                                 by_node(res[:, q, :])).then_inc(out_stored[q], 16)

            with sp.Fori(0, PAIRED - 1) as i:
                pair(i, False)
            pair(PAIRED - 1, True)
            for q in range(2):
                sp.wait_ge(out_stored[q], 16 * PAIRED)

        @block.gpsimd
        def _(pool):
            def load_adj(b, q):
                pool.dma_start(adj_in[q][:, :, :], adj[bass.ds(b, 1), :, :].rearrange("o (t p) j -> p (o t) j", p=P)
                               ).then_inc(adj_loaded[q], 16)

            def rsqrt(n, q):
                wait_apart(pool, mv_done[q], n + 1, passed["pool"])
                pool.tensor_scalar(rstd[:, q, :], mv[:, q, :, 1], EPS, None, ALU.add).then_inc(eps_done[q], 1)
                wait_apart(pool, eps_done[q], n + 1, passed["pool"])
                pool.tensor_tensor(rstd[:, q, :], rstd[:, q, :], power[:, :], ALU.pow).then_inc(rstd_done[q], 1)

            def add_bias(i, l, q):
                wait_apart(pool, h_done[q], i * (L3 + 1) + l + 1, passed["pool"])
                pool.tensor_tensor(by_node(hb[:, q, :]), by_node(h[:, q, :]),
                                   b3_sb[:, l:l + 1, :].broadcast_to([P, NT, F]), ALU.add).then_inc(hb_done[q], 1)

            for q in range(2):
                load_adj(q, q)

            def pair(i, last):
                for q in range(2):
                    rsqrt(i * STAGES, q)
                for l in range(L3):
                    add_bias(i, l, 0)
                    if l > 0:
                        rsqrt(i * STAGES + l, 1)
                    add_bias(i, l, 1)
                    rsqrt(i * STAGES + 1 + l, 0)
                rsqrt(i * STAGES + L3, 1)
                if not last:
                    for q in range(2):
                        wait_apart(pool, sum_done[q], i * L3 + L3, passed["pool"])
                        load_adj(i * 2 + 2 + q, q)
                for q in range(2):
                    rsqrt(i * STAGES + STAGES - 1, q)

            with pool.Fori(0, PAIRED - 1) as i:
                pair(i, False)
            pair(PAIRED - 1, True)

        @block.tensor
        def _(pe):
            def turn(src, q):
                for t in range(NT):
                    mm = pe.transpose(ps_h[:, q, t * P:(t + 1) * P], src[:, q, t * P:(t + 1) * P], ident[:, :])
                return mm

            def project(i, l, q):
                pe.wait_ge(h_done[q], i * (L3 + 1) + l + 1)
                turn(h, q).then_inc(h_turned[q], 1)
                pe.wait_ge(hT_done[q], i * L3 + l + 1)
                for t in range(NT):
                    mm = pe.matmul(ps_h[:, q, t * P:(t + 1) * P], hT[:, q, t * P:(t + 1) * P], w3_sb[:, l, :],
                                   start=True, stop=True)
                mm.then_inc(hw_done[q], 1)

            def neighbours(i, l, q):
                pe.wait_ge(split_done[q], i * L3 + l + 1)
                if l == 0:
                    pe.wait_ge(adj_loaded[q], i * 16 + 16)
                for j in range(NT):
                    for k in range(NT):
                        for part in range(PARTS):
                            mm = pe.matmul(ps_g[:, q, j * P:(j + 1) * P], adj_in[q][:, k, j * P:(j + 1) * P],
                                           hw[:, q, part, k * P:(k + 1) * P],
                                           start=(k, part) == (0, 0), stop=(k, part) == (NT - 1, PARTS - 1))
                mm.then_inc(sum_done[q], 1)

            with pe.Fori(0, PAIRED) as i:
                for q in range(2):
                    pe.wait_ge(y_done[q], i + 1)
                    turn(hT, q).then_inc(y_turned[q], 1)
                for l in range(L3):
                    for q in range(2):
                        project(i, l, q)
                        neighbours(i, l, q)

        @block.scalar
        def _(act):
            def enter(i, q):
                b = i * 2 + q
                act.activation(hT[:, q, :], h2[:, bass.ds(b, 1), :].rearrange("p o n -> p (o n)"), ACT.Identity,
                               bias=affine[:, 1:2], scale=affine[:, 0:1]).then_inc(y_done[q], 1)

            def keep(i, q):
                act.wait_ge(norm_done[q], i * STAGES + 1)
                act.activation(h[:, q, :], x3[:, q, :], ACT.Copy).then_inc(h_done[q], 1)

            def feed(i, l, q):
                act.wait_ge(h_turned[q], i * L3 + l + 1)
                act.activation(hT[:, q, :], ps_h[:, q, :], ACT.Copy).then_inc(hT_done[q], 1)
                act.wait_ge(hw_done[q], i * L3 + l + 1)
                act.activation(hw[:, q, 0, :], ps_h[:, q, :], ACT.Copy).then_inc(high_done[q], 1)

            def relu(i, l, q):
                act.wait_ge(shifted[q], i * L3 + l + 1)
                act.activation(h[:, q, :], z[:, q, :], ACT.Relu).then_inc(h_done[q], 1)

            with act.Fori(0, PAIRED) as i:
                for q in range(2):
                    enter(i, q)
                for q in range(2):
                    keep(i, q)
                for l in range(L3):
                    feed(i, l, 0)
                    if l > 0:
                        relu(i, l - 1, 1)
                    feed(i, l, 1)
                    relu(i, l, 0)
                relu(i, L3 - 1, 1)

        @block.vector
        def _(dve):
            def normalise(i, n, q, dst):
                s = i * STAGES + n + 1
                dve.wait_ge(z_done[q], s)
                for t in range(NT):
                    op = dve.bn_stats(stats[:, q, t, :], z[:, q, t * F:(t + 1) * F])
                op.then_inc(st_done[q], 1)
                wait_apart(dve, st_done[q], s, passed["dve"])
                for t in range(NT):
                    op = dve.bn_aggr(mv[:, q, t, :], stats[:, q, t, :])
                op.then_inc(mv_done[q], 1)
                dve.wait_ge(rstd_done[q], s)
                for t in range(NT):
                    op = dve.tensor_scalar(dst[:, q, t * F:(t + 1) * F], z[:, q, t * F:(t + 1) * F],
                                           mv[:, q, t, 0:1], rstd[:, q, t:t + 1], ALU.subtract, ALU.mult)
                op.then_inc(norm_done[q], 1)

            def enter(i, q):
                dve.wait_ge(y_turned[q], i + 1)
                dve.wait_ge(x2_loaded[q], i * 16 + 16)
                dve.tensor_tensor(z[:, q, :], ps_h[:, q, :], x2_in[:, q, :], ALU.add).then_inc(z_done[q], 1)
                normalise(i, 0, q, x3)

            def split(i, l, q):
                s = i * L3 + l + 1
                dve.wait_ge(high_done[q], s)
                dve.tensor_tensor(rest[:, q, :], ps_h[:, q, :], hw[:, q, 0, :], ALU.subtract).then_inc(rest_done[q], 1)
                dve.wait_ge(rest_done[q], s)
                dve.tensor_copy(hw[:, q, 1, :], rest[:, q, :]).then_inc(mid_done[q], 1)
                dve.wait_ge(mid_done[q], s)
                dve.tensor_tensor(hw[:, q, 2, :], rest[:, q, :], hw[:, q, 1, :], ALU.subtract
                                  ).then_inc(split_done[q], 1)

            def finish(i, l, q):
                s = i * L3 + l + 1
                dve.wait_ge(hb_done[q], s)
                dve.wait_ge(sum_done[q], s)
                dve.tensor_tensor(z[:, q, :], ps_g[:, q, :], hb[:, q, :], ALU.add).then_inc(z_done[q], 1)
                normalise(i, 1 + l, q, z)
                dve.wait_ge(norm_done[q], i * STAGES + l + 2)
                dve.tensor_tensor(by_node(z[:, q, :]), by_node(z[:, q, :]),
                                  g3_sb[:, l:l + 1, :].broadcast_to([P, NT, F]), ALU.mult).then_inc(scaled[q], 1)
                dve.wait_ge(scaled[q], s)
                dve.tensor_tensor(by_node(z[:, q, :]), by_node(z[:, q, :]),
                                  be3_sb[:, l:l + 1, :].broadcast_to([P, NT, F]), ALU.add).then_inc(shifted[q], 1)

            def leave(i, q):
                dve.wait_ge(h_done[q], i * (L3 + 1) + L3 + 1)
                dve.tensor_tensor(z[:, q, :], h[:, q, :], x3[:, q, :], ALU.add).then_inc(z_done[q], 1)
                normalise(i, STAGES - 1, q, res)

            with dve.Fori(0, PAIRED) as i:
                for q in range(2):
                    enter(i, q)
                for l in range(L3):
                    split(i, l, 0)
                    if l > 0:
                        finish(i, l - 1, 1)
                    split(i, l, 1)
                    finish(i, l, 0)
                finish(i, L3 - 1, 1)
                for q in range(2):
                    leave(i, q)
                for q in range(2):
                    dve.wait_ge(out_stored[q], i * 16 + 16)


def kernel(**inputs):
    import numpy as np
    import concourse.bacc as bacc
    from concourse.bass_utils import run_bass_kernel_spmd

    def rows(a):
        return np.ascontiguousarray(np.asarray(inputs[a]))

    code, bias = code_constants()
    w1, w2, a = rows("L1_gnn_W1").T, rows("L1_gnn_W2").T, rows("L1_gnn_a").reshape(D1, 1)
    arrays = {
        "x_in": rows("x"),
        "adj_in": rows("adj"),
        "w1_in": np.concatenate([w1, w1], 1),
        "w2_in": np.concatenate([w2, w2], 1),
        "a_in": np.concatenate([a, a], 0),
        "code_in": code,
        "bias_in": bias,
        "W2_in": rows("L2_gnn_W").transpose(1, 0, 2),
        "b2_in": rows("L2_gnn_b").T,
        "g2_in": rows("L2_gnn_gamma").T,
        "be2_in": rows("L2_gnn_beta").T,
        "W3_in": rows("L3_gnn_Ws").transpose(1, 0, 2),
        "b3_in": np.broadcast_to(rows("L3_gnn_bs"), (P, 3, F)),
        "g3_in": np.broadcast_to(rows("L3_gnn_gammas"), (P, 3, F)),
        "be3_in": np.broadcast_to(rows("L3_gnn_betas"), (P, 3, F)),
    }
    arrays = {n: np.ascontiguousarray(v) for n, v in arrays.items()}
    nc = bacc.Bacc("TRN2", target_bir_lowering=False, num_devices=1)
    args = [nc.dram_tensor(n, v.shape, mybir.dt.from_np(v.dtype), kind="ExternalInput").ap()
            for n, v in arrays.items()]
    out = nc.dram_tensor("out", arrays["x_in"].shape, F32, kind="ExternalOutput").ap()
    program(nc, *args, out)
    return run_bass_kernel_spmd(nc, [arrays], core_ids=[0]).results[0]["out"]


def program(nc, x, adj, w1, w2, a, code, bias, W2, b2, g2, be2, W3, b3, g3, be3, out):
    B = x.shape[0]
    at_d = nc.dram_tensor("adj_turned", (B * NT, P, N), U8).ap()
    x2_d = nc.dram_tensor("x2_rows", (B, P, N), F32).ap()
    graph_layers_0_1(nc, B, x, adj, w1, w2, a, code, bias, at_d, x2_d)
    graph_layers_2_3(nc, B, adj, at_d, x2_d, W2, b2, g2, be2, W3, b3, g3, be3, out)
```

```python
from contextlib import ExitStack

import concourse.bass as bass
from concourse import mybir

ALU = mybir.AluOpType
ACT = mybir.ActivationFunctionType
F32 = mybir.dt.float32
BF16 = mybir.dt.bfloat16
FP8 = mybir.dt.float8e4
U8 = mybir.dt.uint8

P = 128
N = 1024
F = 128
NT = N // P
HALF = 512

BLK = 5
PAT = 1 << BLK
NBLK = -(-P // BLK)
PADDED = NBLK * BLK
PARTS = 3
CODE = PARTS * PAT
NO_EDGE = -1.0e10

D1 = 64
PAIRS = P // 2
QUADS = 4
GROUPS = PAIRS // QUADS
RSLOTS = 4
NO_ATT = -1.0e22
EPS = 1e-5


def wait_apart(eng, sem, value, ready):
    eng.wait_ge(sem, value)
    eng.sem_inc(ready, 1)


ROW_MAX_AT, EXP_AT, PROBS_AT, ATTEND_AT = 4, 6, 9, 13
SCORES_FROM = 6
TABLE_AT = 4
TABLES_AT = (17, 22)


def hidden_place(t, c):
    return (2 * (t * QUADS + c) + 1) * NBLK // (2 * PAIRS)


def score_place(t, h):
    return max(SCORES_FROM + t, hidden_place(t, QUADS - 1) + 3 + h)


SCORES = [(t, h) for t in range(GROUPS) for h in range(2)]


def tile_units(known, layer0, layer1):
    for place in range(NBLK):
        if layer0:
            yield place, "code", place
            if place == 2 and known == NT - 1:
                yield place, "x", 0
            if place == 4:
                yield place, "turn", 0
            if place in TABLES_AT:
                yield place, "table", TABLES_AT.index(place)
        if layer1 and known > 0 and place == PROBS_AT:
            yield place, "probs", 0


PRE = 3
UNITS = NBLK + 3
ALONE = PRE + UNITS * NT + 2
RING = (UNITS + 1) * NT + 2
LOOKS = NBLK * NT
BESIDE = LOOKS + NT
SPLIT = [(0, 16), (16, NBLK)]
TILE_GROUPS = NT * GROUPS
SLOTS = 3
LAG = 2
HOTS = 4
AFTER_TABLES = NBLK - 1 - TABLES_AT[1] + 1
assert 2 * NBLK % HOTS == 0 and NBLK % 2 == 0


def units_before(B, b0, b1, it, known):
    if b1 is None:
        return it * UNITS + (PRE if known < NT else PRE + 1)
    if b0 is None:
        return ALONE + (B - 1) * RING + it - (known > 0)
    extra = (-1 if 0 < known else 0) + (1 if known == NT else 0)
    return b1 * RING + it * (UNITS + 1) + (ALONE + extra)


def unit_pos(known, b1, what, u):
    return [w[1:] for w in tile_units(known, True, b1 is not None)].index((what, u))


def looks_before(B, b0, b1, it, known, u):
    if b1 is None:
        return it * NBLK + u
    atts = 0 if known == 0 else it - 1 + (u > ATTEND_AT - LAG)
    if b0 is None:
        return LOOKS + (B - 1) * BESIDE + atts
    return b1 * BESIDE + it * NBLK + (LOOKS + u) + atts


def ring_order(known, layer0, layer1):
    if known == NT:
        looks = [("look", u) for u in range(NBLK - LAG, NBLK)] + [("maxima", 0)]
        return (looks if layer0 else []) + ([("probs", 0), ("attention", 0)] if layer1 else []) + (
            [("x1", 0), ("k", 0)] if layer0 else [])
    order = []
    units = list(tile_units(known, layer0, layer1))
    for place in range(NBLK):
        for at, what, u in units:
            if at == place:
                order.append((what, u))
                if what == "code" and (u >= LAG or known > 0):
                    order.append(("look", (u - LAG) % NBLK))
        if layer1 and known > 0 and place == ATTEND_AT:
            order.append(("attention", 0))
    return order


def ring_start(known, layer0, layer1):
    if known == 0:
        return -len(ring_order(0, layer0, layer1)) % SLOTS
    return len(ring_order(NT - 1, layer0, layer1)) % SLOTS if known == NT else 0


def ring_slot(known, b0, b1, what, u=0):
    here = known + (what == "look" and u >= NBLK - LAG)
    layers = (b0 is not None, b1 is not None)
    return (ring_start(here, *layers) + ring_order(here, *layers).index((what, u))) % SLOTS


def last_in_slot(known, b0, b1, what, u):
    layers = (b0 is not None, b1 is not None)
    order, start = ring_order(known, *layers), ring_start(known, *layers)
    at = order.index((what, u))
    for i in range(at - SLOTS, -1, -SLOTS):
        return order[i], 0
    if known == 0:
        return None
    slot = (start + at) % SLOTS
    order, start = ring_order(known - 1, *layers), ring_start(known - 1, *layers)
    for i in range(len(order) - 1, -1, -1):
        if (start + i) % SLOTS == slot:
            return order[i], 1
    return None


def hot_slot(known, u):
    return (known * NBLK + u) % HOTS


def over_tiles(eng, tile):
    tile(0, 0)
    tile(1, 1)
    with eng.Fori(1, NT // 2 - 1) as i:
        tile(i * 2, 2)
        tile(i * 2 + 1, 3)
    tile(NT - 2, NT - 2)
    tile(NT - 1, NT - 1)


def interleave(known, graph0, graph1, unit, layer_1):
    units = list(tile_units(known, graph0 is not None, graph1 is not None))
    for place in range(NBLK):
        for pos, (at, what, u) in enumerate(units):
            if at == place:
                unit(pos, what, u)
        if graph1 is not None:
            layer_1(place)


def over_graphs(eng, B, tiles, boundary):
    tiles(0, None)
    boundary(0, None)
    with eng.Fori(0, B - 1) as b:
        tiles(b + 1, b)
        boundary(b + 1, b)
    tiles(None, B - 1)
    boundary(None, B - 1)


def graph_layers_0_1(nc, B, x, adj, w1, w2, a_col, code_w, pat_bias, at_d, x2_d):
    with ExitStack() as ctx:
        def sb(name, shape, dt=F32):
            return ctx.enter_context(nc.sbuf_tensor(name, shape, dt))

        def sem(name):
            return ctx.enter_context(nc.semaphore(name))

        def psum(name):
            return ctx.enter_context(nc.psum_tensor(name, [P, N], F32))

        rings = [psum(f"ring{i}") for i in range(SLOTS)]
        scores = psum("scores")

        adj_sb = sb("adj_sb", [P, 2 * NT, N], BF16)
        x_next = sb("x_next", [P, NT, F])
        x_sb = sb("x_sb", [P, NT, F])
        xT = sb("xT", [P, NT, PADDED])
        low = sb("low", [P, 1])
        tab = sb("tab", [P, NBLK, PAT])
        tab_r = sb("tab_r", [P, NBLK, PAT])
        tab_s = sb("tab_s", [P, NBLK, PARTS, PAT], BF16)
        look = [sb(f"look{i}", [CODE, NBLK, F], BF16) for i in range(2)]
        hot = sb("hot", [CODE, HOTS, N], BF16)
        best = sb("best", [P, 2, N])
        at8 = sb("at8", [P, 2, NT, P], FP8)
        code_sb = sb("code_sb", [P, NBLK, CODE], BF16)
        bias_sb = sb("bias_sb", [CODE, 1])
        ident = sb("ident0", [P, P])
        ident_b = sb("ident_b", [P, P], BF16)
        z0 = sb("z0", [P, NT, F])
        z1 = sb("z1", [P, NT, F])
        x1 = sb("x1", [P, NT, F])
        x1T = sb("x1T", [P, N])
        stats = sb("stats", [P, 2, NT, 6])
        mv = sb("mv", [P, 2, NT, 2])
        rstd = sb("rstd", [P, 2, NT])
        power = sb("power", [P, NT])
        w1_sb = sb("w1_sb", [P, 2 * D1])
        w2_sb = sb("w2_sb", [P, 2 * D1])
        a_sb = sb("a_sb", [P, 1])
        a_wide = sb("a_wide", [P, GROUPS, 32])
        q_sb = sb("q_sb", [P, N])
        k_sb = sb("k_sb", [P, N // 2])
        hid = sb("hid", [P, RSLOTS, QUADS, N])
        mask = sb("mask", [P, N])
        sc = sb("sc", [P, N])
        pr = sb("pr", [P, N])
        prT = sb("prT", [P, NT, P])
        top = sb("top", [P, 1])
        neg_top = sb("neg_top", [P, 1])
        total = sb("total", [P, 1])
        inv = sb("inv", [P, 1])
        x2 = sb("x2_sb", [P, NT, F])

        const_loaded, code_loaded, id_zero = sem("const_loaded"), sem("code_loaded"), sem("id_zero")
        const_built, a_ready = sem("const_built"), sem("a_ready")
        adj_loaded, x_loaded, x_kept = sem("adj_loaded"), sem("x_loaded"), sem("x_kept")
        unit_full, unit_free = sem("unit_full"), sem("unit_free")
        look_full, look_free = sem("look_full"), sem("look_free")
        floor_step = sem("floor_step")
        tab_step, part_step, table_split = sem("tab_step"), sem("part_step"), sem("table_split")
        best_done, best_turned = sem("best_done"), sem("best_turned")
        z0_done = sem("z0_done")
        norm_stats = [sem(f"norm_stats{i}") for i in range(2)]
        norm_aggr = [sem(f"norm_aggr{i}") for i in range(2)]
        norm_eps = [sem(f"norm_eps{i}") for i in range(2)]
        norm_rstd = [sem(f"norm_rstd{i}") for i in range(2)]
        x1_done = sem("x1_done")
        qk_done, q_copied, k_copied = sem("qk_done"), sem("q_copied"), sem("k_copied")
        hid_dve, hid_act, group_done = sem("hid_dve"), sem("hid_act"), sem("group_done")
        mask_done, max_done, neg_done, exp_done = sem("mask_done"), sem("max_done"), sem("neg_done"), sem("exp_done")
        inv_done = sem("inv_done")
        x2_done, x2_stored, x2_free = sem("x2_done"), sem("x2_stored"), sem("x2_free")
        at_stored = [sem(f"at_stored{i}") for i in range(2)]
        sp_passed = sem("sp_passed")
        act_passed, dve_passed, pool_passed = sem("act_passed"), sem("dve_passed"), sem("pool_passed")

        def before(b0, b1, it, known):
            return units_before(B, b0, b1, it, known)

        def turned_last(b0, b1, it, known):
            return before(b0, b1, it, known) + (unit_pos(known, b1, "table", 1) + 1)

        def att_number(b0, b1, it, known):
            if known == NT:
                return b1 * BESIDE + (LOOKS + BESIDE - 1) if b0 is not None else LOOKS + (B - 1) * BESIDE + NT - 1
            return looks_before(B, b0, b1, it, known, ATTEND_AT + 1 - LAG) - 1

        def ring_of(known, b0, b1, what, u=0):
            return rings[ring_slot(known, b0, b1, what, u)]

        def on_dve(t, c):
            return (t * QUADS + c) % 8 not in (1, 4, 7)

        block = ctx.enter_context(nc.Block())

        @block.sync
        def _(sp):
            sp.dma_start(x_next[:, :, :], x[0].rearrange("(t p) f -> p t f", p=P)).then_inc(x_loaded, 16)
            sp.dma_start(bias_sb[:, :], pat_bias).then_inc(const_loaded, 16)
            sp.dma_start(w1_sb[:, :], w1).then_inc(const_loaded, 16)
            sp.dma_start(w2_sb[:, :], w2).then_inc(const_loaded, 16)
            sp.dma_start(a_sb[:, :], a_col).then_inc(const_loaded, 16)
            sp.sem_inc(x2_free, 1)

            def layer_0(b, b1, after):
                sp.wait_ge(x_kept, b + 1)
                sp.dma_start(x_next[:, :, :], x[bass.ds(after, 1), :, :].rearrange("o (t p) f -> p (o t) f", p=P)
                             ).then_inc(x_loaded, 16)
                with sp.Fori(0, NT // 2) as i:
                    for par in range(2):
                        wait_apart(sp, unit_free, before(b, b1, i * 2 + par, 0)
                                   + (unit_pos(NT - 1, b1, "turn", 0) + 1), sp_passed)
                        sp.dma_start(at_d[bass.ds(b * NT + i * 2 + par, 1), :, :].rearrange("o p n -> p (o n)"),
                                     at8[:, par, :, :].rearrange("p t i -> p (t i)").bitcast(U8)
                                     ).then_inc(at_stored[par], 16)

            def store_x2(b):
                sp.wait_ge(x2_done, b + 1)
                sp.dma_start(x2_d[bass.ds(b, 1), :, :].rearrange("o p n -> p (o n)"),
                             x2[:, :, :].rearrange("p t f -> p (t f)")).then_inc(x2_stored, 16)
                sp.wait_ge(x2_stored, b * 16 + 16)
                sp.sem_inc(x2_free, 1)

            layer_0(0, None, 1)
            with sp.Fori(0, B - 2) as b:
                layer_0(b + 1, b, b + 2)
                store_x2(b)
            layer_0(B - 1, B - 2, 0)
            store_x2(B - 2)
            store_x2(B - 1)
            for par in range(2):
                sp.wait_ge(at_stored[par], 8 * NT * B)

        @block.gpsimd
        def _(pool):
            pool.dma_start(code_sb[:, :, :], code_w).then_inc(code_loaded, 16)
            pool.memset(ident[:, :], 0.0).then_inc(id_zero, 1)
            pool.memset(a_wide[:, :, :], 0.0).then_inc(const_built, 1)
            pool.memset(power[:, :], -0.5).then_inc(const_built, 1)
            pool.wait_ge(id_zero, 1)
            pool.affine_select(out=ident[:, :], in_=ident[:, :], compare_op=ALU.not_equal, fill=1.0,
                               base=0, pattern=[[-1, P]], channel_multiplier=1).then_inc(const_built, 1)
            pool.wait_ge(const_built, 3)
            pool.tensor_copy(ident_b[:, :], ident[:, :]).then_inc(const_built, 1)

            def load_adj(half, b, it):
                pool.dma_start(adj_sb[:, bass.ds(half * NT + it, 1), :],
                               adj[bass.ds(b, 1), bass.ds(it * P, P), :].rearrange("o p j -> p o j")
                               ).then_inc(adj_loaded, 16)

            def split_table(n, turned):
                wait_apart(pool, tab_step, n * BLK + BLK, pool_passed)
                if turned is not None:
                    wait_apart(pool, unit_full, turned, pool_passed)
                pool.tensor_copy(tab_s[:, :, 0, :], tab[:, :, :]).then_inc(part_step, 1)
                wait_apart(pool, part_step, n * 3 + 1, pool_passed)
                pool.tensor_tensor(tab_r[:, :, :], tab[:, :, :], tab_s[:, :, 0, :], ALU.subtract).then_inc(part_step, 1)
                wait_apart(pool, part_step, n * 3 + 2, pool_passed)
                pool.tensor_copy(tab_s[:, :, 1, :], tab_r[:, :, :]).then_inc(part_step, 1)
                wait_apart(pool, part_step, n * 3 + 3, pool_passed)
                pool.tensor_tensor(tab_s[:, :, 2, :], tab_r[:, :, :], tab_s[:, :, 1, :],
                                   ALU.subtract).then_inc(table_split, 1)

            def rsqrt(i, n):
                wait_apart(pool, norm_aggr[i], n + 1, pool_passed)
                pool.tensor_scalar(rstd[:, i, :], mv[:, i, :, 1], EPS, None, ALU.add).then_inc(norm_eps[i], 1)
                wait_apart(pool, norm_eps[i], n + 1, pool_passed)
                pool.tensor_tensor(rstd[:, i, :], rstd[:, i, :], power[:, :], ALU.pow).then_inc(norm_rstd[i], 1)

            def keep_x(n, x_turned):
                if not isinstance(n, int) or n:
                    wait_apart(pool, z0_done, n, pool_passed)
                wait_apart(pool, unit_full, x_turned, pool_passed)
                pool.tensor_copy(x_sb[:, :, :], x_next[:, :, :]).then_inc(x_kept, 1)

            def next_x_turned(b0, b1):
                return before(b0, b1, NT - 1, NT - 1) + (unit_pos(NT - 1, b1, "x", 0) + 1)

            pool.wait_ge(x_loaded, 16)
            keep_x(0, 1)
            for it in range(NT):
                if it:
                    pool.wait_ge(adj_loaded, 16 * it)
                load_adj(0, 0, it)
                if it == 1:
                    split_table(0, None)
            split_table(1, PRE)
            with pool.Fori(1, NT) as it:
                split_table(it + 1, turned_last(0, None, it - 1, 0))
                pool.wait_ge(adj_loaded, it * 16 + 16 * (NT - 1))
                load_adj(1, 1, it - 1)
            rsqrt(0, 0)
            keep_x(1, next_x_turned(0, None))
            pool.wait_ge(adj_loaded, 16 * (2 * NT - 1))
            load_adj(1, 1, NT - 1)

            def graph(b, half, more, first):
                def load_next(it):
                    if more:
                        wait_apart(pool, mask_done, b * NT + it + 1, pool_passed)
                        pool.wait_ge(adj_loaded, b * (16 * NT) + it * 16 + 16 * 2 * NT)
                        load_adj(half, b + 2, it)

                n = (b + 1) * NT
                split_table(n + 1, first)
                split_table(n + 2, turned_last(b + 1, b, 0, 0))
                load_next(0)
                with pool.Fori(2, NT) as it:
                    split_table(n + 1 + it, turned_last(b + 1, b, it - 1, 1))
                    load_next(it - 1)
                rsqrt(0, b + 1)
                if more:
                    keep_x(b + 2, next_x_turned(b + 1, b))
                rsqrt(1, b)
                load_next(NT - 1)

            with pool.Fori(0, (B - 2) // 2) as pair:
                with pool.Fori(0, 2) as half:
                    b = pair * 2 + half
                    graph(b, half, True, before(b + 1, b, 0, 0) - AFTER_TABLES)
            graph(B - 2, None, False, before(B - 1, B - 2, 0, 0) - AFTER_TABLES)
            rsqrt(1, B - 1)

        @block.scalar
        def _(act):
            act.wait_ge(const_loaded, 4 * 16)
            act.wait_ge(const_built, 4)

            def copy_x(ring):
                src = ring.rearrange("p (t i) -> p t i", t=NT)
                act.activation(xT[:, :, 0:P], src, ACT.Copy)
                act.activation(xT[:, :, P:PADDED], src[:, :, 2 * P - PADDED:P], ACT.Copy).then_inc(unit_free, 1)

            def copy_table(ring, dst, part):
                lo, hi = SPLIT[part]
                turned = ring[0:CODE, :].bitcast(BF16)[:, 0:(hi - lo) * F]
                act.activation(dst[:, lo:hi, :], turned.rearrange("p (k f) -> p k f", f=F),
                               ACT.Copy).then_inc(unit_free, 1)

            def tiles(b0, b1):
                def tile(it, known):
                    def unit(pos, what, u):
                        full = before(b0, b1, it, known) + (pos + 1)
                        ring = ring_of(known, b0, b1, what, u)
                        if what == "code":
                            wait_apart(act, unit_full, full, act_passed)
                            if known * NBLK + u >= HOTS:
                                ago = ((it, known, u - HOTS) if u >= HOTS
                                       else (it - 1, known - 1, NBLK + u - HOTS))
                                act.wait_ge(look_full, looks_before(B, b0, b1, *ago) + 1)
                            act.activation(hot[:, hot_slot(known, u), :], ring[0:CODE, :],
                                           ACT.Relu, bias=bias_sb[:, 0:1]).then_inc(unit_free, 1)
                        elif what == "turn":
                            if known >= 2:
                                act.wait_ge(at_stored[known % 2], b0 * (8 * NT) + it * 8 - 8 * (known % 2))
                            wait_apart(act, unit_full, full, act_passed)
                            act.activation(at8[:, known % 2, :, :], ring[:, :].rearrange("p (t i) -> p t i", t=NT),
                                           ACT.Copy, saturate=False).then_inc(unit_free, 1)
                        elif what == "x":
                            act.wait_ge(tab_step, b0 * (NT * BLK) + NT * BLK)
                            wait_apart(act, unit_full, full, act_passed)
                            copy_x(ring)
                        elif what == "probs":
                            copy_turned(b0, b1, it, known, pos)
                        else:
                            act.wait_ge(unit_full, full)
                            copy_table(ring, look[(known + 1) % 2], u)

                    def layer_1(place):
                        for t in range(GROUPS):
                            for c in range(QUADS):
                                if on_dve(t, c) or hidden_place(t, c) != place:
                                    continue
                                if (known > 0 or t >= RSLOTS) and c == min(c for c in range(QUADS) if not on_dve(t, c)):
                                    act.wait_ge(group_done, b1 * TILE_GROUPS + it * GROUPS + (t - RSLOTS + 1))
                                op = act.activation(hid[:, t % RSLOTS, c, :], q_sb[:, :], ACT.Relu,
                                                    bias=k_sb[:, bass.ds(it * PAIRS + (c * GROUPS + t), 1)])
                                if c == max(c for c in range(QUADS) if not on_dve(t, c)):
                                    op.then_inc(hid_act, 1)
                        if known > 0 and place == EXP_AT:
                            exponent(b1, it, known)

                    interleave(known, b0, b1, unit, layer_1)

                over_tiles(act, tile)

            def exponent(b, it, known):
                act.wait_ge(neg_done, b * NT + it)
                act.activation(pr[:, :], sc[:, :], ACT.Exp, bias=neg_top[:, 0:1],
                               accum_out=total[:, 0:1]).then_inc(exp_done, 1)

            def copy_turned(b0, b1, it, known, pos):
                if known >= 2:
                    act.wait_ge(look_full, att_number(b0, b1, it - 1, known - 1) + 1)
                act.wait_ge(unit_full, before(b0, b1, it, known) + (pos + 1))
                ring = ring_of(known, b0, b1, "probs")
                act.activation(prT[:, :, :], ring[:, :].rearrange("p (t i) -> p t i", t=NT),
                               ACT.Copy).then_inc(unit_free, 1)

            def boundary(b0, b1):
                if b1 is not None:
                    exponent(b1, NT, NT)
                    copy_turned(b0, b1, NT, NT, 0)
                if b0 is not None:
                    pos = int(b1 is not None)
                    act.wait_ge(unit_full, before(b0, b1, NT, NT) + (pos + 1))
                    act.activation(x1T[:, :], ring_of(NT, b0, b1, "x1")[:, :], ACT.Copy).then_inc(unit_free, 1)
                    act.wait_ge(qk_done, b0 + 1)
                    act.activation(q_sb[:, :], scores[:, :], ACT.Copy).then_inc(q_copied, 1)
                    act.wait_ge(q_copied, b0 + 1)
                    act.wait_ge(k_copied, b0 + 1)
                    for par in range(2):
                        act.wait_ge(at_stored[par], b0 * (8 * NT) + 8 * NT)

            act.wait_ge(unit_full, 1)
            copy_x(rings[0])
            for part in range(2):
                act.wait_ge(unit_full, 2 + part)
                copy_table(rings[1 + part], look[0], part)
            over_graphs(act, B, tiles, boundary)

        @block.tensor
        def _(pe):
            pe.wait_ge(code_loaded, 16)
            pe.wait_ge(const_built, 4)
            pe.wait_ge(a_ready, 2)

            def turn_x(ring, b):
                pe.wait_ge(x_loaded, b * 16 + 16)
                for t in range(NT):
                    mm = pe.transpose(ring[:, t * P:(t + 1) * P], x_next[:, t, :], ident[:, :])
                mm.then_inc(unit_full, 1)

            def turn_table(ring, part):
                lo, hi = SPLIT[part]
                for k in range(lo, hi):
                    mm = pe.transpose(ring[0:CODE, :].bitcast(BF16)[:, (k - lo) * F:(k - lo + 1) * F],
                                      tab_s[:, k, :, :].rearrange("p s q -> p (s q)"), ident_b[:, :])
                mm.then_inc(unit_full, 1)

            def wait_slot(b0, b1, it, known, what, u=0):
                last = last_in_slot(known, b0, b1, what, u)
                if last is None:
                    return
                (what, u), ago = last
                if what == "look":
                    assert u < NBLK - LAG or not ago
                    carried = u >= NBLK - LAG
                    pe.wait_ge(look_free, looks_before(B, b0, b1, it - ago - carried, known - ago - carried, u) + 1)
                elif what == "attention":
                    pe.wait_ge(look_free, att_number(b0, b1, it - ago, known - ago) + 1)
                elif what == "maxima":
                    pe.wait_ge(z0_done, b0 + 1)
                else:
                    pos = 0 if known - ago == NT else unit_pos(known - ago, b1, what, u) if b0 is not None else 0
                    pe.wait_ge(unit_free, before(b0, b1, it - ago, known - ago) + (pos + 1))

            def look_up(b0, b1, it, known, u, behind):
                pe.wait_ge(unit_free, before(b0, b1, it, known) + (unit_pos(known, b1, "code", u) + 1))
                wait_slot(b0, b1, it + behind, known + behind, "look", u)
                looked = ring_of(known, b0, b1, "look", u)
                for h in range(2):
                    mm = pe.matmul(looked[:, h * HALF:(h + 1) * HALF], look[known % 2][:, u, :],
                                   hot[:, hot_slot(known, u), h * HALF:(h + 1) * HALF], start=True, stop=True)
                mm.then_inc(look_full, 1)

            def score(b, n, t, h):
                if h == 0:
                    pe.wait_ge(hid_dve, b * TILE_GROUPS + n + 1)
                    pe.wait_ge(hid_act, b * TILE_GROUPS + n + 1)
                for c in range(QUADS):
                    mm = pe.matmul(scores[32 * c:32 * c + 32, h * HALF:(h + 1) * HALF],
                                   a_wide[:, t, :], hid[:, t % RSLOTS, c, h * HALF:(h + 1) * HALF],
                                   start=t == 0, stop=t == GROUPS - 1, tile_position=(0, 32 * c))
                if h == 1:
                    mm.then_inc(group_done, 1)

            def turn_probs(ring, b, it):
                pe.wait_ge(exp_done, b * NT + it)
                for j in range(NT):
                    mm = pe.transpose(ring[:, j * P:(j + 1) * P], pr[:, j * P:(j + 1) * P], ident[:, :])
                mm.then_inc(unit_full, 1)

            def attend(b0, b1, it, known):
                pe.wait_ge(unit_free, before(b0, b1, it, known) + (1 if b0 is None or known == NT
                                                                   else unit_pos(known, b1, "probs", 0) + 1))
                wait_slot(b0, b1, it, known, "attention")
                looked = ring_of(known, b0, b1, "attention")
                for j in range(NT):
                    mm = pe.matmul(looked[:, 0:F], prT[:, j, :], x1[:, j, :], start=j == 0, stop=j == NT - 1)
                mm.then_inc(look_full, 1)

            def tiles(b0, b1):
                half = b0 % 2 if b0 is not None else None

                def tile(it, known):
                    def unit(pos, what, u):
                        if what == "code" and u == 0:
                            pe.wait_ge(adj_loaded, b0 * (16 * NT) + it * 16 + 16)
                        ring = ring_of(known, b0, b1, what, u)
                        wait_slot(b0, b1, it, known, what, u)
                        if what == "probs":
                            turn_probs(ring, b1, it)
                            return
                        a_tile = adj_sb[:, bass.ds(half * NT + it, 1), :]
                        if what == "code":
                            for h in range(2):
                                mm = pe.matmul(ring[0:CODE, h * HALF:(h + 1) * HALF], code_sb[:, u, :],
                                               a_tile[:, :, h * HALF:(h + 1) * HALF].rearrange("p o j -> p (o j)"),
                                               start=True, stop=True)
                            mm.then_inc(unit_full, 1)
                            if u >= LAG:
                                look_up(b0, b1, it, known, u - LAG, 0)
                            elif known > 0:
                                look_up(b0, b1, it - 1, known - 1, NBLK - LAG + u, 1)
                        elif what == "turn":
                            for j in range(NT):
                                mm = pe.matmul(ring[:, j * P:(j + 1) * P],
                                               a_tile[:, :, j * P:(j + 1) * P].rearrange("p o j -> p (o j)"),
                                               ident_b[:, :], start=j % 4 == 0, stop=True, skip_group_check=True)
                            mm.then_inc(unit_full, 1)
                        elif what == "x":
                            turn_x(ring, b0 + 1)
                        else:
                            if u == 0:
                                pe.wait_ge(table_split, b0 * NT + it + 2)
                            turn_table(ring, u)

                    def layer_1(place):
                        if known > 0:
                            for t, h in SCORES:
                                if score_place(t, h) == place + NBLK:
                                    score(b1, it * GROUPS - GROUPS + t, t, h)
                        for t, h in SCORES:
                            if score_place(t, h) == place:
                                if (t, h) == (0, 0) and known > 0:
                                    pe.wait_ge(max_done, b1 * NT + it)
                                score(b1, it * GROUPS + t, t, h)
                        if known > 0 and place == ATTEND_AT:
                            attend(b0, b1, it, known)

                    interleave(known, b0, b1, unit, layer_1)

                over_tiles(pe, tile)

            def boundary(b0, b1):
                if b0 is not None:
                    for u in range(NBLK - LAG, NBLK):
                        look_up(b0, b1, NT - 1, NT - 1, u, 1)
                if b1 is not None:
                    for t, h in SCORES:
                        if score_place(t, h) >= NBLK:
                            score(b1, TILE_GROUPS - GROUPS + t, t, h)
                if b0 is not None:
                    pe.wait_ge(best_done, b0 + 1)
                    wait_slot(b0, b1, NT, NT, "maxima")
                    for t in range(NT):
                        mm = pe.transpose(ring_of(NT, b0, b1, "maxima")[:, t * P:(t + 1) * P], best[:, 0, t * P:(t + 1) * P], ident[:, :])
                    mm.then_inc(best_turned, 1)
                if b1 is not None:
                    wait_slot(b0, b1, NT, NT, "probs")
                    turn_probs(ring_of(NT, b0, b1, "probs"), b1, NT)
                    attend(b0, b1, NT, NT)
                if b0 is not None:
                    pos = int(b1 is not None)
                    pe.wait_ge(x1_done, b0 + 1)
                    wait_slot(b0, b1, NT, NT, "x1")
                    ring = ring_of(NT, b0, b1, "x1")
                    for t in range(NT):
                        mm = pe.transpose(ring[:, t * P:(t + 1) * P], x1[:, t, :], ident[:, :])
                    mm.then_inc(unit_full, 1)
                    pe.wait_ge(unit_free, before(b0, b1, NT, NT) + (pos + 1))
                    wait_slot(b0, b1, NT, NT, "k")
                    for dst, w in ((scores, w1_sb), (ring_of(NT, b0, b1, "k"), w2_sb)):
                        for h in range(2):
                            mm = pe.matmul(dst[:, h * HALF:(h + 1) * HALF], w[:, :],
                                           x1T[:, h * HALF:(h + 1) * HALF], start=True, stop=True)
                    mm.then_inc(qk_done, 1)
                    pe.wait_ge(k_copied, b0 + 1)
                    if b1 is not None:
                        pe.wait_ge(look_free, att_number(b0, b1, NT, NT) + 1)

            turn_x(rings[0], 0)
            pe.wait_ge(unit_free, 1)
            pe.wait_ge(table_split, 1)
            for part in range(2):
                turn_table(rings[1 + part], part)
            pe.wait_ge(unit_free, PRE)
            over_graphs(pe, B, tiles, boundary)

        @block.vector
        def _(dve):
            dve.wait_ge(const_loaded, 4 * 16)
            dve.wait_ge(const_built, 4)
            for h in range(2):
                half = slice(h * D1, (h + 1) * D1)
                flat = a_wide[half, :, :].rearrange("p t m -> p (t m)")
                diagonal = flat[:, h:h + 34 * (GROUPS - 1) + 1:34]
                dve.tensor_copy(diagonal, a_sb[half, 0:1].broadcast_to([D1, GROUPS])).then_inc(a_ready, 1)

            def floor(b):
                dve.tensor_reduce(low[:, 0:1], xT[:, :, :], mybir.AxisListType.XY, ALU.max).then_inc(floor_step, 1)
                dve.wait_ge(floor_step, b * 2 + 1)
                dve.tensor_scalar(tab[:, :, 0], low[:, 0:1].broadcast_to([P, NBLK]), NO_EDGE, None, ALU.add
                                  ).then_inc(floor_step, 1)
                dve.wait_ge(floor_step, b * 2 + 2)

            def build_table(n, it):
                for place in range(BLK):
                    m = 1 << place
                    if place:
                        dve.wait_ge(tab_step, n * BLK + place)
                    of_place = xT[:, bass.ds(it, 1), place:PADDED:BLK].rearrange("p o k -> p (o k)")
                    dve.tensor_tensor(tab[:, :, m:2 * m], tab[:, :, 0:m],
                                      of_place.rearrange("p (k o) -> p k o", o=1).broadcast_to([P, NBLK, m]),
                                      ALU.max).then_inc(tab_step, 1)

            def take_max(b0, b1, it, known, u):
                n = looks_before(B, b0, b1, it, known, u)
                if known * NBLK + u >= 2:
                    dve.wait_ge(look_free, n - 1)
                dve.wait_ge(look_full, n + 1)
                looked = ring_of(known, b0, b1, "look", u)
                if known == 0 and u < 2:
                    op = dve.tensor_copy(best[:, u, :], looked[:, :])
                else:
                    op = dve.tensor_tensor(best[:, u % 2, :], best[:, u % 2, :], looked[:, :], ALU.max)
                op.then_inc(look_free, 1)

            def measure(i, n, z):
                for t in range(NT):
                    op = dve.bn_stats(stats[:, i, t, :], z[:, t, :])
                op.then_inc(norm_stats[i], 1)
                wait_apart(dve, norm_stats[i], n + 1, dve_passed)
                for t in range(NT):
                    op = dve.bn_aggr(mv[:, i, t, :], stats[:, i, t, :])
                op.then_inc(norm_aggr[i], 1)

            def normalise(i, n, z, dst):
                dve.wait_ge(norm_rstd[i], n + 1)
                for t in range(NT):
                    op = dve.tensor_scalar(dst[:, t, :], z[:, t, :], mv[:, i, t, 0:1], rstd[:, i, t:t + 1],
                                           ALU.subtract, ALU.mult)
                return op

            def build_mask(b, it):
                half = b % 2
                dve.tensor_scalar(mask[:, :],
                                  adj_sb[:, bass.ds(half * NT + it - 1, 1), :].rearrange("p o j -> p (o j)"),
                                  0.0, NO_ATT, ALU.is_le, ALU.mult).then_inc(mask_done, 1)

            def row_max(b, it, known):
                if known >= 2:
                    dve.wait_ge(exp_done, b * NT + it - 1)
                dve.wait_ge(group_done, b * TILE_GROUPS + it * GROUPS)
                wait_apart(dve, mask_done, b * NT + it, dve_passed)
                dve.tensor_tensor_reduce(sc[:, :], scores[:, :], mask[:, :], 1.0, -3.0e38,
                                         ALU.add, ALU.max, top[:, 0:1]).then_inc(max_done, 1)
                dve.wait_ge(max_done, b * NT + it)
                dve.tensor_scalar(neg_top[:, :], top[:, :], -1.0, None, ALU.mult).then_inc(neg_done, 1)

            def add_residual(b0, b1, it, known):
                n = att_number(b0, b1, it, known)
                dve.wait_ge(exp_done, b1 * NT + it)
                dve.reciprocal(inv[:, :], total[:, :]).then_inc(inv_done, 1)
                dve.wait_ge(look_full, n + 1)
                dve.wait_ge(inv_done, b1 * NT + it)
                looked = ring_of(known, b0, b1, "attention")
                dve.scalar_tensor_tensor(z1[:, bass.ds(it - 1, 1), :].rearrange("p o f -> p (o f)"),
                                         looked[:, 0:F], inv[:, 0:1],
                                         x1[:, bass.ds(it - 1, 1), :].rearrange("p o f -> p (o f)"),
                                         ALU.mult, ALU.add).then_inc(look_free, 1)
                return n

            def tiles(b0, b1):
                def tile(it, known):
                    def unit(pos, what, u):
                        if what != "code":
                            return
                        if u >= LAG:
                            take_max(b0, b1, it, known, u - LAG)
                        elif known > 0:
                            take_max(b0, b1, it - 1, known - 1, NBLK - LAG + u)
                        table = b0 * NT + it + 1
                        if u == TABLE_AT and known < NT - 1:
                            dve.wait_ge(table_split, table)
                            build_table(table, it + 1)
                        if u == 4 and known == NT - 1:
                            dve.wait_ge(unit_free, before(b0, b1, it, known) + (unit_pos(known, b1, "x", 0) + 1))
                            dve.wait_ge(table_split, table)
                            floor(b0 + 1)
                            build_table(table, 0)

                    def layer_1(place):
                        if place == 0 and known > 0:
                            build_mask(b1, it)
                        if place == ROW_MAX_AT and known > 0:
                            row_max(b1, it, known)
                        for t in range(GROUPS):
                            own = [c for c in range(QUADS) if on_dve(t, c)]
                            for c in own:
                                if hidden_place(t, c) != place:
                                    continue
                                if c == own[0] and (known > 0 or t >= RSLOTS):
                                    dve.wait_ge(group_done, b1 * TILE_GROUPS + it * GROUPS + (t - RSLOTS + 1))
                                op = dve.tensor_scalar(hid[:, t % RSLOTS, c, :], q_sb[:, :],
                                                       k_sb[:, bass.ds(it * PAIRS + (c * GROUPS + t), 1)], 0.0,
                                                       ALU.add, ALU.max)
                                if c == own[-1]:
                                    op.then_inc(hid_dve, 1)
                        if known > 0 and place == ATTEND_AT:
                            add_residual(b0, b1, it, known)

                    interleave(known, b0, b1, unit, layer_1)

                over_tiles(dve, tile)

            def boundary(b0, b1):
                if b0 is not None:
                    for u in range(NBLK - LAG, NBLK):
                        take_max(b0, b1, NT - 1, NT - 1, u)
                    dve.wait_ge(look_free, looks_before(B, b0, b1, NT - 1, NT - 1, NBLK - 1) + 1)
                    dve.tensor_tensor(best[:, 0, :], best[:, 0, :], best[:, 1, :], ALU.max).then_inc(best_done, 1)
                if b1 is not None:
                    build_mask(b1, NT)
                    row_max(b1, NT, NT)
                if b0 is not None:
                    dve.wait_ge(best_turned, b0 + 1)
                    dve.wait_ge(x_kept, b0 + 1)
                    dve.tensor_tensor(z0[:, :, :], ring_of(NT, b0, b1, "maxima")[:, :].rearrange("p (t f) -> p t f", t=NT),
                                      x_sb[:, :, :], ALU.add).then_inc(z0_done, 1)
                    dve.wait_ge(z0_done, b0 + 1)
                    measure(0, b0, z0)
                if b1 is not None:
                    n = add_residual(b0, b1, NT, NT)
                    dve.wait_ge(look_free, n + 1)
                if b0 is not None:
                    normalise(0, b0, z0, x1).then_inc(x1_done, 1)
                if b1 is not None:
                    measure(1, b1, z1)
                if b0 is not None:
                    dve.wait_ge(qk_done, b0 + 1)
                    looked = ring_of(NT, b0, b1, "k")
                    dve.tensor_copy(k_sb[0:D1, :], looked[0:D1, 0:N:2])
                    dve.tensor_copy(k_sb[D1:P, :], looked[D1:P, 1:N:2]).then_inc(k_copied, 1)
                if b1 is not None:
                    dve.wait_ge(x2_free, b1 + 1)
                    normalise(1, b1, z1, x2).then_inc(x2_done, 1)
                if b0 is not None:
                    dve.wait_ge(k_copied, b0 + 1)
                    dve.wait_ge(q_copied, b0 + 1)

            dve.wait_ge(unit_free, 1)
            floor(0)
            build_table(0, 0)
            over_graphs(dve, B, tiles, boundary)


def code_constants():
    import numpy as np

    weights = np.zeros((P, NBLK, PARTS, PAT), np.float32)
    for u in range(NBLK):
        for place in range(BLK):
            source = u * BLK + place
            source = source if source < P else source - (PADDED - P)
            for q in range(PAT):
                weights[source, u, :, q] += 2 * (q >> place & 1) - 1
    bits = np.array([bin(q).count("1") for q in range(PAT)], np.float32)
    return weights.reshape(P, NBLK, CODE), np.tile(1 - bits, PARTS).reshape(CODE, 1)


def graph_layers_2_3(nc, B, adj, at_d, x2_d, W2, b2, g2, be2, W3, b3, g3, be3, out):
    L2, L3 = W2.shape[1], W3.shape[1]
    PAIRED = B // 2

    with ExitStack() as ctx:
        def sb(name, shape, dt=F32):
            return ctx.enter_context(nc.sbuf_tensor(name, shape, dt))

        def sem(name):
            return ctx.enter_context(nc.semaphore(name))

        ps_h = ctx.enter_context(nc.psum_tensor("ps_h", [P, 2, N], F32))
        ps_g = ctx.enter_context(nc.psum_tensor("ps_g", [P, 2, N], F32))

        h2 = sb("h2", [P, B, N])
        affine = sb("affine", [P, 2])
        ident = sb("ident1", [P, P])
        power = sb("power1", [P, NT])
        hT = sb("hT", [P, 2, N])
        hw = sb("hw", [P, 2, PARTS, N], BF16)
        rest = sb("rest", [P, 2, N])
        x2_in = sb("x2_in", [P, 2, N])
        w2_sb = sb("w2_all", [P, L2, F])
        w3_sb = sb("w3_all", [P, L3, F])
        b2_sb, g2_sb, be2_sb = sb("b2_sb", [P, L2]), sb("g2_sb", [P, L2]), sb("be2_sb", [P, L2])
        b3_sb, g3_sb, be3_sb = (sb(n, [P, L3, F]) for n in ("b3_sb", "g3_sb", "be3_sb"))

        params_loaded = sem("params_loaded")
        ident_zero = sem("ident_zero")
        built = sem("built")
        passed = {e: sem(f"passed_{e}") for e in ("act", "dve", "pool", "pe")}
        affine_done = sem("affine_done")

        shared = dict(
            B=B, L2=L2, L3=L3, PAIRED=PAIRED, adj=adj, at_d=at_d, x2_d=x2_d, out=out,
            W2=W2, b2=b2, g2=g2, be2=be2, W3=W3, b3=b3, g3=g3, be3=be3,
            ps_h=ps_h, ps_g=ps_g, h2=h2, affine=affine, ident=ident, power=power, hT=hT, hw=hw, rest=rest,
            x2_in=x2_in, w2_sb=w2_sb, w3_sb=w3_sb, b2_sb=b2_sb, g2_sb=g2_sb, be2_sb=be2_sb,
            b3_sb=b3_sb, g3_sb=g3_sb, be3_sb=be3_sb, params_loaded=params_loaded, ident_zero=ident_zero,
            built=built, passed=passed, affine_done=affine_done)
        layer_2(nc, shared)
        layer_3(nc, shared)


def layer_2(nc, v):
    B, L2, PAIRED = v["B"], v["L2"], v["PAIRED"]
    ps_h, ps_g, h2, affine, ident, power = (v[n] for n in ("ps_h", "ps_g", "h2", "affine", "ident", "power"))
    hT, hw, rest, x2_in = (v[n] for n in ("hT", "hw", "rest", "x2_in"))
    w2_sb, w3_sb, b2_sb, g2_sb, be2_sb = (v[n] for n in ("w2_sb", "w3_sb", "b2_sb", "g2_sb", "be2_sb"))
    at_d, x2_d, passed = v["at_d"], v["x2_d"], v["passed"]
    params_loaded, ident_zero, built, affine_done = (v[n] for n in ("params_loaded", "ident_zero", "built", "affine_done"))
    loads = [(w2_sb, v["W2"]), (w3_sb, v["W3"]), (b2_sb, v["b2"]), (g2_sb, v["g2"]), (be2_sb, v["be2"]),
             (v["b3_sb"], v["b3"]), (v["g3_sb"], v["g3"]), (v["be3_sb"], v["be3"])]
    with ExitStack() as ctx:
        def sb(name, shape, dt=F32):
            return ctx.enter_context(nc.sbuf_tensor(name, shape, dt))

        def sem(name):
            return ctx.enter_context(nc.semaphore(name))

        at = sb("at", [P, 2, NT, N], FP8)
        stats = sb("bn_st", [P, 2 * B, 6])
        mv = sb("bn_mv", [P, 2])
        rstd = sb("bn_rstd", [P, 1])
        prod = sb("bn_prod", [P, 1])

        x2_rows = [x2_in[:, 0, :], x2_in[:, 1, :], hT[:, 0, :], hT[:, 1, :]]
        x2_turns = [ps_h[:, 0, :], ps_h[:, 1, :], ps_g[:, 0, :], ps_g[:, 1, :]]
        TURNS = len(x2_rows)
        assert B % TURNS == 0 and B > TURNS
        x2_in_loaded = [sem(f"x2_in_loaded{q}") for q in range(TURNS)]
        at_loaded = [sem(f"at_loaded{q}") for q in range(2)]
        x2_turned = sem("x2_turned")
        x2_copied = sem("x2_copied")
        hin_done, hw_done, high_done = sem("hin_done"), sem("hw_done"), sem("high_done")
        rest_done, mid_done, split_done = sem("rest_done"), sem("mid_done"), sem("split_done")
        sum_done, relu_done = sem("sum_done"), sem("relu_done")
        bn_stats_done, bn_aggr_done = sem("bn_stats_done"), sem("bn_aggr_done")
        bn_eps_added, bn_rstd_done = sem("bn_eps_added"), sem("bn_rstd_done")
        scale_done, prod_done = sem("scale_done"), sem("prod_done")

        def pipelined(eng, l, first, ahead, behind):
            ahead(l, first, 0)
            with eng.Fori(0, PAIRED - 1) as i:
                for q in range(2):
                    ahead(l, i * 2 + q + 1, 1 - q)
                    behind(l, i * 2 + q, q)
            ahead(l, B - 1, 1)
            behind(l, B - 2, 0)
            behind(l, B - 1, 1)

        block = ctx.enter_context(nc.Block())

        @block.sync
        def _(sp):
            def load_at(b, q):
                src = at_d[bass.ds(b * NT, NT), :, :].rearrange("t p n -> p t n")
                sp.dma_start(at[:, q, :, :].bitcast(U8), src).then_inc(at_loaded[q], 16)

            for dst, src in loads:
                sp.dma_start(dst[tuple([slice(None)] * len(src.shape))], src).then_inc(params_loaded, 16)
            for q in range(TURNS):
                sp.dma_start(x2_rows[q], x2_d[q]).then_inc(x2_in_loaded[q], 16)
            with sp.Fori(1, B // TURNS) as i:
                for q in range(TURNS):
                    sp.wait_ge(x2_turned, i * TURNS + q - (TURNS - 1))
                    sp.dma_start(x2_rows[q], x2_d[bass.ds(i * TURNS + q, 1), :, :].rearrange("o p n -> p (o n)")
                                 ).then_inc(x2_in_loaded[q], 16)
            for q in range(2):
                load_at(q, q)

            def layer(l, last):
                with sp.Fori(0, PAIRED - 1) as i:
                    for q in range(2):
                        sp.wait_ge(sum_done, l * B + i * 2 + q + 1)
                        load_at(i * 2 + q + 2, q)
                if not last:
                    for q in range(2):
                        sp.wait_ge(sum_done, l * B + B - 2 + q + 1)
                        load_at(q, q)

            with sp.Fori(0, L2 - 1) as l:
                layer(l, False)
            layer(L2 - 1, True)

        @block.gpsimd
        def _(pool):
            pool.memset(ident[:, :], 0.0).then_inc(ident_zero, 1)
            pool.memset(power[:, :], -0.5).then_inc(built, 1)
            pool.wait_ge(ident_zero, 1)
            pool.affine_select(out=ident[:, :], in_=ident[:, :], compare_op=ALU.not_equal, fill=1.0,
                               base=0, pattern=[[-1, P]], channel_multiplier=1).then_inc(built, 1)
            pool.wait_ge(built, 2)
            with pool.Fori(0, L2) as l:
                wait_apart(pool, bn_aggr_done, l + 1, passed["pool"])
                pool.tensor_scalar(rstd[:, :], mv[:, 1:2], EPS, None, ALU.add).then_inc(bn_eps_added, 1)
                wait_apart(pool, bn_eps_added, l + 1, passed["pool"])
                pool.tensor_tensor(rstd[:, :], rstd[:, :], power[:, 0:1], ALU.pow).then_inc(bn_rstd_done, 1)

        @block.tensor
        def _(pe):
            pe.wait_ge(built, 2)
            pe.wait_ge(params_loaded, 16 * len(loads))

            def turn_x2(i, q):
                pe.wait_ge(x2_in_loaded[q], i * 16 + 16)
                for t in range(NT):
                    mm = pe.transpose(x2_turns[q][:, t * P:(t + 1) * P], x2_rows[q][:, t * F:(t + 1) * F],
                                      ident[:, :])
                mm.then_inc(x2_turned, 1)

            for q in range(TURNS):
                turn_x2(0, q)
            with pe.Fori(1, B // TURNS) as i:
                for q in range(TURNS):
                    pe.wait_ge(x2_copied, i * TURNS + q - (TURNS - 1))
                    turn_x2(i, q)

            def project(l, b, q):
                pe.wait_ge(hin_done, l * B + b + 1)
                for t in range(NT):
                    mm = pe.matmul(ps_h[:, q, t * P:(t + 1) * P], hT[:, q, t * P:(t + 1) * P],
                                   w2_sb[:, bass.ds(l, 1), :].rearrange("p o f -> p (o f)"),
                                   start=True, stop=True)
                mm.then_inc(hw_done, 1)

            def neighbours(l, b, q):
                wait_apart(pe, split_done, l * B + b + 1, passed["pe"])
                wait_apart(pe, at_loaded[q], l * (8 * B) + (b - q) * 8 + 16, passed["pe"])
                for k in range(NT):
                    for part in range(PARTS):
                        for h in range(2):
                            mm = pe.matmul(ps_g[:, q, h * HALF:(h + 1) * HALF], hw[:, q, part, k * P:(k + 1) * P],
                                           at[:, q, h * NT // 2:(h + 1) * NT // 2, k * P:(k + 1) * P],
                                           start=(k, part) == (0, 0), stop=(k, part) == (NT - 1, PARTS - 1))
                mm.then_inc(sum_done, 1)

            with pe.Fori(0, L2) as l:
                pipelined(pe, l, 0, project, neighbours)

        @block.scalar
        def _(act):
            act.wait_ge(x2_copied, B)
            act.wait_ge(params_loaded, 16 * len(loads))

            def row(b):
                return h2[:, bass.ds(b, 1), :].rearrange("p o n -> p (o n)")

            def enter(b, q):
                act.activation(hT[:, q, :], row(b), ACT.Identity, bias=affine[:, 1:2],
                               scale=affine[:, 0:1]).then_inc(hin_done, 1)

            def high(l, b, q):
                act.wait_ge(hw_done, l * B + b + 1)
                act.activation(hw[:, q, 0, :], ps_h[:, q, :], ACT.Copy).then_inc(high_done, 1)

            def leave(l, b, q):
                wait_apart(act, sum_done, l * B + b + 1, passed["act"])
                act.activation(row(b), ps_g[:, q, :], ACT.Relu, bias=b2_sb[:, bass.ds(l, 1)]
                               ).then_inc(relu_done, 1)

            with act.Fori(0, L2) as l:
                act.wait_ge(affine_done, l + 1)
                enter(0, 0)
                high(l, 0, 0)
                enter(1, 1)
                with act.Fori(0, PAIRED - 1) as i:
                    for q in range(2):
                        b = i * 2 + q
                        high(l, b + 1, 1 - q)
                        enter(b + 2, q)
                        leave(l, b, q)
                high(l, B - 1, 1)
                leave(l, B - 2, 0)
                leave(l, B - 1, 1)

        @block.vector
        def _(dve):
            dve.wait_ge(params_loaded, 16 * len(loads))
            dve.memset(affine[:, 0:1], 1.0)
            dve.memset(affine[:, 1:2], 0.0).then_inc(affine_done, 1)

            with dve.Fori(0, B // TURNS) as i:
                for q in range(TURNS):
                    b = i * TURNS + q
                    dve.wait_ge(x2_turned, b + 1)
                    dve.tensor_copy(h2[:, bass.ds(b, 1), :].rearrange("p o n -> p (o n)"), x2_turns[q]
                                    ).then_inc(x2_copied, 1)

            def split(l, b, q):
                s = l * B + b + 1
                dve.wait_ge(high_done, s)
                dve.tensor_tensor(rest[:, q, :], ps_h[:, q, :], hw[:, q, 0, :], ALU.subtract).then_inc(rest_done, 1)
                dve.wait_ge(rest_done, s)
                dve.tensor_copy(hw[:, q, 1, :], rest[:, q, :]).then_inc(mid_done, 1)
                dve.wait_ge(mid_done, s)
                dve.tensor_tensor(hw[:, q, 2, :], rest[:, q, :], hw[:, q, 1, :], ALU.subtract).then_inc(split_done, 1)

            def measure(l, b, q):
                dve.wait_ge(relu_done, l * B + b + 1)
                for h in range(2):
                    op = dve.bn_stats(stats[:, bass.ds(b * 2 + h, 1), :].rearrange("p o s -> p (o s)"),
                                      h2[:, bass.ds(b, 1), h * HALF:(h + 1) * HALF].rearrange("p o n -> p (o n)"))
                op.then_inc(bn_stats_done, 1)

            with dve.Fori(0, L2) as l:
                pipelined(dve, l, 0, split, measure)
                wait_apart(dve, bn_stats_done, l * B + B, passed["dve"])
                dve.bn_aggr(mv[:, :], stats[:, :, :].rearrange("p k s -> p (k s)")).then_inc(bn_aggr_done, 1)
                dve.wait_ge(bn_rstd_done, l + 1)
                dve.tensor_tensor(affine[:, 0:1], g2_sb[:, bass.ds(l, 1)], rstd[:, :], ALU.mult).then_inc(scale_done, 1)
                dve.wait_ge(scale_done, l + 1)
                dve.tensor_tensor(prod[:, :], mv[:, 0:1], affine[:, 0:1], ALU.mult).then_inc(prod_done, 1)
                dve.wait_ge(prod_done, l + 1)
                dve.tensor_tensor(affine[:, 1:2], be2_sb[:, bass.ds(l, 1)], prod[:, :], ALU.subtract
                                  ).then_inc(affine_done, 1)


def layer_3(nc, v):
    B, L3 = v["B"], v["L3"]
    ps_h, ps_g, h2, affine, ident, power = (v[n] for n in ("ps_h", "ps_g", "h2", "affine", "ident", "power"))
    hT, hw, rest, x2_in = (v[n] for n in ("hT", "hw", "rest", "x2_in"))
    w3_sb, b3_sb, g3_sb, be3_sb = (v[n] for n in ("w3_sb", "b3_sb", "g3_sb", "be3_sb"))
    adj, x2_d, out, passed = v["adj"], v["x2_d"], v["out"], v["passed"]
    IN_FLIGHT = 4
    ROUNDS = B // IN_FLIGHT
    STEPS = L3 * IN_FLIGHT
    ENTER_LAYER = min(1, L3 - 1)
    assert B % IN_FLIGHT == 0 and L3 >= 2
    with ExitStack() as ctx:
        def sb(name, shape, dt=F32):
            return ctx.enter_context(nc.sbuf_tensor(name, shape, dt))

        def sem(name):
            return ctx.enter_context(nc.semaphore("l3_" + name))

        adj_in = [sb(f"adj_in{q}", [P, NT, N], BF16) for q in range(IN_FLIGHT)]
        h = sb("h", [P, IN_FLIGHT, N])
        z = sb("z3", [P, IN_FLIGHT, N])
        stats = sb("st3", [P, 3, NT, 6])
        mv = sb("mv3", [P, 3, 2, NT, 2])
        rstd = sb("rstd3", [P, 3, 2, NT])
        mean_rstd = sb("mean_rstd", [P, 3, 2, NT])
        shift = sb("shift3", [P, 3, 2, NT])

        adj_loaded = [sem(f"adj_loaded{q}") for q in range(IN_FLIGHT)]
        x2_loaded = [sem(f"x2_loaded{q}") for q in range(IN_FLIGHT)]
        out_stored, z_free = sem("out_stored"), sem("z_free")
        y_done, y_turned, y_added, x3_done = sem("y_done"), sem("y_turned"), sem("y_added"), sem("x3_done")
        last_h, x3_added, out_done = sem("last_h"), sem("x3_added"), sem("out_done")
        h_done, h_turned, hT_done, hb_done = sem("h_done"), sem("h_turned"), sem("hT_done"), sem("hb_done")
        hw_done, high_done, rest_done = sem("hw_done"), sem("high_done"), sem("rest_done")
        mid_done, split_done = sem("mid_done"), sem("split_done")
        sum_done, sum_read = sem("sum_done"), sem("sum_read")
        scaled, shifted, layer_normed = sem("scaled"), sem("shifted"), sem("layer_normed")
        IN, LAYER, OUT = range(3)
        normed = [x3_done, layer_normed, out_done]
        st_done, mv_done, eps_done, rstd_done, product_done, shift_done = (
            [sem(f"{name}{k}") for k in range(3)]
            for name in ("st_done", "mv_done", "eps_done", "rstd_done", "product_done", "shift_done"))

        block = ctx.enter_context(nc.Block())

        def by_node(t):
            return t.rearrange("p (t f) -> p t f", t=NT)

        def row(b):
            return h2[:, bass.ds(b, 1), :].rearrange("p o n -> p (o n)")

        def x2_of(b, q):
            return z[:, q, :] if isinstance(b, int) and b < IN_FLIGHT else x2_in[:, q % 2, :]

        @block.sync
        def _(sp):
            def load_x2(b, q):
                sp.dma_start(x2_of(b, q), x2_d[bass.ds(b, 1), :, :].rearrange("o p n -> p (o n)")
                             ).then_inc(x2_loaded[q], 16)

            sp.sem_inc(z_free, IN_FLIGHT)
            for q in range(IN_FLIGHT):
                load_x2(q, q)

            def store(i):
                for q in range(IN_FLIGHT):
                    sp.wait_ge(out_done, i * IN_FLIGHT + q + 1)
                    sp.dma_start(out[bass.ds(i * IN_FLIGHT + q, 1), :, :].rearrange("o (t p) f -> p (o t) f", p=P),
                                 by_node(z[:, q, :])).then_inc(out_stored, 16)
                    sp.wait_ge(out_stored, i * (16 * IN_FLIGHT) + 16 * (q + 1))
                    sp.sem_inc(z_free, 1)

            with sp.Fori(0, ROUNDS - 1) as i:
                for q in range(IN_FLIGHT):
                    sp.wait_ge(x3_done, i * IN_FLIGHT + IN_FLIGHT + q - 1)
                    load_x2(i * IN_FLIGHT + IN_FLIGHT + q, q)
                store(i)
            store(ROUNDS - 1)

        @block.gpsimd
        def _(pool):
            def load_adj(b, q):
                pool.dma_start(adj_in[q][:, :, :], adj[bass.ds(b, 1), :, :].rearrange("o (t p) j -> p (o t) j", p=P)
                               ).then_inc(adj_loaded[q], 16)

            def rsqrt(kind, n, slot=0):
                wait_apart(pool, mv_done[kind], n + 1, passed["pool"])
                pool.tensor_scalar(rstd[:, kind, slot, :], mv[:, kind, slot, :, 1], EPS, None, ALU.add
                                   ).then_inc(eps_done[kind], 1)
                wait_apart(pool, eps_done[kind], n + 1, passed["pool"])
                pool.tensor_tensor(rstd[:, kind, slot, :], rstd[:, kind, slot, :], power[:, :], ALU.pow
                                   ).then_inc(rstd_done[kind], 1)
                if kind != LAYER:
                    wait_apart(pool, rstd_done[kind], n + 1, passed["pool"])
                    pool.tensor_tensor(mean_rstd[:, kind, slot, :], mv[:, kind, slot, :, 0], rstd[:, kind, slot, :],
                                       ALU.mult).then_inc(product_done[kind], 1)
                    wait_apart(pool, product_done[kind], n + 1, passed["pool"])
                    pool.tensor_scalar(shift[:, kind, slot, :], mean_rstd[:, kind, slot, :], -1.0, None, ALU.mult
                                       ).then_inc(shift_done[kind], 1)

            def add_bias(n, s, b):
                l, q = s // IN_FLIGHT, s % IN_FLIGHT
                wait_apart(pool, h_done, n + 1, passed["pool"])
                if l == 0:
                    wait_apart(pool, z_free, b + 1, passed["pool"])
                pool.tensor_tensor(by_node(z[:, q, :]), by_node(h[:, q, :]),
                                   b3_sb[:, l:l + 1, :].broadcast_to([P, NT, F]), ALU.add).then_inc(hb_done, 1)

            for q in range(IN_FLIGHT):
                load_adj(q, q)
            for q in range(IN_FLIGHT):
                rsqrt(IN, q, q % 2)
            for s in range(2):
                add_bias(s, s, s)

            def work(i, last):
                for s in range(STEPS):
                    l, q = s // IN_FLIGHT, s % IN_FLIGHT
                    rsqrt(LAYER, i * STEPS + s)
                    if l == L3 - 1 and q > 0:
                        rsqrt(OUT, i * IN_FLIGHT + q - 1, (q - 1) % 2)
                    if l == ENTER_LAYER and not last:
                        rsqrt(IN, i * IN_FLIGHT + IN_FLIGHT + q, q % 2)
                    if l == L3 - 1 and not last:
                        wait_apart(pool, sum_done, i * STEPS + s + 1, passed["pool"])
                        load_adj(i * IN_FLIGHT + IN_FLIGHT + q, q)
                    if s + 2 < STEPS:
                        add_bias(i * STEPS + s + 2, s + 2, i * IN_FLIGHT + s + 2)
                    elif not last:
                        add_bias(i * STEPS + s + 2, s + 2 - STEPS, i * IN_FLIGHT + IN_FLIGHT + s + 2 - STEPS)
                rsqrt(OUT, i * IN_FLIGHT + IN_FLIGHT - 1, (IN_FLIGHT - 1) % 2)

            with pool.Fori(0, ROUNDS - 1) as i:
                work(i, False)
            work(ROUNDS - 1, True)

        @block.tensor
        def _(pe):
            def turn_y(b, q, slot):
                pe.wait_ge(y_done, b + 1)
                for t in range(NT):
                    mm = pe.transpose(ps_g[:, slot, t * P:(t + 1) * P], hT[:, slot, t * P:(t + 1) * P], ident[:, :])
                mm.then_inc(y_turned, 1)

            def turn(n, s):
                q = s % IN_FLIGHT
                pe.wait_ge(h_done, n + 1)
                for t in range(NT):
                    mm = pe.transpose(ps_h[:, s % 2, t * P:(t + 1) * P], h[:, q, t * P:(t + 1) * P], ident[:, :])
                mm.then_inc(h_turned, 1)

            def project(n, s):
                l = s // IN_FLIGHT
                pe.wait_ge(hT_done, n + 1)
                for t in range(NT):
                    mm = pe.matmul(ps_h[:, s % 2, t * P:(t + 1) * P], hT[:, s % 2, t * P:(t + 1) * P],
                                   w3_sb[:, l, :], start=True, stop=True)
                mm.then_inc(hw_done, 1)

            def neighbours(i, s, q):
                if s < IN_FLIGHT:
                    pe.wait_ge(adj_loaded[q], i * 16 + 16)
                pe.wait_ge(sum_read, i * STEPS + s + 1)
                for j in range(NT):
                    for k in range(NT):
                        for part in range(PARTS):
                            mm = pe.matmul(ps_g[:, s % 2, j * P:(j + 1) * P], adj_in[q][:, k, j * P:(j + 1) * P],
                                           hw[:, s % 2, part, k * P:(k + 1) * P],
                                           start=(k, part) == (0, 0), stop=(k, part) == (NT - 1, PARTS - 1))
                mm.then_inc(sum_done, 1)

            for q in range(IN_FLIGHT):
                if q >= 2:
                    pe.wait_ge(y_added, q - 1)
                turn_y(q, q, q % 2)
            turn(0, 0)
            project(0, 0)
            turn(1, 1)
            pe.wait_ge(y_added, IN_FLIGHT)

            def work(i, last):
                for s in range(STEPS):
                    l, q = s // IN_FLIGHT, s % IN_FLIGHT
                    n = i * STEPS + s
                    if s + 1 < STEPS or not last:
                        project(n + 1, (s + 1) % STEPS)
                    pe.wait_ge(split_done, n + 1)
                    if s + 2 < STEPS or not last:
                        turn(n + 2, (s + 2) % STEPS)
                    before = s - 1 - ENTER_LAYER * IN_FLIGHT
                    if 0 <= before < IN_FLIGHT and not last:
                        pe.wait_ge(y_added, i * IN_FLIGHT + IN_FLIGHT + before + 1)
                    neighbours(i, s, q)
                    if l == ENTER_LAYER and not last:
                        pe.wait_ge(sum_read, n + 2)
                        turn_y(i * IN_FLIGHT + IN_FLIGHT + q, q, (s + 1) % 2)

            with pe.Fori(0, ROUNDS - 1) as i:
                work(i, False)
            work(ROUNDS - 1, True)

        @block.scalar
        def _(act):
            def enter(b, slot):
                act.activation(hT[:, slot, :], row(b), ACT.Identity,
                               bias=affine[:, 1:2], scale=affine[:, 0:1]).then_inc(y_done, 1)

            def keep(b, q):
                wait_apart(act, x3_done, b + 1, passed["act"])
                act.activation(h[:, q, :], row(b), ACT.Copy).then_inc(h_done, 1)

            def copy_turned(n, s):
                act.wait_ge(h_turned, n + 1)
                act.activation(hT[:, s % 2, :], ps_h[:, s % 2, :], ACT.Copy).then_inc(hT_done, 1)

            def high(n, s):
                act.wait_ge(hw_done, n + 1)
                act.activation(hw[:, s % 2, 0, :], ps_h[:, s % 2, :], ACT.Copy).then_inc(high_done, 1)

            def normalise(kind, b, q, src, dst):
                wait_apart(act, shift_done[kind], b + 1, passed["act"])
                for t in range(NT):
                    op = act.activation(dst[:, t * F:(t + 1) * F], src[:, t * F:(t + 1) * F], ACT.Identity,
                                        bias=shift[:, kind, q % 2, t:t + 1], scale=rstd[:, kind, q % 2, t:t + 1])
                op.then_inc(normed[kind], 1)

            def make_x3(b, q):
                normalise(IN, b, q, x2_of(b, q), row(b))

            def make_result(b, q):
                normalise(OUT, b, q, z[:, q, :], z[:, q, :])

            for q in range(IN_FLIGHT):
                if q >= 2:
                    act.wait_ge(y_turned, q - 1)
                enter(q, q % 2)
            for q in range(IN_FLIGHT):
                make_x3(q, q)
                keep(q, q)
            copy_turned(0, 0)
            high(0, 0)
            copy_turned(1, 1)
            high(1, 1)
            copy_turned(2, 2)

            def work(i, last):
                for s in range(STEPS):
                    l, q = s // IN_FLIGHT, s % IN_FLIGHT
                    n = i * STEPS + s
                    if l == ENTER_LAYER and not last:
                        enter(i * IN_FLIGHT + IN_FLIGHT + q, (s + 1) % 2)
                    if l == L3 - 1 and q > 0 and not last:
                        swap(i, q - 1)
                    if s + 2 < STEPS or not last:
                        high(n + 2, (s + 2) % STEPS)
                    if s + 3 < STEPS or not last:
                        copy_turned(n + 3, (s + 3) % STEPS)
                    if 0 <= s - 1 - ENTER_LAYER * IN_FLIGHT < IN_FLIGHT and not last:
                        q_in = (s - 1) % IN_FLIGHT
                        make_x3(i * IN_FLIGHT + IN_FLIGHT + q_in, q_in)
                    if l == L3 - 1 and q > 1:
                        make_result(i * IN_FLIGHT + q - 2, q - 2)
                    act.wait_ge(shifted, n + 1)
                    act.activation(h[:, q, :], z[:, q, :], ACT.Relu).then_inc(
                        last_h if l == L3 - 1 else h_done, 1)
                if not last:
                    swap(i, IN_FLIGHT - 1)
                for q in range(IN_FLIGHT - 2, IN_FLIGHT):
                    make_result(i * IN_FLIGHT + q, q)

            def swap(i, q):
                act.wait_ge(x3_added, i * IN_FLIGHT + q + 1)
                keep(i * IN_FLIGHT + IN_FLIGHT + q, q)

            with act.Fori(0, ROUNDS - 1) as i:
                work(i, False)
            work(ROUNDS - 1, True)

        @block.vector
        def _(dve):
            dve.sem_inc(sum_read, 2)

            def measure(kind, n, src, slot=0):
                for t in range(NT):
                    op = dve.bn_stats(stats[:, kind, t, :], src[:, t * F:(t + 1) * F])
                op.then_inc(st_done[kind], 1)
                wait_apart(dve, st_done[kind], n + 1, passed["dve"])
                for t in range(NT):
                    op = dve.bn_aggr(mv[:, kind, slot, t, :], stats[:, kind, t, :])
                op.then_inc(mv_done[kind], 1)

            def normalise(n, src, dst):
                wait_apart(dve, rstd_done[LAYER], n + 1, passed["dve"])
                for t in range(NT):
                    op = dve.tensor_scalar(dst[:, t * F:(t + 1) * F], src[:, t * F:(t + 1) * F],
                                           mv[:, LAYER, 0, t, 0:1], rstd[:, LAYER, 0, t:t + 1], ALU.subtract, ALU.mult)
                op.then_inc(layer_normed, 1)

            def add_y(b, q, loads, slot):
                dve.wait_ge(x2_loaded[q], loads * 16)
                dve.wait_ge(y_turned, b + 1)
                dve.tensor_tensor(x2_of(b, q), ps_g[:, slot, :], x2_of(b, q), ALU.add
                                  ).then_inc(y_added, 1)

            def measure_x3(b, q):
                dve.wait_ge(y_added, b + 1)
                if isinstance(b, int) and b >= 2:
                    dve.wait_ge(x3_done, b - 1)
                measure(IN, b, x2_of(b, q), q % 2)

            def split(n, s):
                dve.wait_ge(high_done, n + 1)
                dve.tensor_tensor(rest[:, s % 2, :], ps_h[:, s % 2, :], hw[:, s % 2, 0, :], ALU.subtract
                                  ).then_inc(rest_done, 1)
                dve.wait_ge(rest_done, n + 1)
                dve.tensor_copy(hw[:, s % 2, 1, :], rest[:, s % 2, :]).then_inc(mid_done, 1)
                dve.wait_ge(mid_done, n + 1)
                dve.tensor_tensor(hw[:, s % 2, 2, :], rest[:, s % 2, :], hw[:, s % 2, 1, :], ALU.subtract
                                  ).then_inc(split_done, 1)

            def add_sum(n, s, q):
                dve.wait_ge(hb_done, n + 1)
                dve.wait_ge(sum_done, n + 1)
                dve.tensor_tensor(z[:, q, :], ps_g[:, s % 2, :], z[:, q, :], ALU.add).then_inc(sum_read, 1)
                dve.wait_ge(sum_read, n + 3)
                measure(LAYER, n, z[:, q, :])

            def finish(n, l, q):
                normalise(n, z[:, q, :], z[:, q, :])
                dve.wait_ge(layer_normed, n + 1)
                dve.tensor_tensor(by_node(z[:, q, :]), by_node(z[:, q, :]),
                                  g3_sb[:, l:l + 1, :].broadcast_to([P, NT, F]), ALU.mult).then_inc(scaled, 1)
                dve.wait_ge(scaled, n + 1)
                dve.tensor_tensor(by_node(z[:, q, :]), by_node(z[:, q, :]),
                                  be3_sb[:, l:l + 1, :].broadcast_to([P, NT, F]), ALU.add).then_inc(shifted, 1)

            def add_x3(b, q):
                wait_apart(dve, last_h, b + 1, passed["dve"])
                dve.tensor_tensor(z[:, q, :], h[:, q, :], row(b), ALU.add).then_inc(x3_added, 1)

            def measure_result(b, q):
                dve.wait_ge(x3_added, b + 1)
                measure(OUT, b, z[:, q, :], q % 2)

            for q in range(IN_FLIGHT):
                add_y(q, q, 1, q % 2)
                measure_x3(q, q)
            split(0, 0)
            split(1, 1)

            def work(i, last):
                for s in range(STEPS):
                    l, q = s // IN_FLIGHT, s % IN_FLIGHT
                    n = i * STEPS + s
                    b = i * IN_FLIGHT + q
                    entering = l == ENTER_LAYER and not last
                    leaving = l == L3 - 1 and q > 0
                    if leaving:
                        add_x3(b - 1, q - 1)
                    add_sum(n, s, q)
                    if entering:
                        add_y(b + IN_FLIGHT, q, i + 2, (s + 1) % 2)
                    if s + 2 < STEPS or not last:
                        split(n + 2, (s + 2) % STEPS)
                    if entering:
                        measure_x3(b + IN_FLIGHT, q)
                    if leaving:
                        measure_result(b - 1, q - 1)
                    finish(n, l, q)
                add_x3(i * IN_FLIGHT + IN_FLIGHT - 1, IN_FLIGHT - 1)
                measure_result(i * IN_FLIGHT + IN_FLIGHT - 1, IN_FLIGHT - 1)

            with dve.Fori(0, ROUNDS - 1) as i:
                work(i, False)
            work(ROUNDS - 1, True)


def kernel(**inputs):
    import numpy as np
    import concourse.bacc as bacc
    from concourse.bass_utils import run_bass_kernel_spmd

    def rows(a):
        return np.ascontiguousarray(np.asarray(inputs[a]))

    code, bias = code_constants()
    w1, w2, a = rows("L1_gnn_W1").T, rows("L1_gnn_W2").T, rows("L1_gnn_a").reshape(D1, 1)
    arrays = {
        "x_in": rows("x"),
        "adj_in": rows("adj"),
        "w1_in": np.concatenate([w1, w1], 1),
        "w2_in": np.concatenate([w2, w2], 1),
        "a_in": np.concatenate([a, a], 0),
        "code_in": code,
        "bias_in": bias,
        "W2_in": rows("L2_gnn_W").transpose(1, 0, 2),
        "b2_in": rows("L2_gnn_b").T,
        "g2_in": rows("L2_gnn_gamma").T,
        "be2_in": rows("L2_gnn_beta").T,
        "W3_in": rows("L3_gnn_Ws").transpose(1, 0, 2),
        "b3_in": np.broadcast_to(rows("L3_gnn_bs"), (P, 3, F)),
        "g3_in": np.broadcast_to(rows("L3_gnn_gammas"), (P, 3, F)),
        "be3_in": np.broadcast_to(rows("L3_gnn_betas"), (P, 3, F)),
    }
    arrays = {n: np.ascontiguousarray(v) for n, v in arrays.items()}
    nc = bacc.Bacc("TRN2", target_bir_lowering=False, num_devices=1)
    args = [nc.dram_tensor(n, v.shape, mybir.dt.from_np(v.dtype), kind="ExternalInput").ap()
            for n, v in arrays.items()]
    out = nc.dram_tensor("out", arrays["x_in"].shape, F32, kind="ExternalOutput").ap()
    program(nc, *args, out)
    return run_bass_kernel_spmd(nc, [arrays], core_ids=[0]).results[0]["out"]


def program(nc, x, adj, w1, w2, a, code, bias, W2, b2, g2, be2, W3, b3, g3, be3, out):
    B = x.shape[0]
    at_d = nc.dram_tensor("adj_turned", (B * NT, P, N), U8).ap()
    x2_d = nc.dram_tensor("x2_rows", (B, P, N), F32).ap()
    graph_layers_0_1(nc, B, x, adj, w1, w2, a, code, bias, at_d, x2_d)
    graph_layers_2_3(nc, B, adj, at_d, x2_d, W2, b2, g2, be2, W3, b3, g3, be3, out)
```
